# Optimizing a Trainium2 kernel written in Bass

```python
import numpy as np
import jax
import jax.numpy as jnp

def _softmax(x, axis=-1):
    return jax.nn.softmax(x, axis=axis)

def _gelu(x):
    return jax.nn.gelu(x, approximate=True)

def _silu(x):
    return jax.nn.silu(x)

def _sigmoid(x):
    return jax.nn.sigmoid(x)

def _layernorm(x, axis=-1, eps=1e-05):
    m = jnp.mean(x, axis=axis, keepdims=True)
    v = jnp.var(x, axis=axis, keepdims=True)
    return (x - m) / jnp.sqrt(v + eps)

def _scatter_add(tgt, idx, src, axis=0):
    return tgt.at[idx].add(src)

def _segment_sum(src, seg, n):
    return jax.ops.segment_sum(src, seg, n)
kernel_name = 'mk_decoder_preln_d2_seqx_r8_7fca3c'

def setup_inputs(seed: int=0):
    np.random.seed(seed)
    _w = jnp.asarray

    def _rec_inputs():
        import jax
        import jax.numpy as jnp
        _rk = jax.random.key(seed)
        x = 7.22e-05 + 1 * jax.random.normal(jax.random.fold_in(_rk, 1), (4, 256, 128), jnp.float32)
        _lenS = 256 - jax.random.randint(jax.random.fold_in(_rk, 7), (4,), 0, max(1, 256 // 4) + 1, jnp.int32)
        _lenS2 = 256 - jax.random.randint(jax.random.fold_in(_rk, 8), (4,), 0, max(1, 256 // 4) + 1, jnp.int32)
        _ctx_1024P = jax.random.normal(jax.random.fold_in(_rk, 11), (4, 16, 128), jnp.float32)
        _ctx_1024c = jax.random.dirichlet(jax.random.fold_in(_rk, 511), 0.3 * jnp.ones((16,), jnp.float32), (4, 256))
        _ctx_1024t = jnp.einsum('bsk,bkd->bsd', _ctx_1024c, _ctx_1024P)
        _ctx_1024t = _ctx_1024t * jax.lax.rsqrt(jnp.mean(jnp.square(_ctx_1024t)) + 1e-12) * 0.953939
        ctx_1024 = 4.13588e-05 + 0.999923 * (_ctx_1024t + 0.3 * jax.random.normal(jax.random.fold_in(_rk, 611), (4, 256, 128), jnp.float32))
        _validS = jnp.arange(256)[None, :] < _lenS[:, None]
        _validS2 = jnp.arange(256)[None, :] < _lenS2[:, None]
        _causal = jnp.tril(jnp.ones((256, 256), dtype=bool))
        mask_BxS2_ik0 = jnp.where(jnp.broadcast_to(_validS2[:, :], (4, 256)), 0, 1).astype(jnp.int32)
        return (x, ctx_1024, mask_BxS2_ik0)
    x, ctx_1024, mask_BxS2_ik0 = _rec_inputs()

    def _L0_attn_setup():
        import jax, jax.numpy as jnp
        import numpy as np
        HIDDEN = 128
        N_HEAD = 16
        HEAD_DIM = HIDDEN // N_HEAD
        BATCH = 1
        SEQ = 512
        THETA = 10000.0

        def _rope_cos_sin(seq_len, head_dim, dtype=jnp.float32):
            inv_freq = 1.0 / THETA ** (jnp.arange(0, head_dim, 2, dtype=dtype) / head_dim)
            t = jnp.arange(seq_len, dtype=dtype)
            freqs = jnp.outer(t, inv_freq)
            return (jnp.cos(freqs), jnp.sin(freqs))

        def _apply_rope(x, cos, sin):
            x2 = x.reshape(*x.shape[:-1], -1, 2)
            x_re, x_im = (x2[..., 0], x2[..., 1])
            c = cos[None, :, None, :]
            s = sin[None, :, None, :]
            out_re = x_re * c - x_im * s
            out_im = x_re * s + x_im * c
            out = jnp.stack([out_re, out_im], axis=-1)
            return out.reshape(x.shape)
        key = jax.random.key(seed)
        kx, kq, kk, kv = jax.random.split(key, 4)
        scale = 1.0 / np.sqrt(HIDDEN)
        return {'x': jax.random.normal(kx, (BATCH, SEQ, HIDDEN), dtype=jnp.float32), 'wq': jax.random.normal(kq, (HIDDEN, HIDDEN), dtype=jnp.float32) * scale, 'wk': jax.random.normal(kk, (HIDDEN, HIDDEN), dtype=jnp.float32) * scale, 'wv': jax.random.normal(kv, (HIDDEN, HIDDEN), dtype=jnp.float32) * scale}
    _L0_attn_all = _L0_attn_setup()
    _L0_attn_in = {k: v for k, v in _L0_attn_all.items() if k in ('wq', 'wk', 'wv')}
    del _L0_attn_all

    def _L0_xattn_setup():
        import jax, jax.numpy as jnp
        import numpy as np
        B, T, D_MODEL, D_HIDDEN, MAX_SEQLEN = (4, 256, 128, 128, 256)
        key = jax.random.key(seed)
        ks = jax.random.split(key, 8)
        scale = 0.02
        return {'q': jax.random.normal(ks[0], (B, T, D_MODEL), dtype=jnp.float32), 'k': jax.random.normal(ks[1], (B, T, D_MODEL), dtype=jnp.float32), 'v': jax.random.normal(ks[2], (B, T, D_MODEL), dtype=jnp.float32), 'Wq': jax.random.normal(ks[3], (D_HIDDEN, D_MODEL), dtype=jnp.float32) * scale, 'Wk': jax.random.normal(ks[4], (D_HIDDEN, D_MODEL), dtype=jnp.float32) * scale, 'Wv': jax.random.normal(ks[5], (D_HIDDEN, D_MODEL), dtype=jnp.float32) * scale, 'Wo': jax.random.normal(ks[6], (D_MODEL, D_HIDDEN), dtype=jnp.float32) * scale, 'W_bias': jax.random.normal(ks[7], (MAX_SEQLEN, MAX_SEQLEN), dtype=jnp.float32) * scale}
    _L0_xattn_all = _L0_xattn_setup()
    _L0_xattn_in = {k: v for k, v in _L0_xattn_all.items() if k in ('Wq', 'Wk', 'Wv', 'Wo', 'W_bias')}
    del _L0_xattn_all

    def _L0_ffn_setup():
        import jax, jax.numpy as jnp
        import numpy as np
        D_MODEL = 128
        HIDDEN = 512
        NUM_EXPERTS = 8
        TOP_K = 2
        key = jax.random.key(seed)
        k_x, k_g, k_in, k_out = jax.random.split(key, 4)
        bound_in = 1.0 / HIDDEN
        bound_out = 1.0 / D_MODEL
        x = jax.random.normal(k_x, (2, 256, D_MODEL), dtype=jnp.float32)
        w_gate = jax.random.uniform(k_g, (NUM_EXPERTS, D_MODEL), dtype=jnp.float32, minval=-D_MODEL ** (-0.5), maxval=D_MODEL ** (-0.5))
        w_in = jax.random.uniform(k_in, (NUM_EXPERTS, HIDDEN, D_MODEL), dtype=jnp.float32, minval=-bound_in, maxval=bound_in)
        w_out = jax.random.uniform(k_out, (NUM_EXPERTS, D_MODEL, HIDDEN), dtype=jnp.float32, minval=-bound_out, maxval=bound_out)
        return {'x': x, 'w_gate': w_gate, 'w_in': w_in, 'w_out': w_out}
    _L0_ffn_all = _L0_ffn_setup()
    _L0_ffn_in = {k: v for k, v in _L0_ffn_all.items() if k in ('w_gate', 'w_in', 'w_out')}
    del _L0_ffn_all

    def _L1_attn_setup():
        import jax, jax.numpy as jnp
        import numpy as np
        B, L, E, H = (8, 256, 128, 16)
        D = E // H
        EPS = 1e-06
        key = jax.random.key(seed)
        ks = jax.random.split(key, 9)
        s = 1.0 / np.sqrt(E)

        def lin_w(k):
            return jax.random.uniform(k, (E, E), jnp.float32, -s, s)

        def lin_b(k):
            return jax.random.uniform(k, (E,), jnp.float32, -s, s)
        return {'query': jax.random.normal(ks[0], (B, L, E), jnp.float32), 'Wq': lin_w(ks[1]), 'bq': lin_b(ks[2]), 'Wk': lin_w(ks[3]), 'bk': lin_b(ks[4]), 'Wv': lin_w(ks[5]), 'bv': lin_b(ks[6]), 'Wo': lin_w(ks[7]), 'bo': lin_b(ks[8])}
    _L1_attn_all = _L1_attn_setup()
    _L1_attn_in = {k: v for k, v in _L1_attn_all.items() if k in ('Wq', 'bq', 'Wk', 'bk', 'Wv', 'bv', 'Wo', 'bo')}
    del _L1_attn_all

    def _L1_xattn_setup():
        import jax, jax.numpy as jnp
        import numpy as np
        B, S, D, H = (2, 256, 128, 16)
        DK = D // H
        SQRT_DK = DK ** 0.5
        NEG = -1000000000.0
        key = jax.random.key(seed)
        ks = jax.random.split(key, 7)
        scale = 1.0 / np.sqrt(D)
        return {'x': jax.random.normal(ks[0], (B, S, D), jnp.float32), 'encoder_output': jax.random.normal(ks[1], (B, S, D), jnp.float32), 'mask': jax.random.randint(ks[2], (B, S), 0, 2, jnp.int32), 'WQ': jax.random.normal(ks[3], (D, D), jnp.float32) * scale, 'WK': jax.random.normal(ks[4], (D, D), jnp.float32) * scale, 'WV': jax.random.normal(ks[5], (D, D), jnp.float32) * scale, 'WO': jax.random.normal(ks[6], (D, D), jnp.float32) * scale}
    _L1_xattn_all = _L1_xattn_setup()
    _L1_xattn_in = {k: v for k, v in _L1_xattn_all.items() if k in ('WQ', 'WK', 'WV', 'WO')}
    del _L1_xattn_all

    def _L1_ffn_setup():
        import jax, jax.numpy as jnp
        import numpy as np
        B, S, H, F, E, R, TOPK = (4, 256, 128, 512, 4, 4, 2)

        def _more_forward(x, Wg, bg, W1, b1, W2, b2):
            b, s, h = x.shape
            cur = x
            for r in range(R):
                flat = cur.reshape(-1, h)
                logits = flat @ Wg[r] + bg[r]
                vals, idx = jax.lax.top_k(logits, TOPK)
                w = jax.nn.softmax(vals, axis=-1)
                cw = jnp.sum(jax.nn.one_hot(idx, E, dtype=flat.dtype) * w[..., None], axis=1)
                hmid = jax.nn.gelu(jnp.einsum('nh,ehf->enf', flat, W1) + b1[:, None, :])
                y = jnp.einsum('enf,efh->enh', hmid, W2) + b2[:, None, :]
                out = jnp.einsum('ne,enh->nh', cw, y)
                cur = cur + out.reshape(b, s, h)
            return cur
        key = jax.random.key(seed)
        ks = jax.random.split(key, 8)
        scale = 0.02
        return {'x': jax.random.normal(ks[0], (B, S, H), dtype=jnp.float32), 'Wg': jax.random.normal(ks[1], (R, H, E), dtype=jnp.float32) * scale, 'bg': jnp.zeros((R, E), dtype=jnp.float32), 'W1': jax.random.normal(ks[2], (E, H, F), dtype=jnp.float32) * scale, 'b1': jnp.zeros((E, F), dtype=jnp.float32), 'W2': jax.random.normal(ks[3], (E, F, H), dtype=jnp.float32) * scale, 'b2': jnp.zeros((E, H), dtype=jnp.float32)}
    _L1_ffn_all = _L1_ffn_setup()
    _L1_ffn_in = {k: v for k, v in _L1_ffn_all.items() if k in ('Wg', 'bg', 'W1', 'b1', 'W2', 'b2')}
    del _L1_ffn_all
    return {'x': x, 'ctx_1024': ctx_1024, 'mask_BxS2_ik0': mask_BxS2_ik0, 'L0_attn_wq': _L0_attn_in['wq'], 'L0_attn_wk': _L0_attn_in['wk'], 'L0_attn_wv': _L0_attn_in['wv'], 'L0_xattn_Wq': _L0_xattn_in['Wq'], 'L0_xattn_Wk': _L0_xattn_in['Wk'], 'L0_xattn_Wv': _L0_xattn_in['Wv'], 'L0_xattn_Wo': _L0_xattn_in['Wo'], 'L0_xattn_W_bias': _L0_xattn_in['W_bias'], 'L0_ffn_w_gate': _L0_ffn_in['w_gate'], 'L0_ffn_w_in': _L0_ffn_in['w_in'], 'L0_ffn_w_out': _L0_ffn_in['w_out'], 'L1_attn_Wq': _L1_attn_in['Wq'], 'L1_attn_bq': _L1_attn_in['bq'], 'L1_attn_Wk': _L1_attn_in['Wk'], 'L1_attn_bk': _L1_attn_in['bk'], 'L1_attn_Wv': _L1_attn_in['Wv'], 'L1_attn_bv': _L1_attn_in['bv'], 'L1_attn_Wo': _L1_attn_in['Wo'], 'L1_attn_bo': _L1_attn_in['bo'], 'L1_xattn_WQ': _L1_xattn_in['WQ'], 'L1_xattn_WK': _L1_xattn_in['WK'], 'L1_xattn_WV': _L1_xattn_in['WV'], 'L1_xattn_WO': _L1_xattn_in['WO'], 'L1_ffn_Wg': _L1_ffn_in['Wg'], 'L1_ffn_bg': _L1_ffn_in['bg'], 'L1_ffn_W1': _L1_ffn_in['W1'], 'L1_ffn_b1': _L1_ffn_in['b1'], 'L1_ffn_W2': _L1_ffn_in['W2'], 'L1_ffn_b2': _L1_ffn_in['b2']}

def reference(x, ctx_1024, mask_BxS2_ik0, L0_attn_wq, L0_attn_wk, L0_attn_wv, L0_xattn_Wq, L0_xattn_Wk, L0_xattn_Wv, L0_xattn_Wo, L0_xattn_W_bias, L0_ffn_w_gate, L0_ffn_w_in, L0_ffn_w_out, L1_attn_Wq, L1_attn_bq, L1_attn_Wk, L1_attn_bk, L1_attn_Wv, L1_attn_bv, L1_attn_Wo, L1_attn_bo, L1_xattn_WQ, L1_xattn_WK, L1_xattn_WV, L1_xattn_WO, L1_ffn_Wg, L1_ffn_bg, L1_ffn_W1, L1_ffn_b1, L1_ffn_W2, L1_ffn_b2):
    import jax
    import jax.numpy as jnp

    def _L0_attn_ref(x, wq, wk, wv):
        import jax, jax.numpy as jnp
        import numpy as np
        HIDDEN = 128
        N_HEAD = 16
        HEAD_DIM = HIDDEN // N_HEAD
        BATCH = 1
        SEQ = 512
        THETA = 10000.0

        def _rope_cos_sin(seq_len, head_dim, dtype=jnp.float32):
            inv_freq = 1.0 / THETA ** (jnp.arange(0, head_dim, 2, dtype=dtype) / head_dim)
            t = jnp.arange(seq_len, dtype=dtype)
            freqs = jnp.outer(t, inv_freq)
            return (jnp.cos(freqs), jnp.sin(freqs))

        def _apply_rope(x, cos, sin):
            x2 = x.reshape(*x.shape[:-1], -1, 2)
            x_re, x_im = (x2[..., 0], x2[..., 1])
            c = cos[None, :, None, :]
            s = sin[None, :, None, :]
            out_re = x_re * c - x_im * s
            out_im = x_re * s + x_im * c
            out = jnp.stack([out_re, out_im], axis=-1)
            return out.reshape(x.shape)
        B, S, _ = x.shape
        xq = (x @ wq.T).reshape(B, S, N_HEAD, HEAD_DIM).astype(jnp.float32)
        xk = (x @ wk.T).reshape(B, S, N_HEAD, HEAD_DIM).astype(jnp.float32)
        xv = (x @ wv.T).reshape(B, S, N_HEAD, HEAD_DIM).astype(jnp.float32)
        cos, sin = _rope_cos_sin(S, HEAD_DIM)
        q = _apply_rope(xq, cos, sin)
        k = _apply_rope(xk, cos, sin)
        scores = jnp.einsum('bqhd,bkhd->bhqk', q, k) / jnp.sqrt(jnp.asarray(HEAD_DIM, dtype=q.dtype))
        attn = jax.nn.softmax(scores, axis=-1)
        out = jnp.einsum('bhqk,bkhd->bqhd', attn, xv)
        return out.reshape(B, S, N_HEAD * HEAD_DIM)

    def _L0_xattn_ref(q, k, v, Wq, Wk, Wv, Wo, W_bias):
        import jax, jax.numpy as jnp
        import numpy as np
        B, T, D_MODEL, D_HIDDEN, MAX_SEQLEN = (4, 256, 128, 128, 256)
        Ti = q.shape[1]
        Tj = k.shape[1]
        Q = jnp.einsum('btm,hm->bth', q, Wq)
        K = jnp.einsum('btm,hm->bth', k, Wk)
        V = jnp.einsum('btm,hm->bth', v, Wv)
        pos_bias = W_bias[:Ti, :Tj][None]
        max_key = jnp.max(K, axis=0, keepdims=True)
        max_pos_bias = jnp.max(pos_bias, axis=0, keepdims=True)
        exp_key = jnp.exp(K - max_key)
        exp_pos_bias = jnp.exp(pos_bias - max_pos_bias)
        num = jnp.einsum('bij,bjd->bid', exp_pos_bias, exp_key * V)
        den = jnp.einsum('bij,bjd->bid', exp_pos_bias, exp_key)
        Yt = jax.nn.sigmoid(Q) * num / den
        return jnp.einsum('bth,mh->btm', Yt, Wo)

    def _L0_ffn_ref(x, w_gate, w_in, w_out):
        import jax, jax.numpy as jnp
        import numpy as np
        D_MODEL = 128
        HIDDEN = 512
        NUM_EXPERTS = 8
        TOP_K = 2
        B, S, D = x.shape
        E = w_in.shape[0]
        xt = x.reshape(-1, D)
        logits = (xt @ w_gate.T).astype(jnp.float32)
        top_logits, top_idx = jax.lax.top_k(logits, TOP_K)
        top_gates = jax.nn.softmax(top_logits, axis=-1).astype(x.dtype)
        gates = (jax.nn.one_hot(top_idx, E, dtype=x.dtype) * top_gates[..., None]).sum(axis=1)
        y = jnp.zeros_like(xt)
        for e in range(E):
            h = xt @ w_in[e].T
            y = y + gates[:, e:e + 1] * (h @ w_out[e].T)
        return y.reshape(B, S, D)

    def _L1_attn_ref(query, Wq, bq, Wk, bk, Wv, bv, Wo, bo):
        import jax, jax.numpy as jnp
        import numpy as np
        B, L, E, H = (8, 256, 128, 16)
        D = E // H
        EPS = 1e-06
        bsz, tgt_len, embed_dim = query.shape
        n_head = H
        head_dim = embed_dim // n_head
        m = tgt_len
        q = query @ Wq + bq
        k = query @ Wk + bk
        v = query @ Wv + bv

        def to_heads(x):
            return x.reshape(bsz, tgt_len, n_head, head_dim).transpose(0, 2, 1, 3)
        q = jax.nn.softmax(to_heads(q), axis=-1)
        k = jax.nn.softmax(to_heads(k), axis=-1)
        v = to_heads(v)
        comp_q = 1.0 - q
        comp_k = 1.0 - k
        idx = np.pi / 2 * jnp.arange(1, m + 1, dtype=jnp.float32) / m
        sin = jnp.sin(idx)[None, None, :, None]
        cos = jnp.cos(idx)[None, None, :, None]

        def feat(x):
            return jnp.concatenate([x * sin, x * cos], axis=-1)
        qf, comp_qf = (feat(q), feat(comp_q))
        kf, comp_kf = (feat(k), feat(comp_k))

        def branch(qf_, kf_):
            kv = jnp.einsum('bhld,bhlm->bhdm', kf_, v)
            z = 1.0 / jnp.maximum(jnp.einsum('bhld,bhd->bhl', qf_, kf_.sum(axis=2)), EPS)
            return jnp.einsum('bhld,bhdm,bhl->bhlm', qf_, kv, z)
        attn = branch(qf, kf) + branch(comp_qf, comp_kf)
        out = attn.transpose(2, 0, 1, 3).reshape(tgt_len, bsz, embed_dim)
        out = out @ Wo + bo
        return out.reshape(bsz, tgt_len, embed_dim)

    def _L1_xattn_ref(x, encoder_output, mask, WQ, WK, WV, WO):
        import jax, jax.numpy as jnp
        import numpy as np
        B, S, D, H = (2, 256, 128, 16)
        DK = D // H
        SQRT_DK = DK ** 0.5
        NEG = -1000000000.0
        b, s, d = x.shape
        q = (x @ WQ).reshape(b, s, H, DK).transpose(0, 2, 1, 3)
        k = (encoder_output @ WK).reshape(b, s, H, DK).transpose(0, 2, 1, 3)
        v = (encoder_output @ WV).reshape(b, s, H, DK).transpose(0, 2, 1, 3)
        scores = jnp.einsum('bhqd,bhkd->bhqk', q, k) / SQRT_DK
        future = jnp.triu(jnp.ones((s, s), jnp.int32), 1)
        m = mask[:, None, :, None] + future[None, None, :, :]
        scores = jnp.where(m != 0, NEG, scores)
        attn = jax.nn.softmax(scores, axis=-1)
        ctx = jnp.einsum('bhqk,bhkd->bqhd', attn, v).reshape(b, s, d)
        return ctx @ WO

    def _L1_ffn_ref(x, Wg, bg, W1, b1, W2, b2):
        import jax, jax.numpy as jnp
        import numpy as np
        B, S, H, F, E, R, TOPK = (4, 256, 128, 512, 4, 4, 2)

        def _more_forward(x, Wg, bg, W1, b1, W2, b2):
            b, s, h = x.shape
            cur = x
            for r in range(R):
                flat = cur.reshape(-1, h)
                logits = flat @ Wg[r] + bg[r]
                vals, idx = jax.lax.top_k(logits, TOPK)
                w = jax.nn.softmax(vals, axis=-1)
                cw = jnp.sum(jax.nn.one_hot(idx, E, dtype=flat.dtype) * w[..., None], axis=1)
                hmid = jax.nn.gelu(jnp.einsum('nh,ehf->enf', flat, W1) + b1[:, None, :])
                y = jnp.einsum('enf,efh->enh', hmid, W2) + b2[:, None, :]
                out = jnp.einsum('ne,enh->nh', cw, y)
                cur = cur + out.reshape(b, s, h)
            return cur
        return _more_forward(x, Wg, bg, W1, b1, W2, b2)
    x = x + _L0_attn_ref(_layernorm(x, axis=-1), L0_attn_wq, L0_attn_wk, L0_attn_wv)
    x = x + _L0_xattn_ref(_layernorm(x, axis=-1), ctx_1024, ctx_1024, L0_xattn_Wq, L0_xattn_Wk, L0_xattn_Wv, L0_xattn_Wo, L0_xattn_W_bias)
    x = x + _L0_ffn_ref(_layernorm(x, axis=-1), L0_ffn_w_gate, L0_ffn_w_in, L0_ffn_w_out)
    x = x + _L1_attn_ref(_layernorm(x, axis=-1), L1_attn_Wq, L1_attn_bq, L1_attn_Wk, L1_attn_bk, L1_attn_Wv, L1_attn_bv, L1_attn_Wo, L1_attn_bo)
    x = x + _L1_xattn_ref(_layernorm(x, axis=-1), ctx_1024, mask_BxS2_ik0, L1_xattn_WQ, L1_xattn_WK, L1_xattn_WV, L1_xattn_WO)
    x = x + _L1_ffn_ref(_layernorm(x, axis=-1), L1_ffn_Wg, L1_ffn_bg, L1_ffn_W1, L1_ffn_b1, L1_ffn_W2, L1_ffn_b2)
    return x

_drawn_inputs = setup_inputs


def setup_inputs(seed=0):
    import zlib

    import numpy as np

    out = dict(_drawn_inputs(seed))
    spreads = {'L1_ffn_bg': (0.0, 0.1), 'L1_ffn_b1': (0.0, 0.286), 'L1_ffn_b2': (0.0, 0.1)}
    factors = {'L0_xattn_Wq': 8.0,
     'L0_xattn_Wk': 8.0,
     'L0_xattn_Wv': 3.587,
     'L0_xattn_Wo': 3.761,
     'L0_ffn_w_gate': 8.0,
     'L0_ffn_w_in': 8.0,
     'L0_ffn_w_out': 8.0,
     'L1_attn_Wq': 8.0,
     'L1_attn_bq': 53.701,
     'L1_attn_Wk': 8.0,
     'L1_attn_bk': 59.49}
    for name, (base, spread) in spreads.items():
        noise = np.random.default_rng([zlib.crc32(name.encode()), seed]).standard_normal(out[name].shape)
        drawn = base * np.exp(spread * noise) if base else spread * noise
        out[name] = jnp.asarray(drawn.astype(out[name].dtype))
    for name, factor in factors.items():
        out[name] = (out[name] * factor).astype(out[name].dtype)
    return out
```

```python
import concourse.bass as bass
from concourse import mybir
from contextlib import ExitStack

B, T, D = 4, 256, 128
H, DH = 16, 8
P = 128
NT = B * T // P
TPB = T // P
HALF = B * T // 2
HPG = 4
G = H // HPG
QUAD = P // HPG
MAXROW = 3 * DH
E0, F0 = 8, 512
E1, F1, R1 = 4, 512, 4
FC = F1 // P
LN_EPS, Z_EPS = 1e-5, 1e-6


class OwnOrder:

    def __init__(self, engine, semaphore):
        self.engine, self.semaphore, self.base, self.n = engine, semaphore, 0, 0

    def mark(self, instruction):
        instruction.then_inc(self.semaphore, 1)
        self.n += 1

    def wait(self):
        self.engine.wait_ge(self.semaphore, self.base + self.n)

    def step(self, instruction):
        self.mark(instruction)
        self.wait()

    def loop(self, i, per):
        self.outer, self.per = self.base + self.n, per
        self.base, self.n = i * per + self.outer, 0

    def end(self, count):
        assert self.n == self.per, self.n
        self.base, self.n = self.outer + count * self.per, 0


def decoder_kernel(nc, w, out, stop=99):
    f32, f32r, bf16 = mybir.dt.float32, mybir.dt.float32r, mybir.dt.bfloat16
    ALU, ACT, AX = mybir.AluOpType, mybir.ActivationFunctionType, mybir.AxisListType
    ds = bass.ds
    ctx = ExitStack()
    with ctx:
        def sb(name, shape, dt=f32):
            return ctx.enter_context(nc.sbuf_tensor(name, shape, dt))

        def sem(name):
            return ctx.enter_context(nc.semaphore(name))

        x = sb("x", [P, NT, D])
        ident = sb("ident", [P, P])
        identb = sb("identb", [P, P], bf16)
        trib = sb("trib", [P, 2, TPB, T], bf16)
        one_row = sb("one_row", [P, 1])
        sincos = sb("sincos", [P, TPB, 2])
        diag = sb("diag", [P, P])
        diag_h = sb("diag_h", [P, H])
        tie0 = sb("tie0", [P, E0, E0])
        tie1 = sb("tie1", [P, E1, E1])
        wgate0 = sb("wgate0", [P, E0])
        wi0 = sb("wi0", [P, E0, F0 // P, D])
        wo0 = sb("wo0", [P, E0, F0 // P, D])
        wqkv1 = sb("wqkv1", [P, 3, D])
        bqkv1 = sb("bqkv1", [P, 3, D])
        wo1 = sb("wo1", [P, D])
        bo1 = sb("bo1", [P, D])
        wx1 = sb("wx1", [P, 2, D])
        mask_i = sb("mask_i", [P, NT], mybir.dt.int32)
        wg1 = sb("wg1", [P, R1, E1])
        bg1 = sb("bg1", [P, R1, E1])
        b1 = sb("b1", [P, E1, FC])
        b2 = sb("b2", [P, E1])

        selr = sb("selr", [P, 2, G, 2, P], f32r)
        mean_w = sb("mean_w", [P, P])
        halfs = sb("halfs", [P, NT])
        v1_tok = sb("v1_tok", [P, NT, D])
        k1hi = sb("k1hi", [P, B * T], f32r)
        k1lo = sb("k1lo", [P, B * T], f32r)
        maskf = sb("maskf", [P, NT])

        early = ExitStack()

        def sb_early(name, shape, dt=f32):
            return early.enter_context(nc.sbuf_tensor(name, shape, dt))

        rope = sb_early("rope", [P, 2, T])
        w0 = sb_early("w0", [P, 5, D])
        ctxT = sb_early("ctxT", [P, B * T])
        wctx = sb_early("wctx", [P, 4, D])
        wx0 = sb_early("wx0", [P, 2, D])
        wbiasT = sb_early("wbiasT", [P, TPB, T])
        expbT = sb_early("expbT", [P, TPB, T])
        ek = sb_early("ek", [P, TPB, B, D])
        ekv = sb_early("ekv", [P, TPB, B, D])
        v_tok = sb_early("v_tok", [P, NT, D])
        early.close()
        w1hi = sb("w1hi", [P, E1, F1], f32r)
        w1lo = sb("w1lo", [P, E1, F1], f32r)
        w2hi = sb("w2hi", [P, E1, FC, D], f32r)
        w2lo = sb("w2lo", [P, E1, FC, D], f32r)
        cwT = sb("cwT", [2 * E1, 2, HALF], f32r)
        sel_er = sb("sel_er", [2 * E1, E1, P], f32r)

        stats = sb("stats", [P, NT, 6])
        mv = sb("mv", [P, NT, 2])
        rstd = sb("rstd", [P, NT])
        vare = sb("vare", [P, NT])
        xn = sb("xn", [P, NT, D])
        xnT = sb("xnT", [P, B * T])
        big = sb("big", [P, 8192])
        bigr = sb("bigr", [P, 8192], f32r)
        ps = ctx.enter_context(nc.psum_tensor("ps", [P, 8, 512], f32))

        w1f = wo0[:, 0:E1, :, :].rearrange("p e c d -> p e (c d)")
        w2f = wi0[:, 0:E1, :, :]
        sel = big[:, 4096:6144].rearrange("p (a g i m) -> p a g i m", a=2, g=G, i=2)
        qt1 = big[:, 0:2048].rearrange("p (a n) -> p a n", a=2)
        qt2 = big[:, 2048:4096].rearrange("p (a n) -> p a n", a=2)
        qhi = bigr[:, 0:2048].rearrange("p (a n) -> p a n", a=2)
        qlo = bigr[:, 2048:4096].rearrange("p (a n) -> p a n", a=2)
        stack = bigr[:, 4096:8192].rearrange("p (i a g t) -> p i a g t", i=2, a=2, g=G)
        vaug = sb("vaug", [P, 2, TPB, H, QUAD])
        nmax = sb("nmax", [P, 2, TPB, G, P])
        prob = big[:, 4096:6144].rearrange("p (s k t) -> p s k t", s=4, k=TPB)
        oT = big[:, 6144:8192].rearrange("p (i g t) -> p i g t", i=2, g=G)
        gt, eqt = (xn[:, n:n + 4, :].rearrange("p n d -> p (n d)") for n in (0, 4))
        we0 = big[:, 7168:8192].rearrange("p (e d) -> p e d", e=E0)
        eq = big[:, 0:1024]
        den = big[:, 1024:2048]
        yT = big[:, 2048:3072]
        prod = big[:, 0:2048].rearrange("p (i e d) -> p i e d", i=2, e=E0)
        qkv = big[:, 0:1536].rearrange("p (i t c) -> p i t c", i=2, t=TPB)
        kc = big[:, 1536:2048].rearrange("p (i t c) -> p i t c", i=2, t=TPB)
        rv = big[:, 2048:3080].rearrange("p (i t c) -> p i t c", i=2, t=TPB)
        qT = big[:, 3080:4104].rearrange("p (i a c) -> p i a c", i=2, a=2)
        bd = big[:, 4104:4680].rearrange("p (a c) -> p a c", a=2)
        part = big[:, 4680:4968].rearrange("p (a c) -> p a c", a=2)
        comb = big[:, 4968:5256].rearrange("p (a c) -> p a c", a=2)
        att2 = big[:, 5256:5512].rearrange("p (a c) -> p a c", a=2)
        att = big[:, 5512:5768].rearrange("p (t c) -> p t c", t=TPB)
        attT = big[:, 5768:6792]
        gel = big[:, 0:2048].rearrange("p (s n) -> p s n", s=4)
        cwb = big[:, 2048:6144].rearrange("p (u n) -> p u n", u=8)
        yw = big[:, 6144:7168].rearrange("p (u n) -> p u n", u=2)
        ghi = bigr[:, 0:4096].rearrange("p (u c n) -> p u c n", u=2, c=FC)
        glo = bigr[:, 4096:8192].rearrange("p (u c n) -> p u c n", u=2, c=FC)
        xhi, xlo = k1hi, k1lo
        oN = sb("oN", [P, TPB, D])
        odif = sb("odif", [P, TPB, D])
        vmean = sb("vmean", [P, B, D])
        mxq = sb("mxq", [P, 2, 2 * TPB, 32])
        sumq = sb("sumq", [P, 2, 2 * TPB, 32])
        lg = sb("lg", [P, NT * E0])
        rank = sb("rank", [P, NT * E0])
        selh = sb("selh", [P, NT * E0])
        lsel = sb("lsel", [P, NT * E0])
        half_sum = sb("half_sum", [P, NT])
        dif = sb("dif", [P, NT * E0])
        cw = sb("cw", [P, NT * E0])
        cwr = sb("cwr", [P, NT * E0], f32r)
        cwhl = sb("cwhl", [P, 4, 2 * E1])
        sel_e = sb("sel_e", [2 * E1, E1, P])
        oNT = sb("oNT", [P, TPB, P])
        rs = sb("rs", [P, TPB, H])

        S = {}

        def s(name):
            if name not in S:
                S[name] = sem(name)
            return S[name]

        block = ctx.enter_context(nc.Block())

        @block.sync
        def _(sp):
            def load(name, dst, src):
                sp.dma_start(dst, src).then_inc(s("ld_" + name), 16)
            load("x", x[:, :, :], w["x"].rearrange("(n p) d -> p n d", p=P))
            load("ident", ident[:, :], w["ident"])
            load("ctx", ctxT[:, :], w["ctxT"])
            load("ctx", wctx[:, :, :], w["wctx"])
            load("w0", w0[:, :, :], w["w0"])
            load("rope", rope[:, :, :], w["rope"])
            load("sel", sel, w["sel"])
            load("sel", one_row[:, :], w["one_row"])
            load("xa0", wx0[:, :, :], w["wx0"])
            load("xa0", wbiasT[:, :, :], w["wbiasT"])
            load("ff0", wi0[:, :, :, :], w["wi0"])
            load("ff0", wo0[:, :, :, :], w["wo0"])
            load("gate0", wgate0[:, :], w["wgate0"])
            load("gate0", tie0[:, :, :], w["tie0"].partition_broadcast(P))
            load("at1", wqkv1[:, :, :], w["wqkv1"])
            load("at1", bqkv1[:, :, :], w["bqkv1"].partition_broadcast(P))
            load("at1", wo1[:, :], w["wo1"])
            load("at1", bo1[:, :], w["bo1"].partition_broadcast(P))
            load("at1", sincos[:, :, :], w["sincos"])
            load("at1", diag[:, :], w["diag"])
            load("at1", diag_h[:, :], w["diag_h"])
            load("xa1", wx1[:, :, :], w["wx1"])
            load("xa1", trib[:, :, :, :], w["tri"])
            load("xa1", identb[:, :], w["identb"])
            load("xa1", mask_i[:, :], w["mask"])
            load("ff1", wg1[:, :, :], w["wg1"])
            load("ff1", bg1[:, :, :], w["bg1"].partition_broadcast(P))
            load("ff1", b1[:, :, :], w["b1"])
            load("ff1", b2[:, :], w["b2"])
            load("ff1", tie1[:, :, :], w["tie1"].partition_broadcast(P))
            load("ff1", sel_e[:, :, :], w["sel_e"])
            sp.wait_ge(s("we_pe"), E0)
            load("w1", w1f, w["w1"])
            load("w1", w2f, w["w2"])
            sp.wait_ge(s("final"), 2)
            sp.dma_start(out.rearrange("(n p) d -> p n d", p=P), x[:, :, :]).then_inc(s("stored"), 16)
            sp.wait_ge(s("stored"), 16)
            if stop < 5:
                for n, c in (("ff0", 2), ("gate0", 2), ("at1", 7), ("xa1", 4), ("ff1", 6), ("w1", 2), ("xa0", 2), ("ctx", 2)):
                    sp.wait_ge(s("ld_" + n), 16 * c)

        @block.gpsimd
        def _(pool):
            own = OwnOrder(pool, s("pool_own"))
            pool.sem_inc(s("ff1_pad"), 2)
            pool.memset(halfs[:, :], -0.5).then_inc(s("const"), 1)
            pool.memset(mean_w[:, :], 1.0 / T).then_inc(s("const"), 1)
            pool.memset(nmax[:, :, :, :, :], 0.0).then_inc(s("const"), 1)
            pool.memset(vaug[:, :, :, :, :], 0.0).then_inc(s("const"), 1)
            pool.wait_ge(s("const"), 4)
            pool.memset(vaug[:, :, :, :, DH:DH + 1], 1.0).then_inc(s("const"), 1)
            pool.wait_ge(s("const"), 5)

            def layernorm(L):
                pool.wait_ge(s(L + "_mv"), NT)
                own.step(pool.tensor_scalar(vare[:, :], mv[:, :, 1], LN_EPS, None, ALU.add))
                pool.tensor_tensor(rstd[:, :], vare[:, :], halfs[:, :], ALU.pow).then_inc(s(L + "_rstd"), 1)

            def attention_values(L, vals):
                with pool.Fori(0, B // 2) as pair:
                    for i in range(2):
                        b = 2 * pair + i
                        pool.wait_ge(s(L + "_pv"), H * b + H)
                        pool.tensor_copy(vaug[:, i, :, :, 0:DH],
                                         vals[:, ds(TPB * b, TPB), :].rearrange("p k (h d) -> p k h d", d=DH)
                                         ).then_inc(s(L + "_vaug"), 1)

            layernorm("at0")
            for u in range(4):
                qk, hf = u % 2, u // 2
                c = slice(hf * HALF, hf * HALF + HALF)
                pool.wait_ge(s("at0_rot"), 2 * (u + 1))
                pool.tensor_tensor(qt1[:, qk, c], qt1[:, qk, c], qt2[:, qk, c], ALU.add).then_inc(s("at0_sum"), 1)
                pool.wait_ge(s("at0_hi"), u + 1)
                pool.tensor_tensor(qlo[:, qk, c], qt1[:, qk, c], qhi[:, qk, c].bitcast(f32), ALU.subtract
                                   ).then_inc(s("at0_lo"), 1)
            pool.wait_ge(s("at0_vev"), 2)
            attention_values("at0", v_tok)
            pool.wait_ge(s("ctx_ek"), 1)
            pool.tensor_tensor(ekv[:, :, :, :], ek[:, :, :, :], ekv[:, :, :, :], ALU.mult).then_inc(s("ctx_ekv"), 1)
            if stop == 0:
                return
            layernorm("xa0")
            if stop == 1:
                return
            layernorm("ff0")
            pool.wait_ge(s("ld_w1"), 32)
            own.mark(pool.tensor_copy(w1hi[:, :, :], w1f))
            own.mark(pool.tensor_copy(w2hi[:, :, :, :], w2f))
            own.wait()
            own.mark(pool.tensor_tensor(w1lo[:, :, :], w1f, w1hi[:, :, :].bitcast(f32), ALU.subtract))
            pool.tensor_tensor(w2lo[:, :, :, :], w2f, w2hi[:, :, :, :].bitcast(f32), ALU.subtract).then_inc(s("w1split"), 1)
            if stop == 2:
                return
            layernorm("at1")
            pool.wait_ge(s("ld_at1"), 7 * 16)
            for i in range(2):
                pool.tensor_copy(rv[:, i, :, 2 * D:2 * D + 2], sincos[:, :, :])
            pool.wait_ge(s("at1_xn"), NT)
            pool.tensor_tensor(x[:, :, :], x[:, :, :], bo1[:, :].unsqueeze(1).broadcast_to([P, NT, D]), ALU.add
                               ).then_inc(s("at1_bo"), 1)
            for b in range(B):
                i = b % 2
                pool.wait_ge(s("at1_qe"), TPB * (b + 1))
                if b >= 2:
                    pool.wait_ge(s("at1_kv"), b - 1)
                for t in range(TPB):
                    for a in range(2):
                        last = pool.tensor_scalar(rv[:, i, t, a * D:a * D + D], qkv[:, i, t, 2 * D:3 * D],
                                                  sincos[:, t, a:a + 1], None, ALU.mult)
                last.then_inc(s("at1_rv"), 1)
                pool.wait_ge(s("at1_nrm"), b + 1)
                pool.tensor_scalar(kc[:, i, :, :], qkv[:, i, :, D:2 * D], -1.0, 1.0, ALU.mult, ALU.add
                                   ).then_inc(s("at1_kc"), 1)
            if stop == 3:
                return
            layernorm("xa1")
            attention_values("xa1", v1_tok)
            if stop == 4:
                return
            layernorm("ff1")
            cur = xnT

            def round_(r):
                for u in range(2 * E1):
                    U, hf = 2 * E1 * r + u, u // E1
                    c = slice(hf * HALF, hf * HALF + HALF)
                    pool.wait_ge(s("ff1_cmb"), 2 + U + 1)
                    pool.wait_ge(s("ff1_pad"), 2 + U)
                    pool.tensor_tensor(cur[:, c], cur[:, c], yw[:, u % 2, :], ALU.add).then_inc(s("ff1_pad"), 1)

            with pool.Fori(0, R1) as r:
                round_(r)

        @block.scalar
        def _(act):
            for L in ("at0", "xa1"):
                act.sem_inc(s(L + "_stkev"), 2)
                act.sem_inc(s(L + "_exp"), 2)
                act.sem_inc(s(L + "_oT"), 1)
            act.sem_inc(s("ff1_gel"), 4)
            act.sem_inc(s("ff1_ctev"), 1)
            act.sem_inc(s("ff1_cwb"), 1)

            def evacuate_xnT(L):
                for hf in range(2):
                    act.wait_ge(s(L + "_xT"), hf + 1)
                    act.activation(xnT[:, hf * HALF:hf * HALF + HALF], ps[:, 6 + hf, :], ACT.Copy
                                   ).then_inc(s(L + "_xnT"), 1)

            for n in range(NT):
                b, jt = n // TPB, n % TPB
                act.wait_ge(s("ctx_pe"), n + 1)
                act.activation(ek[:, jt, b, :], ps[:, n, 0:D], ACT.Copy)
                act.activation(ekv[:, jt, b, :], ps[:, n, D:2 * D], ACT.Copy)
                act.activation(v1_tok[:, n, :], ps[:, n, 2 * D:3 * D], ACT.Copy).then_inc(s("ctx_ev"), 1)
            for hf in range(2):
                act.wait_ge(s("ctx_pe"), NT + hf + 1)
                act.activation(k1hi[:, hf * HALF:hf * HALF + HALF], ps[:, hf, :], ACT.Copy).then_inc(s("ctx_ev"), 1)

            evacuate_xnT("at0")
            for hf in range(2):
                act.wait_ge(s("at0_v"), hf + 1)
                act.activation(v_tok[:, 4 * hf:4 * hf + 4, :], ps[:, 4 + hf, :].rearrange("p (n d) -> p n d", d=D),
                               ACT.Copy).then_inc(s("at0_vev"), 1)
            for u in range(4):
                qk, hf = u % 2, u // 2
                c = slice(hf * HALF, hf * HALF + HALF)
                act.wait_ge(s("at0_sum"), u + 1)
                act.activation(qhi[:, qk, c], qt1[:, qk, c], ACT.Copy).then_inc(s("at0_hi"), 1)
            act.wait_ge(s("ctx_kd"), 1)
            act.activation(ek[:, :, :, :], ek[:, :, :, :], ACT.Exp).then_inc(s("ctx_ek"), 1)
            act.wait_ge(s("ctx_bd"), 1)
            act.activation(expbT[:, :, :], expbT[:, :, :], ACT.Exp).then_inc(s("ctx_ek"), 1)

            def attention(L, causal):
                with act.Fori(0, B // 2) as pair:
                    for i in range(2):
                        b = 2 * pair + i
                        for n in range(4):
                            side, gg = n % 2, n // 2
                            act.wait_ge(s(L + "_stk"), 4 * b + n + 1)
                            dst = stack[:, i, side, 2 * gg:2 * gg + 2, :]
                            src = ps[:, 6 + side, :].rearrange("p (g t) -> p g t", g=2)
                            if side:
                                act.activation(dst, src, ACT.Identity, bias=one_row[:, :]).then_inc(s(L + "_stkev"), 1)
                            else:
                                act.activation(dst, src, ACT.Copy).then_inc(s(L + "_stkev"), 1)
                        for h in range(H):
                            hh = H * b + h
                            act.wait_ge(s(L + "_s"), hh + 1)
                            act.wait_ge(s(L + "_pv"), hh + 32 - 3)
                            act.activation(prob[:, h % 4, :, :],
                                           ps[:, 2 + h % 2, :].rearrange("p (k t) -> p k t", k=TPB),
                                           ACT.Exp, scale=DH ** -0.5).then_inc(s(L + "_exp"), 1)
                            if h in (9, 15):
                                gg = 0 if h == 9 else 1
                                act.wait_ge(s(L + "_pv"), H * b + 32 + 8 * gg + 8)
                                act.activation(oT[:, i, 2 * gg:2 * gg + 2, :],
                                               ps[:, 4, :].rearrange("p (g t) -> p g t", g=2), ACT.Copy
                                               ).then_inc(s(L + "_oT"), 1)
                        if causal:
                            act.wait_ge(s(L + "_onT"), b + 1)
                            act.activation(oNT[:, :, :], ps[:, 5, 0:TPB * P].rearrange("p (t n) -> p t n", t=TPB),
                                           ACT.Copy).then_inc(s(L + "_onTev"), 1)

            attention("at0", False)
            for k in range(2):
                act.wait_ge(s("we_pe"), 4 * (k + 1))
                act.activation(we0[:, 4 * k:4 * k + 4, :], ps[:, 4 + k, :].rearrange("p (e d) -> p e d", d=D),
                               ACT.Copy).then_inc(s("we_ev"), 1)
            if stop == 0:
                return
            evacuate_xnT("xa0")
            for hf in range(2):
                act.wait_ge(s("xa0_q"), hf + 1)
                act.activation(eq[:, hf * HALF:hf * HALF + HALF], ps[:, 0, :], ACT.Exp, scale=-1.0
                               ).then_inc(s("xa0_eq"), 1)
            if stop == 1:
                return
            evacuate_xnT("ff0")
            act.wait_ge(s("ff0_dif"), 1)
            act.activation(dif[:, :], dif[:, :], ACT.Tanh).then_inc(s("ff0_th"), 1)
            if stop == 2:
                return
            evacuate_xnT("at1")
            for b in range(B):
                act.wait_ge(s("at1_sub"), b + 1)
                act.activation(qkv[:, b % 2, :, 0:2 * D], qkv[:, b % 2, :, 0:2 * D], ACT.Exp).then_inc(s("at1_ex"), 1)
                if b >= 1:
                    act.wait_ge(s("at1_aT"), b)
                    act.activation(attT.rearrange("p (l b) -> p b l", b=B)[:, b - 1, :], ps[:, 7, 0:T], ACT.Copy
                                   ).then_inc(s("at1_aTe"), 1)
            act.wait_ge(s("at1_aT"), B)
            act.activation(attT.rearrange("p (l b) -> p b l", b=B)[:, B - 1, :], ps[:, 7, 0:T], ACT.Copy
                           ).then_inc(s("at1_aTe"), 1)
            if stop == 3:
                return
            evacuate_xnT("xa1")
            for hf in range(2):
                act.wait_ge(s("xa1_q"), hf + 1)
                act.activation(qhi[:, 0, hf * HALF:hf * HALF + HALF], ps[:, hf, :], ACT.Copy).then_inc(s("xa1_hi"), 1)
            attention("xa1", True)
            if stop == 4:
                return
            evacuate_xnT("ff1")

            def spread_weights(U, u):
                act.wait_ge(s("ff1_bcd"), U + 1)
                act.activation(cwb[:, u % 8, :], ps[:, 6, :], ACT.Copy).then_inc(s("ff1_cwb"), 1)

            def gelus(U, u):
                for c in range(FC):
                    n = FC * U + c
                    act.wait_ge(s("ff1_up"), n + 1)
                    act.wait_ge(s("ff1_glo"), n + 1)
                    act.activation(gel[:, c, :], ps[:, c, :], ACT.Gelu_apprx_tanh,
                                   bias=b1[:, u % E1, c:c + 1]).then_inc(s("ff1_gel"), 1)

            def gate_tanh(Hf):
                act.wait_ge(s("ff1_dif"), Hf + 1)
                act.activation(dif[:, 0:4 * E1], dif[:, 0:4 * E1], ACT.Tanh).then_inc(s("ff1_th"), 1)

            def gate_rows(Hf, hf):
                act.wait_ge(s("ff1_ct"), Hf + 1)
                act.activation(cwT[:, hf, :], ps[0:2 * E1, 7, :], ACT.Copy).then_inc(s("ff1_ctev"), 1)

            def round_(r, last):
                U0, H0 = 2 * E1 * r, 2 * r
                for u in range(2 * E1):
                    if u == 3:
                        gate_rows(H0 + 1, 1)
                    if u == 7 and not last:
                        gate_rows(H0 + 2, 0)
                    if not (last and u == 7):
                        spread_weights(U0 + u + 1, u + 1)
                        gelus(U0 + u + 1, u + 1)
                    if u == 1:
                        gate_tanh(H0 + 1)
                    if u == 5 and not last:
                        gate_tanh(H0 + 2)

            gate_tanh(0)
            gate_rows(0, 0)
            spread_weights(0, 0)
            gelus(0, 0)
            with act.Fori(0, R1 - 1) as r:
                round_(r, False)
            round_(R1 - 1, True)

        @block.vector
        def _(dve):
            own = OwnOrder(dve, s("dve_own"))
            v = nc.vector
            for L in ("at0", "xa1"):
                dve.sem_inc(s(L + "_red"), 2)
                dve.sem_inc(s(L + "_mrg"), 1)
                dve.sem_inc(s(L + "_on"), 1)
                dve.sem_inc(s(L + "_res"), 1)
            dve.sem_inc(s("ff1_glo"), 4)
            dve.sem_inc(s("ff1_cmb"), 2)

            def layernorm(L):
                own.wait()
                for n in range(NT):
                    own.mark(v.bn_stats(stats[:, n, :], x[:, n, :]))
                own.wait()
                for n in range(NT):
                    v.bn_aggr(mv[:, n, :], stats[:, n, :]).then_inc(s(L + "_mv"), 1)
                dve.wait_ge(s(L + "_rstd"), 1)
                for n in range(NT):
                    v.tensor_scalar(xn[:, n, :], x[:, n, :], mv[:, n, 0:1], rstd[:, n:n + 1], ALU.subtract, ALU.mult
                                    ).then_inc(s(L + "_xn"), 1)

            dve.wait_ge(s("ld_x"), 16)
            dve.wait_ge(s("ld_sel"), 32)
            own.mark(v.tensor_copy(selr[:, :, :, :, :], sel))
            layernorm("at0")
            dve.wait_ge(s("ctx_ev"), NT)
            m01, m23, mk = (big[:, n * 256:n * 256 + 256].rearrange("p (k d) -> p k d", k=TPB) for n in (16, 17, 18))
            own.mark(v.tensor_tensor(m01, ek[:, :, 0, :], ek[:, :, 1, :], ALU.max))
            own.mark(v.tensor_tensor(m23, ek[:, :, 2, :], ek[:, :, 3, :], ALU.max))
            own.wait()
            own.step(v.tensor_tensor(mk, m01, m23, ALU.max))
            for k in range(TPB):
                last = v.tensor_tensor(ek[:, k, :, :], ek[:, k, :, :], mk[:, k:k + 1, :].broadcast_to([P, B, D]),
                                       ALU.subtract)
            last.then_inc(s("ctx_kd"), 1)
            dve.wait_ge(s("ctx_ev"), NT + 2)
            for hf in range(2):
                c = slice(hf * HALF, hf * HALF + HALF)
                v.tensor_tensor(k1lo[:, c], ps[:, hf, :], k1hi[:, c].bitcast(f32), ALU.subtract).then_inc(s("ctx_lo"), 1)
            dve.wait_ge(s("ctx_vm"), 1)
            v.tensor_copy(vmean[:, :, :], ps[:, 2, :].rearrange("p (b d) -> p b d", b=B)).then_inc(s("ctx_lo"), 1)

            dve.wait_ge(s("ld_rope"), 16)
            for u in range(4):
                qk, hf = u % 2, u // 2
                c = slice(hf * HALF, hf * HALF + HALF)
                for part_, dst in ((0, qt1), (1, qt2)):
                    dve.wait_ge(s("at0_qk"), 2 * u + part_ + 1)
                    v.tensor_tensor(dst[:, qk, c].rearrange("p (b t) -> p b t", b=2),
                                    ps[:, 2 * qk + part_, :].rearrange("p (b t) -> p b t", b=2),
                                    rope[:, part_:part_ + 1, :].broadcast_to([P, 2, T]), ALU.mult
                                    ).then_inc(s("at0_rot"), 1)
            dve.wait_ge(s("ld_xa0"), 32)
            v.tensor_tensor(expbT[:, :, :], wbiasT[:, :, :], wbiasT[:, :, :], ALU.subtract).then_inc(s("ctx_bd"), 1)

            def attention(L, causal):
                with dve.Fori(0, B // 2) as pair:
                    own.loop(pair, 2 * (TPB * 3 if causal else TPB * 2))
                    for i in range(2):
                        b = 2 * pair + i
                        for k in range(H + 2):
                            if k < H:
                                dve.wait_ge(s(L + "_mx"), H * b + k + 1)
                                g, j = k // HPG, k % HPG
                                col = QUAD * j + MAXROW
                                v.tensor_reduce(nmax[:, i, :, g, col:col + 1],
                                                ps[:, k % 2, :].rearrange("p (t k) -> p t k", t=TPB), AX.X, ALU.max,
                                                negate=True).then_inc(s(L + "_red"), 1)
                            if k >= 5 and (k - 5) % 4 == 0:
                                g = (k - 5) // 4
                                dve.wait_ge(s(L + "_t"), G * b + g + 1)
                                q = stack[:, i, 0, g, :]
                                v.tensor_tensor(q, ps[:, 5, 0:T], q.bitcast(f32), ALU.add).then_inc(s(L + "_mrg"), 1)
                        for t in range(TPB):
                            dve.wait_ge(s(L + "_o"), TPB * b + t + 1)
                            o = ps[:, 7, :].rearrange("p (h c) -> p h c", c=QUAD)
                            own.step(v.reciprocal(rs[:, t, :].unsqueeze(2), o[:, :, DH:DH + 1]))
                            on = v.tensor_tensor(oN[:, t, :].rearrange("p (h d) -> p h d", d=DH), o[:, :, 0:DH],
                                                 rs[:, t, :].unsqueeze(2).broadcast_to([P, H, DH]), ALU.mult)
                            if causal:
                                own.step(on)
                                own.step(v.tensor_tensor(odif[:, t:t + 1, :], vmean[:, ds(b, 1), :], oN[:, t:t + 1, :],
                                                         ALU.subtract))
                                v.scalar_tensor_tensor(oN[:, t, :], odif[:, t, :], maskf[:, ds(TPB * b + t, 1)],
                                                       oN[:, t, :], ALU.mult, ALU.add).then_inc(s(L + "_on"), 1)
                            else:
                                on.then_inc(s(L + "_on"), 1)
                                dve.wait_ge(s(L + "_on"), 1 + TPB * b + t + 1)
                                xb = x[:, ds(TPB * b + t, 1), :]
                                own.mark(v.tensor_tensor(xb, xb, oN[:, t:t + 1, :], ALU.add))
                        if causal:
                            dve.wait_ge(s(L + "_wo"), b + 1)
                            xb = x[:, ds(TPB * b, TPB), :]
                            v.tensor_tensor(xb, xb, ps[:, 6, 0:TPB * D].rearrange("p (t d) -> p t d", t=TPB), ALU.add
                                            ).then_inc(s(L + "_res"), 1)
                    own.end(B // 2)

            dve.wait_ge(s("const"), 5)
            attention("at0", False)

            def finish():
                own.wait()
                dve.sem_inc(s("final"), 2)
            if stop == 0:
                return finish()
            layernorm("xa0")
            for hf in range(2):
                c = slice(hf * HALF, hf * HALF + HALF)
                dve.wait_ge(s("xa0_eq"), hf + 1)
                dve.wait_ge(s("xa0_dn"), hf + 1)
                own.step(v.scalar_tensor_tensor(den[:, c], eq[:, c], 1.0, ps[:, 1, :], ALU.add, ALU.mult))
                own.step(v.reciprocal(den[:, c], den[:, c]))
                v.tensor_tensor(yT[:, c], ps[:, 2, :], den[:, c], ALU.mult).then_inc(s("xa0_y"), 1)
                dve.wait_ge(s("xa0_o"), hf + 1)
                xb = x[:, 4 * hf:4 * hf + 4, :]
                v.tensor_tensor(xb, xb, ps[:, 3, :].rearrange("p (n d) -> p n d", d=D), ALU.add).then_inc(s("xa0_res"), 1)
            dve.wait_ge(s("xa0_res"), 2)
            if stop == 1:
                return finish()

            def gates_before(lps, bias, tie, n, E):
                m = n * E
                lv, lv3 = lg[:, 0:m], lg[:, 0:m].rearrange("p (n e) -> p n e", e=E)
                if bias is None:
                    own.step(v.tensor_copy(lv3, lps))
                else:
                    own.step(v.tensor_tensor(lv3, lps, bias, ALU.add))
                other = lv3.unsqueeze(2).broadcast_to([P, n, E, E])
                this = lv3.unsqueeze(3).broadcast_to([P, n, E, E])
                gt4 = gt[:, 0:m * E].rearrange("p (n e f) -> p n e f", e=E, f=E)
                eq4 = eqt[:, 0:m * E].rearrange("p (n e f) -> p n e f", e=E, f=E)
                own.mark(v.tensor_tensor(gt4, other, this, ALU.is_gt))
                own.step(v.tensor_tensor(eq4, other, this, ALU.is_equal))
                own.step(v.tensor_tensor(eq4, eq4, tie.unsqueeze(1).broadcast_to([P, n, E, E]), ALU.mult))
                own.step(v.tensor_tensor(gt4, gt4, eq4, ALU.add))
                own.step(v.tensor_reduce(rank[:, 0:m], gt[:, 0:m * E].rearrange("p (m f) -> p m f", f=E), AX.X, ALU.add))
                own.step(v.tensor_scalar(selh[:, 0:m], rank[:, 0:m], 2.0, 0.5, ALU.is_lt, ALU.mult))
                own.step(v.tensor_tensor(lsel[:, 0:m], selh[:, 0:m], lv, ALU.mult))
                own.step(v.tensor_reduce(half_sum[:, 0:n], lsel[:, 0:m].rearrange("p (n e) -> p n e", e=E), AX.X, ALU.add))
                return v.tensor_tensor(dif[:, 0:m].rearrange("p (n e) -> p n e", e=E), lv3,
                                       half_sum[:, 0:n].unsqueeze(2).broadcast_to([P, n, E]), ALU.subtract)

            layernorm("ff0")
            dve.wait_ge(s("ld_gate0"), 32)
            dve.wait_ge(s("ff0_lg"), 1)
            gates_before(ps[:, 4, 0:NT * E0].rearrange("p (n e) -> p n e", e=E0), None, tie0[:, :, :], NT, E0
                         ).then_inc(s("ff0_dif"), 1)
            dve.wait_ge(s("ff0_th"), 1)
            own.step(v.scalar_tensor_tensor(cw[:, :], dif[:, :], 1.0, selh[:, :], ALU.add, ALU.mult))
            for n in range(NT):
                dve.wait_ge(s("ff0_y"), n + 1)
                own_n = v.tensor_tensor(prod[:, n % 2, :, :],
                                        ps[:, 2 * (n % 2):2 * (n % 2) + 2, :].rearrange("p k (e d) -> p (k e) d", d=D),
                                        cw[:, n * E0:n * E0 + E0].unsqueeze(2).broadcast_to([P, E0, D]), ALU.mult)
                own_n.then_inc(s("ff0_pr"), 1)
                dve.wait_ge(s("ff0_pr"), n + 1)
                own.step(v.tensor_reduce(yT[:, 0:D], prod[:, n % 2, :, :].rearrange("p e d -> p d e"), AX.X, ALU.add))
                own.step(v.tensor_tensor(x[:, n, :], x[:, n, :], yT[:, 0:D], ALU.add))
            if stop == 2:
                return finish()

            layernorm("at1")
            dve.wait_ge(s("ld_at1"), 7 * 16)

            def project(b):
                i = b % 2
                for t in range(TPB):
                    n = TPB * b + t
                    dve.wait_ge(s("at1_qkv"), n + 1)
                    v.tensor_tensor(qkv[:, i, t, :], ps[:, n % 2, 0:3 * D], bqkv1[:, :, :].rearrange("p a d -> p (a d)"),
                                    ALU.add).then_inc(s("at1_qe"), 1)
                dve.wait_ge(s("at1_qe"), TPB * (b + 1))
                heads = qkv[:, i, :, 0:2 * D].rearrange("p t (g d) -> p t g d", d=DH)
                own.step(v.tensor_reduce(mxq[:, i, 0:TPB, :], heads, AX.X, ALU.max))
                v.tensor_tensor(heads, heads, mxq[:, i, 0:TPB, :].unsqueeze(3).broadcast_to([P, TPB, 2 * H, DH]),
                                ALU.subtract).then_inc(s("at1_sub"), 1)

            project(0)
            for b in range(B):
                i = b % 2
                if b + 1 < B:
                    project(b + 1)
                dve.wait_ge(s("at1_ex"), b + 1)
                heads = qkv[:, i, :, 0:2 * D].rearrange("p t (g d) -> p t g d", d=DH)
                sums = sumq[:, i, 0:TPB, :]
                own.step(v.tensor_reduce(sums, heads, AX.X, ALU.add))
                own.step(v.reciprocal(sums, sums))
                v.tensor_tensor(heads, heads, sums.unsqueeze(3).broadcast_to([P, TPB, 2 * H, DH]), ALU.mult
                                ).then_inc(s("at1_nrm"), 1)
                dve.wait_ge(s("at1_qT"), b + 1)
                v.tensor_copy(qT[:, i, 0, :], ps[:, 6, 0:T])
                v.tensor_scalar(qT[:, i, 1, :], ps[:, 6, 0:T], -1.0, 1.0, ALU.mult, ALU.add).then_inc(s("at1_qTe"), 1)
                dve.wait_ge(s("at1_kv"), b + 1)
                for a in range(2):
                    halves = bd[:, a, :].rearrange("p (z c) -> p z c", z=2)
                    v.tensor_tensor(halves[:, :, 0:D], ps[:, 4 + a, 0:2 * D].rearrange("p (z c) -> p z c", z=2),
                                    diag[:, :].unsqueeze(1).broadcast_to([P, 2, D]), ALU.mult)
                    last = v.tensor_tensor(halves[:, :, D:D + H],
                                           ps[:, 4 + a, 2 * D:2 * D + 2].unsqueeze(2).broadcast_to([P, 2, H]),
                                           diag_h[:, :].unsqueeze(1).broadcast_to([P, 2, H]), ALU.mult)
                last.then_inc(s("at1_bd"), 1)
                for t in range(TPB):
                    dve.wait_ge(s("at1_out"), TPB * b + t + 1)
                    if b >= 1 and t == 0:
                        dve.wait_ge(s("at1_aT"), b)
                    own.step(v.tensor_scalar(part[:, :, :], ps[:, 2:4, 0:D + H], sincos[:, t, 0:1], None, ALU.mult))
                    own.step(v.scalar_tensor_tensor(comb[:, :, :], ps[:, 2:4, D + H:2 * (D + H)], sincos[:, t, 1:2],
                                                    part[:, :, :], ALU.mult, ALU.add))
                    z = comb[:, :, D:D + H]
                    own.step(v.tensor_scalar(z, z, Z_EPS, None, ALU.max))
                    own.step(v.reciprocal(z, z))
                    own.step(v.tensor_tensor(att2[:, :, :].rearrange("p a (h d) -> p a h d", d=DH),
                                             comb[:, :, 0:D].rearrange("p a (h d) -> p a h d", d=DH),
                                             z.unsqueeze(3).broadcast_to([P, 2, H, DH]), ALU.mult))
                    v.tensor_tensor(att[:, t, :], att2[:, 0, :], att2[:, 1, :], ALU.add).then_inc(s("at1_att"), 1)
            dve.wait_ge(s("at1_bo"), 1)
            for hf in range(2):
                dve.wait_ge(s("at1_wo"), hf + 1)
                xb = x[:, 4 * hf:4 * hf + 4, :]
                own.mark(v.tensor_tensor(xb, xb, ps[:, hf, :].rearrange("p (n d) -> p n d", d=D), ALU.add))
            if stop == 3:
                return finish()

            layernorm("xa1")
            dve.wait_ge(s("ld_xa1"), 64)
            own.mark(v.tensor_scalar(maskf[:, :], mask_i[:, :], 0, None, ALU.not_equal))
            own.wait()
            for hf in range(2):
                c = slice(hf * HALF, hf * HALF + HALF)
                dve.wait_ge(s("xa1_hi"), hf + 1)
                v.tensor_tensor(qlo[:, 0, c], ps[:, hf, :], qhi[:, 0, c].bitcast(f32), ALU.subtract
                                ).then_inc(s("xa1_lo"), 1)
            attention("xa1", True)
            dve.wait_ge(s("xa1_res"), 1 + B)
            if stop == 4:
                return finish()

            layernorm("ff1")
            dve.wait_ge(s("ld_ff1"), 6 * 16)
            own.step(v.tensor_copy(sel_er[:, :, :], sel_e[:, :, :]))
            cur = xnT

            def split_cur(hf):
                c = slice(hf * HALF, hf * HALF + HALF)
                own.step(v.tensor_copy(xhi[:, c], cur[:, c]))
                v.tensor_tensor(xlo[:, c], cur[:, c], xhi[:, c].bitcast(f32), ALU.subtract).then_inc(s("ff1_xs"), 1)

            def gate_a(Hf, r):
                dve.wait_ge(s("ff1_lg"), Hf + 1)
                gates_before(ps[:, 7, 0:4 * E1].rearrange("p (n e) -> p n e", e=E1),
                             bg1[:, ds(r, 1), :].broadcast_to([P, 4, E1]), tie1[:, :, :], 4, E1
                             ).then_inc(s("ff1_dif"), 1)

            def gate_b(Hf):
                m = 4 * E1
                dve.wait_ge(s("ff1_th"), Hf + 1)
                own.step(v.scalar_tensor_tensor(cw[:, 0:m], dif[:, 0:m], 1.0, selh[:, 0:m], ALU.add, ALU.mult))
                own.step(v.tensor_copy(cwr[:, 0:m], cw[:, 0:m]))
                c3, r3 = (a[:, 0:m].rearrange("p (n e) -> p n e", e=E1) for a in (cw, cwr))
                own.mark(v.tensor_copy(cwhl[:, :, 0:E1], r3.bitcast(f32)))
                v.tensor_tensor(cwhl[:, :, E1:2 * E1], c3, r3.bitcast(f32), ALU.subtract).then_inc(s("ff1_cwd"), 1)

            def split_gelus(U, u):
                for c in range(FC):
                    n = FC * U + c
                    dve.wait_ge(s("ff1_gel"), 4 + n + 1)
                    if c == 0:
                        dve.wait_ge(s("ff1_dn"), U + 1)
                    v.tensor_copy(ghi[:, u % 2, c, :], gel[:, c, :]).then_inc(s("ff1_ghi"), 1)
                    dve.wait_ge(s("ff1_ghi"), n + 1)
                    v.tensor_tensor(glo[:, u % 2, c, :], gel[:, c, :], ghi[:, u % 2, c, :].bitcast(f32), ALU.subtract
                                    ).then_inc(s("ff1_glo"), 1)

            def combine(U, u):
                dve.wait_ge(s("ff1_dn"), 2 + U + 1)
                dve.wait_ge(s("ff1_cwb"), 1 + U + 1)
                dve.wait_ge(s("ff1_pad"), U + 1)
                v.scalar_tensor_tensor(yw[:, u % 2, :], ps[:, 4 + u % 2, :], b2[:, u % E1:u % E1 + 1], cwb[:, u, :],
                                       ALU.add, ALU.mult).then_inc(s("ff1_cmb"), 1)

            def round_(r, last):
                U0, H0 = 2 * E1 * r, 2 * r
                for u in range(2 * E1):
                    if u == 0:
                        dve.wait_ge(s("ff1_pad"), U0 + 2)
                        split_cur(1)
                    if u == 4 and not last:
                        dve.wait_ge(s("ff1_pad"), U0 + 2 + E1)
                        split_cur(0)
                    if u == 2:
                        gate_b(H0 + 1)
                    if u == 6 and not last:
                        gate_b(H0 + 2)
                    if not (last and u == 7):
                        split_gelus(U0 + u + 1, u + 1)
                    combine(U0 + u, u)
                    if u == 1:
                        gate_a(H0 + 1, r)
                    if u == 5 and not last:
                        gate_a(H0 + 2, r + 1)

            dve.wait_ge(s("ff1_xnT"), 2)
            split_cur(0)
            gate_a(0, 0)
            gate_b(0)
            split_gelus(0, 0)
            per = 2 * 1 + 2 * (9 + 3)
            with dve.Fori(0, R1 - 1) as r:
                own.loop(r, per)
                round_(r, False)
                own.end(R1 - 1)
            round_(R1 - 1, True)
            for hf in range(2):
                dve.wait_ge(s("fin_T"), hf + 1)
                xb = x[:, 4 * hf:4 * hf + 4, :]
                v.tensor_tensor(xb, xb, ps[:, hf, :].rearrange("p (n d) -> p n d", d=D), ALU.add).then_inc(s("final"), 1)

        @block.tensor
        def _(pe):
            for L in ("at0", "xa1"):
                pe.sem_inc(s(L + "_pv"), 32)
            pe.sem_inc(s("ff1_dn"), 2)

            def transpose_xn(L):
                for n in range(NT):
                    pe.wait_ge(s(L + "_xn"), n + 1)
                    last = pe.transpose(ps[:, 6 + n // 4, (n % 4) * P:(n % 4) * P + P], xn[:, n, :], ident[:, :])
                    if n % 4 == 3:
                        last.then_inc(s(L + "_xT"), 1)

            pe.wait_ge(s("ld_ctx"), 32)
            for n in range(NT):
                pe.matmul(ps[:, n, 0:3 * D], ctxT[:, n * P:n * P + P], wctx[:, 0:3, :], start=True, stop=True
                          ).then_inc(s("ctx_pe"), 1)
            for hf in range(2):
                pe.wait_ge(s("ctx_ev"), hf + 1)
                pe.matmul(ps[:, hf, :], wctx[:, 3, :], ctxT[:, hf * HALF:hf * HALF + HALF], start=True, stop=True
                          ).then_inc(s("ctx_pe"), 1)
            pe.wait_ge(s("const"), 5)
            pe.wait_ge(s("ctx_ev"), NT)
            for b in range(B):
                for k in range(TPB):
                    last = pe.matmul(ps[:, 2, b * D:b * D + D], mean_w[:, :], v1_tok[:, TPB * b + k, :],
                                     start=(k == 0), stop=(k == TPB - 1))
            last.then_inc(s("ctx_vm"), 1)

            pe.wait_ge(s("ld_ident"), 16)
            transpose_xn("at0")
            pe.wait_ge(s("ld_w0"), 16)
            pe.wait_ge(s("ctx_lo"), 3)
            for hf in range(2):
                pe.wait_ge(s("at0_xnT"), hf + 1)
                c = slice(hf * HALF, hf * HALF + HALF)
                for k in range(4):
                    if hf:
                        pe.wait_ge(s("at0_rot"), k + 1)
                    pe.matmul(ps[:, k, :], w0[:, k, :], xnT[:, c], start=True, stop=True).then_inc(s("at0_qk"), 1)
                for n in range(4):
                    tile = 4 * hf + n
                    last = pe.matmul(ps[:, 4 + hf, n * D:n * D + D], xnT[:, tile * P:tile * P + P], w0[:, 4, :],
                                     start=True, stop=True)
                last.then_inc(s("at0_v"), 1)

            def attention(L, causal, k_hi, k_lo):
                def stacks(b, i):
                    pe.wait_ge(s(L + "_on"), TPB * b + 1)
                    if causal:
                        pe.wait_ge(s(L + "_res"), b + 1)
                    for n in range(4):
                        side, gg = n % 2, n // 2
                        hi, lo = ((qhi[:, 0, :], qlo[:, 0, :]), (k_hi, k_lo))[side]
                        pe.wait_ge(s(L + "_stkev"), 4 * b + n + 1)
                        for gl in range(2):
                            o = ps[:, 6 + side, gl * T:gl * T + T]
                            pe.matmul(o, selr[:, side, 2 * gg + gl, 0, :], hi[:, ds(b * T, T)], start=True, stop=False)
                            last = pe.matmul(o, selr[:, side, 2 * gg + gl, 1, :], lo[:, ds(b * T, T)],
                                             start=False, stop=True)
                        last.then_inc(s(L + "_stk"), 1)

                def rows(a, i, side, h):
                    j = h % HPG
                    return stack[QUAD * j:QUAD * j + QUAD, i, side, h // HPG, a]

                with pe.Fori(0, B // 2) as pair:
                    for i in range(2):
                        b = 2 * pair + i
                        stacks(b, i)
                        for k in range(H + 8):
                            if k < H:
                                h = k
                                if h % 8 == 0:
                                    pe.wait_ge(s(L + "_stkev"), 2 + 4 * b + 2 + h // 4)
                                pe.wait_ge(s(L + "_red"), H * b + h + 1)
                                for t in range(TPB):
                                    o = ps[:, h % 2, t * T:t * T + T]
                                    last = pe.matmul(o, rows(slice(t * P, t * P + P), i, 0, h), rows(slice(0, T), i, 1, h),
                                                     start=True, stop=not causal)
                                    if causal:
                                        last = pe.matmul(o, identb[:, :], trib[:, 0, t, :], start=False, stop=True)
                                last.then_inc(s(L + "_mx"), 1)
                            if k >= 5 and (k - 5) % 4 == 0 and (k - 5) // 4 < G:
                                g = (k - 5) // 4
                                pe.wait_ge(s(L + "_red"), 2 + H * b + HPG * g + HPG)
                                pe.wait_ge(s(L + "_mrg"), G * b + g + 1)
                                for t in range(TPB):
                                    last = pe.transpose(ps[:, 5, t * P:t * P + P], nmax[:, i, t, g, :], ident[:, :])
                                last.then_inc(s(L + "_t"), 1)
                            if 6 <= k < H + 6:
                                h = k - 6
                                if h % HPG == 0:
                                    pe.wait_ge(s(L + "_mrg"), 1 + G * b + h // HPG + 1)
                                pe.wait_ge(s(L + "_exp"), H * b + h + 1)
                                for t in range(TPB):
                                    o = ps[:, 2 + h % 2, t * T:t * T + T]
                                    last = pe.matmul(o, rows(slice(t * P, t * P + P), i, 1, h), rows(slice(0, T), i, 0, h),
                                                     start=True, stop=not causal)
                                    if causal:
                                        last = pe.matmul(o, identb[:, :], trib[:, 1, t, :], start=False, stop=True)
                                last.then_inc(s(L + "_s"), 1)
                            if k >= 8:
                                h = k - 8
                                g, j = h // HPG, h % HPG
                                if h == 0:
                                    pe.wait_ge(s(L + "_vaug"), b + 1)
                                if h % 8 == 0:
                                    pe.wait_ge(s(L + "_oT"), TPB * b + h // 8 + 1)
                                pe.wait_ge(s(L + "_exp"), 2 + H * b + h + 1)
                                for t in range(TPB):
                                    last = pe.matmul(ps[QUAD * j:QUAD * j + QUAD, 4, (g % 2) * T:(g % 2) * T + T],
                                                     vaug[:, i, t, h, :], prob[:, h % 4, t, :],
                                                     start=(t == 0), stop=(t == TPB - 1))
                                last.then_inc(s(L + "_pv"), 1)
                        pe.wait_ge(s(L + "_oT"), 1 + 2 * b + 2)
                        for t in range(TPB):
                            pe.wait_ge(s(L + "_on"), TPB * b + t + 1)
                            for g in range(G):
                                last = pe.transpose(ps[:, 7, g * P:g * P + P], oT[:, i, g, t * P:t * P + P], ident[:, :])
                            last.then_inc(s(L + "_o"), 1)
                        if causal:
                            pe.wait_ge(s(L + "_on"), 1 + TPB * b + TPB)
                            for t in range(TPB):
                                last = pe.transpose(ps[:, 5, t * P:t * P + P], oN[:, t, :], ident[:, :])
                            last.then_inc(s(L + "_onT"), 1)
                            pe.wait_ge(s(L + "_onTev"), b + 1)
                            for t in range(TPB):
                                last = pe.matmul(ps[:, 6, t * D:t * D + D], oNT[:, t, :], wx1[:, 1, :],
                                                 start=True, stop=True)
                            last.then_inc(s(L + "_wo"), 1)

            pe.wait_ge(s("at0_lo"), 4)
            pe.wait_ge(s("at0_vev"), 2)
            attention("at0", False, qhi[:, 1, :], qlo[:, 1, :])

            pe.wait_ge(s("ld_ff0"), 32)
            for e in range(E0):
                for c in range(F0 // P):
                    last = pe.matmul(ps[:, 4 + e // 4, (e % 4) * D:(e % 4) * D + D], wi0[:, e, c, :], wo0[:, e, c, :],
                                     start=(c == 0), stop=(c == F0 // P - 1))
                last.then_inc(s("we_pe"), 1)
            if stop == 0:
                return

            transpose_xn("xa0")
            pe.wait_ge(s("ld_xa0"), 32)
            pe.wait_ge(s("ctx_ek"), 2)
            pe.wait_ge(s("ctx_ekv"), 1)
            for hf in range(2):
                pe.wait_ge(s("xa0_xnT"), hf + 1)
                if hf:
                    pe.wait_ge(s("xa0_eq"), 1)
                    pe.wait_ge(s("xa0_y"), 1)
                pe.matmul(ps[:, 0, :], wx0[:, 0, :], xnT[:, hf * HALF:hf * HALF + HALF], start=True, stop=True
                          ).then_inc(s("xa0_q"), 1)
                for bank, src in ((1, ek), (2, ekv)):
                    for bl in range(2):
                        for k in range(TPB):
                            last = pe.matmul(ps[:, bank, bl * T:bl * T + T], src[:, k, 2 * hf + bl, :], expbT[:, k, :],
                                             start=(k == 0), stop=(k == TPB - 1))
                last.then_inc(s("xa0_dn"), 1)
                pe.wait_ge(s("xa0_y"), hf + 1)
                if hf:
                    pe.wait_ge(s("xa0_res"), 1)
                for n in range(4):
                    tile = 4 * hf + n
                    last = pe.matmul(ps[:, 3, n * D:n * D + D], yT[:, tile * P:tile * P + P], wx0[:, 1, :],
                                     start=True, stop=True)
                last.then_inc(s("xa0_o"), 1)
            if stop == 1:
                return

            transpose_xn("ff0")
            pe.wait_ge(s("ld_gate0"), 32)
            pe.wait_ge(s("we_ev"), 2)
            pe.wait_ge(s("ff0_xnT"), 2)
            for n in range(NT):
                last = pe.matmul(ps[:, 4, n * E0:n * E0 + E0], xnT[:, n * P:n * P + P], wgate0[:, :], start=True, stop=True)
            last.then_inc(s("ff0_lg"), 1)
            for n in range(NT):
                if n >= 2:
                    pe.wait_ge(s("ff0_pr"), n - 1)
                for k in range(2):
                    last = pe.matmul(ps[:, 2 * (n % 2) + k, :], xnT[:, n * P:n * P + P], we0[:, 4 * k:4 * k + 4, :],
                                     start=True, stop=True)
                last.then_inc(s("ff0_y"), 1)
            if stop == 2:
                return

            transpose_xn("at1")
            pe.wait_ge(s("ld_at1"), 7 * 16)

            def qkv_tiles(b):
                for t in range(TPB):
                    n = TPB * b + t
                    pe.wait_ge(s("at1_xnT"), n // 4 + 1)
                    if n >= 2:
                        pe.wait_ge(s("at1_qe"), n - 1)
                    pe.matmul(ps[:, n % 2, 0:3 * D], xnT[:, n * P:n * P + P], wqkv1[:, :, :], start=True, stop=True
                              ).then_inc(s("at1_qkv"), 1)

            qkv_tiles(0)
            for b in range(B):
                i = b % 2
                if b + 1 < B:
                    qkv_tiles(b + 1)
                pe.wait_ge(s("at1_nrm"), b + 1)
                if b >= 1:
                    pe.wait_ge(s("at1_qTe"), b)
                else:
                    pe.wait_ge(s("at1_xnT"), 2)
                for t in range(TPB):
                    last = pe.transpose(ps[:, 6, t * P:t * P + P], qkv[:, i, t, 0:D], ident[:, :])
                last.then_inc(s("at1_qT"), 1)
                pe.wait_ge(s("at1_rv"), b + 1)
                pe.wait_ge(s("at1_kc"), b + 1)
                if b >= 1:
                    pe.wait_ge(s("at1_bd"), b)
                for a in range(2):
                    for t in range(TPB):
                        keys = (qkv[:, i, t, D:2 * D], kc[:, i, t, :])[a]
                        last = pe.matmul(ps[:, 4 + a, 0:2 * D + 2], keys, rv[:, i, t, :],
                                         start=(t == 0), stop=(t == TPB - 1))
                last.then_inc(s("at1_kv"), 1)
                pe.wait_ge(s("at1_bd"), b + 1)
                pe.wait_ge(s("at1_qTe"), b + 1)
                for t in range(TPB):
                    if TPB * b + t >= 1:
                        pe.wait_ge(s("at1_att"), TPB * b + t)
                    for a in range(2):
                        last = pe.matmul(ps[:, 2 + a, 0:2 * (D + H)], qT[:, i, a, t * P:t * P + P], bd[:, a, :],
                                         start=True, stop=True)
                    last.then_inc(s("at1_out"), 1)
                pe.wait_ge(s("at1_att"), TPB * (b + 1))
                if b >= 1:
                    pe.wait_ge(s("at1_aTe"), b)
                for t in range(TPB):
                    last = pe.transpose(ps[:, 7, t * P:t * P + P], att[:, t, :], ident[:, :])
                last.then_inc(s("at1_aT"), 1)
            pe.wait_ge(s("at1_aTe"), B)
            for hf in range(2):
                for n in range(4):
                    r = 4 * hf + n
                    last = pe.matmul(ps[:, hf, n * D:n * D + D], attT[:, r * P:r * P + P], wo1[:, :], start=True, stop=True)
                last.then_inc(s("at1_wo"), 1)
            if stop == 3:
                return

            transpose_xn("xa1")
            pe.wait_ge(s("ld_xa1"), 64)
            for hf in range(2):
                pe.wait_ge(s("xa1_xnT"), hf + 1)
                pe.matmul(ps[:, hf, :], wx1[:, 0, :], xnT[:, hf * HALF:hf * HALF + HALF], start=True, stop=True
                          ).then_inc(s("xa1_q"), 1)
            pe.wait_ge(s("xa1_lo"), 2)
            attention("xa1", True, k1hi[:, :], k1lo[:, :])
            if stop == 4:
                return

            transpose_xn("ff1")
            cur = xnT
            pe.wait_ge(s("ff1_xnT"), 2)
            pe.wait_ge(s("ld_ff1"), 6 * 16)
            pe.wait_ge(s("w1split"), 1)

            def logits(Hf, hf, r):
                pe.wait_ge(s("ff1_ctev"), Hf + 1)
                for n in range(4):
                    tile = 4 * hf + n
                    last = pe.matmul(ps[:, 7, n * E1:n * E1 + E1], cur[:, tile * P:tile * P + P],
                                     wg1[:, ds(r, 1), :], start=True, stop=True)
                last.then_inc(s("ff1_lg"), 1)

            def gate_rows(Hf):
                pe.wait_ge(s("ff1_cwd"), Hf + 1)
                for n in range(4):
                    last = pe.transpose(ps[0:2 * E1, 7, n * P:n * P + P], cwhl[:, n, :], ident[:, :])
                last.then_inc(s("ff1_ct"), 1)

            def up(U, u):
                u = u % (2 * E1)
                hf, e = u // E1, u % E1
                if e == 0:
                    pe.wait_ge(s("ff1_ctev"), 1 + U // E1 + 1 if isinstance(U, int) else 0) if False else None
                c = slice(hf * HALF, hf * HALF + HALF)
                pe.wait_ge(s("ff1_cwb"), U + 1)
                pe.matmul(ps[:, 6, :], sel_er[:, e, :], cwT[:, hf, :], start=True, stop=True).then_inc(s("ff1_bcd"), 1)
                for k in range(FC):
                    pe.wait_ge(s("ff1_gel"), FC * U + k + 1)
                    f = slice(k * P, k * P + P)
                    pe.matmul(ps[:, k, :], w1hi[:, e, f], xhi[:, c], start=True, stop=False)
                    pe.matmul(ps[:, k, :], w1lo[:, e, f], xhi[:, c], start=False, stop=False)
                    pe.matmul(ps[:, k, :], w1hi[:, e, f], xlo[:, c], start=False, stop=True).then_inc(s("ff1_up"), 1)

            def down(U, u):
                e = u % E1
                pe.wait_ge(s("ff1_cmb"), U + 1)
                o = ps[:, 4 + u % 2, :]
                for k in range(FC):
                    pe.wait_ge(s("ff1_glo"), 4 + FC * U + k + 1)
                    pe.matmul(o, w2hi[:, e, k, :], ghi[:, u % 2, k, :], start=(k == 0), stop=False)
                    pe.matmul(o, w2lo[:, e, k, :], ghi[:, u % 2, k, :], start=False, stop=False)
                    last = pe.matmul(o, w2hi[:, e, k, :], glo[:, u % 2, k, :], start=False, stop=(k == FC - 1))
                last.then_inc(s("ff1_dn"), 1)

            def round_(r, last):
                U0, H0 = 2 * E1 * r, 2 * r
                for u in range(2 * E1):
                    if u == 1:
                        pe.wait_ge(s("ff1_pad"), U0 + 2)
                        logits(H0 + 1, 1, r)
                    if u == 5 and not last:
                        pe.wait_ge(s("ff1_pad"), U0 + 2 + E1)
                        logits(H0 + 2, 0, r + 1)
                    if u == 3:
                        pe.wait_ge(s("ff1_ctev"), 1 + H0 + 2)
                        pe.wait_ge(s("ff1_xs"), H0 + 2)
                    if u == 7 and not last:
                        pe.wait_ge(s("ff1_ctev"), 1 + H0 + 3)
                        pe.wait_ge(s("ff1_xs"), H0 + 3)
                    if not (last and u == 7):
                        up(U0 + u + 1, u + 1)
                    down(U0 + u, u)
                    if u == 2:
                        gate_rows(H0 + 1)
                    if u == 6 and not last:
                        gate_rows(H0 + 2)

            logits(0, 0, 0)
            gate_rows(0)
            pe.wait_ge(s("ff1_ctev"), 2)
            pe.wait_ge(s("ff1_xs"), 1)
            up(0, 0)
            with pe.Fori(0, R1 - 1) as r:
                round_(r, False)
            round_(R1 - 1, True)
            pe.wait_ge(s("ff1_pad"), 2 + 2 * E1 * R1)
            for hf in range(2):
                for n in range(4):
                    tile = 4 * hf + n
                    last = pe.transpose(ps[:, hf, n * P:n * P + P], cur[:, tile * P:tile * P + P], ident[:, :])
                last.then_inc(s("fin_T"), 1)


def shape_constants():
    import numpy as np
    f = np.float32
    c = {"ident": np.eye(P, dtype=f)}
    inv_freq = (f(1.0) / f(10000.0) ** (np.arange(0, DH, 2, dtype=f) / f(DH))).astype(f)
    angle = np.outer(np.arange(T, dtype=f), inv_freq).astype(f)
    pair = (np.arange(D) % DH) // 2
    sign = np.where(np.arange(D) % 2 == 0, -1, 1).astype(f)
    c["rope"] = np.ascontiguousarray(np.stack([np.cos(angle)[:, pair].T, np.sin(angle)[:, pair].T * sign[:, None]], 1)).astype(f)
    sel = np.zeros((P, 2, G, 2, P), f)
    for g in range(G):
        for j in range(HPG):
            for d in range(DH):
                src = (HPG * g + j) * DH + d
                for side, parts in enumerate(((0, 1, 0), (0, 0, 1))):
                    for copy, part in enumerate(parts):
                        sel[src, side, g, part, QUAD * j + DH * copy + d] = 1
    c["sel"] = sel
    c["one_row"] = (np.arange(P) % QUAD == MAXROW).astype(f).reshape(P, 1)
    p, t = np.arange(P)[:, None, None], np.arange(TPB)[None, :, None]
    other = np.arange(T)[None, None, :]
    c["tri"] = np.stack([np.where(other > p + P * t, -1e9, 0), np.where(p + P * t > other, -1e9, 0)], 1).astype(np.dtype("bfloat16"))
    c["identb"] = np.eye(P, dtype=np.dtype("bfloat16"))
    idx = (f(np.pi / 2) * np.arange(1, T + 1, dtype=f) / f(T)).astype(f)
    c["sincos"] = np.ascontiguousarray(np.stack([np.sin(idx), np.cos(idx)], 1).reshape(TPB, P, 2).transpose(1, 0, 2)).astype(f)
    head = np.arange(D) // DH
    c["diag"] = (head[:, None] == head[None, :]).astype(f)
    c["diag_h"] = (head[:, None] == np.arange(H)[None, :]).astype(f)
    for n, E in (("tie0", E0), ("tie1", E1)):
        c[n] = (np.arange(E)[None, :] < np.arange(E)[:, None]).astype(f)
    c["sel_e"] = np.ascontiguousarray(np.broadcast_to(
        (np.arange(2 * E1)[:, None] % E1 == np.arange(E1)[None, :])[:, :, None], (2 * E1, E1, P))).astype(f)
    return c


def laid_out(a):
    import numpy as np
    T_ = lambda m: np.ascontiguousarray(np.asarray(m).T)
    swap = np.arange(D) ^ 1
    w = {
        "x": np.asarray(a["x"]).reshape(B * T, D),
        "ctxT": T_(np.asarray(a["ctx_1024"]).reshape(B * T, D)),
        "w0": np.stack([T_(a["L0_attn_wq"]), T_(np.asarray(a["L0_attn_wq"])[swap]), T_(a["L0_attn_wk"]),
                        T_(np.asarray(a["L0_attn_wk"])[swap]), T_(a["L0_attn_wv"])], 1),
        "wctx": np.stack([T_(a["L0_xattn_Wk"]), T_(a["L0_xattn_Wv"]), np.asarray(a["L1_xattn_WV"]),
                          np.asarray(a["L1_xattn_WK"])], 1),
        "wx0": np.stack([T_(a["L0_xattn_Wq"]), T_(a["L0_xattn_Wo"])], 1),
        "wbiasT": T_(a["L0_xattn_W_bias"]).reshape(TPB, P, T).transpose(1, 0, 2),
        "wgate0": T_(a["L0_ffn_w_gate"]),
        "wi0": np.asarray(a["L0_ffn_w_in"]).reshape(E0, F0 // P, P, D).transpose(2, 0, 1, 3),
        "wo0": np.asarray(a["L0_ffn_w_out"]).transpose(0, 2, 1).reshape(E0, F0 // P, P, D).transpose(2, 0, 1, 3),
        "wqkv1": np.stack([np.asarray(a["L1_attn_W" + n]) for n in "qkv"], 1),
        "bqkv1": np.stack([np.asarray(a["L1_attn_b" + n]) for n in "qkv"], 0),
        "wo1": np.asarray(a["L1_attn_Wo"]),
        "bo1": np.asarray(a["L1_attn_bo"]),
        "wx1": np.stack([np.asarray(a["L1_xattn_WQ"]), np.asarray(a["L1_xattn_WO"])], 1),
        "mask": np.asarray(a["mask_BxS2_ik0"]).reshape(NT, P).T,
        "wg1": np.asarray(a["L1_ffn_Wg"]).transpose(1, 0, 2),
        "bg1": np.asarray(a["L1_ffn_bg"]),
        "w1": np.asarray(a["L1_ffn_W1"]).transpose(1, 0, 2),
        "b1": np.asarray(a["L1_ffn_b1"]).reshape(E1, FC, P).transpose(2, 0, 1),
        "w2": np.asarray(a["L1_ffn_W2"]).reshape(E1, FC, P, D).transpose(2, 0, 1, 3),
        "b2": T_(a["L1_ffn_b2"]),
    }
    w.update(shape_constants())
    return {"in_" + n: np.ascontiguousarray(m) for n, m in w.items()}


def kernel(**inputs):
    import numpy as np
    import concourse.bacc as bacc
    from concourse.bass_utils import run_bass_kernel_spmd

    arrays = laid_out(inputs)
    nc = bacc.Bacc("TRN2", target_bir_lowering=False, num_devices=1)
    w = {n[3:]: nc.dram_tensor(n, m.shape, mybir.dt.from_np(m.dtype), kind="ExternalInput").ap() for n, m in arrays.items()}
    out = nc.dram_tensor("out", (B * T, D), mybir.dt.float32, kind="ExternalOutput").ap()
    decoder_kernel(nc, w, out)
    r = run_bass_kernel_spmd(nc, [arrays], core_ids=[0])
    return np.asarray(r.results[0]["out"]).reshape(B, T, D)
```

```python
import concourse.bass as bass
from concourse import mybir
from contextlib import ExitStack

B, T, D = 4, 256, 128
H, DH = 16, 8
P = 128
NT = B * T // P
TPB = T // P
HALF = B * T // 2
HPG = 4
G = H // HPG
QUAD = P // HPG
MAXROW = 3 * DH
E0, F0 = 8, 512
E1, F1, R1 = 4, 512, 4
FC = F1 // P
LN_EPS, Z_EPS = 1e-5, 1e-6


class OwnOrder:

    def __init__(self, engine, semaphore):
        self.engine, self.semaphore, self.base, self.n = engine, semaphore, 0, 0

    def mark(self, instruction):
        instruction.then_inc(self.semaphore, 1)
        self.n += 1

    def wait(self):
        self.engine.wait_ge(self.semaphore, self.base + self.n)

    def step(self, instruction):
        self.mark(instruction)
        self.wait()

    def loop(self, i, per):
        self.outer, self.per = self.base + self.n, per
        self.base, self.n = i * per + self.outer, 0

    def end(self, count):
        assert self.n == self.per, self.n
        self.base, self.n = self.outer + count * self.per, 0


def decoder_kernel(nc, w, out, stop=99):
    f32, f32r, bf16 = mybir.dt.float32, mybir.dt.float32r, mybir.dt.bfloat16
    ALU, ACT, AX = mybir.AluOpType, mybir.ActivationFunctionType, mybir.AxisListType
    ds = bass.ds
    ctx = ExitStack()
    with ctx:
        def sb(name, shape, dt=f32):
            return ctx.enter_context(nc.sbuf_tensor(name, shape, dt))

        def sem(name):
            return ctx.enter_context(nc.semaphore(name))

        x = sb("x", [P, NT, D])
        ident = sb("ident", [P, P])
        identb = sb("identb", [P, P], bf16)
        trib = sb("trib", [P, TPB + 1, P], bf16)
        one_row = sb("one_row", [P, 1])
        sincos = sb("sincos", [P, TPB, 2])
        diag = sb("diag", [P, P])
        diag_h = sb("diag_h", [P, H])
        tie0 = sb("tie0", [P, E0, E0])
        tie1 = sb("tie1", [P, E1, E1])
        wgate0 = sb("wgate0", [P, E0])
        wi0 = sb("wi0", [P, E0, F0 // P, D])
        wo0 = sb("wo0", [P, E0, F0 // P, D])
        wqkv1 = sb("wqkv1", [P, 3, D])
        bqkv1 = sb("bqkv1", [P, 3, D])
        wo1 = sb("wo1", [P, D])
        bo1 = sb("bo1", [P, D])
        wx1 = sb("wx1", [P, 2, D])
        mask_i = sb("mask_i", [P, NT], mybir.dt.int32)
        wg1 = sb("wg1", [P, R1, E1])
        bg1 = sb("bg1", [P, R1, E1])
        b1 = sb("b1", [P, E1, FC])
        b2 = sb("b2", [P, E1])

        selr = sb("selr", [P, 2, G, 2, P], f32r)
        mean_w = sb("mean_w", [P, P])
        halfs = sb("halfs", [P, NT])
        v1_tok = sb("v1_tok", [P, NT, D])
        k1hi = sb("k1hi", [P, B * T], f32r)
        k1lo = sb("k1lo", [P, B * T], f32r)
        maskf = sb("maskf", [P, NT])

        early = ExitStack()

        def sb_early(name, shape, dt=f32):
            return early.enter_context(nc.sbuf_tensor(name, shape, dt))

        rope = sb_early("rope", [P, 2, T])
        w0 = sb_early("w0", [P, 5, D])
        ctxT = sb_early("ctxT", [P, B * T])
        wctx = sb_early("wctx", [P, 4, D])
        wx0 = sb_early("wx0", [P, 2, D])
        wbiasT = sb_early("wbiasT", [P, TPB, T])
        expbT = sb_early("expbT", [P, TPB, T])
        ek = sb_early("ek", [P, TPB, B, D])
        ekv = sb_early("ekv", [P, TPB, B, D])
        v_tok = sb_early("v_tok", [P, NT, D])
        early.close()
        w1hi = sb("w1hi", [P, E1, F1], f32r)
        w1lo = sb("w1lo", [P, E1, F1], f32r)
        w2hi = sb("w2hi", [P, E1, FC, D], f32r)
        w2lo = sb("w2lo", [P, E1, FC, D], f32r)
        cwT = sb("cwT", [2 * E1, 2, HALF], f32r)
        sel_er = sb("sel_er", [2 * E1, E1, P], f32r)

        stats = sb("stats", [P, NT, 6])
        mv = sb("mv", [P, NT, 2])
        rstd = sb("rstd", [P, NT])
        vare = sb("vare", [P, NT])
        xn = sb("xn", [P, NT, D])
        xnT = sb("xnT", [P, B * T])
        big = sb("big", [P, 8192])
        bigr = sb("bigr", [P, 8192], f32r)
        ps = ctx.enter_context(nc.psum_tensor("ps", [P, 8, 512], f32))

        w1f = wo0[:, 0:E1, :, :].rearrange("p e c d -> p e (c d)")
        w2f = wi0[:, 0:E1, :, :]
        sel = big[:, 4096:6144].rearrange("p (a g i m) -> p a g i m", a=2, g=G, i=2)
        rot1 = (big[:, 0:1024].rearrange("p (a n) -> p a n", a=2),
                xn[:, :, :].rearrange("p (a t) d -> p a (t d)", a=2))
        rot2 = tuple(big[:, n:n + 1024].rearrange("p (a n) -> p a n", a=2) for n in (1024, 7168))
        ctx_max = big[:, 6144:6912].rearrange("p (m k d) -> p m k d", m=3, k=TPB)
        qhi = bigr[:, 0:2048].rearrange("p (a n) -> p a n", a=2)
        qlo = bigr[:, 2048:4096].rearrange("p (a n) -> p a n", a=2)
        qs = sb("qs", [P, G, T], f32r)
        ks = sb("ks", [P, G, T], f32r)
        km = bigr[:, 4096:8192].rearrange("p (h t) -> p h t", h=H)
        vaug = sb("vaug", [P, TPB, H, QUAD])
        nmax = sb("nmax", [P, TPB, G, P])
        prob = big[:, 0:4096].rearrange("p (s n) -> p s n", s=8)
        oT = big[:, 6144:7168].rearrange("p (g t) -> p g t", g=G)
        gt, eqt = (xn[:, n:n + 4, :].rearrange("p n d -> p (n d)") for n in (0, 4))
        we0 = big[:, 7168:8192].rearrange("p (e d) -> p e d", e=E0)
        eq = big[:, 0:1024]
        den = big[:, 1024:2048]
        yT = big[:, 2048:3072]
        prod = big[:, 0:2048].rearrange("p (i e d) -> p i e d", i=2, e=E0)
        qkv = big[:, 0:1536].rearrange("p (i t c) -> p i t c", i=2, t=TPB)
        kc = big[:, 1536:2048].rearrange("p (i t c) -> p i t c", i=2, t=TPB)
        rv = big[:, 2048:3080].rearrange("p (i t c) -> p i t c", i=2, t=TPB)
        qT = big[:, 3080:4104].rearrange("p (i a c) -> p i a c", i=2, a=2)
        bd = big[:, 4104:4680].rearrange("p (a c) -> p a c", a=2)
        part = big[:, 4680:4968].rearrange("p (a c) -> p a c", a=2)
        comb = big[:, 4968:5256].rearrange("p (a c) -> p a c", a=2)
        att2 = big[:, 5256:5512].rearrange("p (a c) -> p a c", a=2)
        att = big[:, 5512:5768].rearrange("p (t c) -> p t c", t=TPB)
        attT = big[:, 5768:6792]
        gel = big[:, 0:2048].rearrange("p (s n) -> p s n", s=4)
        cwb = big[:, 2048:6144].rearrange("p (u n) -> p u n", u=8)
        yw = big[:, 6144:7168].rearrange("p (u n) -> p u n", u=2)
        ghi = bigr[:, 0:4096].rearrange("p (u c n) -> p u c n", u=2, c=FC)
        glo = bigr[:, 4096:8192].rearrange("p (u c n) -> p u c n", u=2, c=FC)
        xhi, xlo = k1hi, k1lo
        oN = sb("oN", [P, TPB, D])
        odif = sb("odif", [P, TPB, D])
        vmean = sb("vmean", [P, B, D])
        mxq = sb("mxq", [P, 2, 2 * TPB, 32])
        sumq = sb("sumq", [P, 2, 2 * TPB, 32])
        lg = sb("lg", [P, NT * E0])
        rank = sb("rank", [P, NT * E0])
        selh = sb("selh", [P, NT * E0])
        lsel = sb("lsel", [P, NT * E0])
        half_sum = sb("half_sum", [P, NT])
        dif = sb("dif", [P, NT * E0])
        cw = sb("cw", [P, NT * E0])
        cwr = sb("cwr", [P, NT * E0], f32r)
        cwhl = sb("cwhl", [P, 4, 2 * E1])
        sel_e = sb("sel_e", [2 * E1, E1, P])
        oNT = sb("oNT", [P, TPB, P])
        rs = sb("rs", [P, TPB, H])

        S = {}

        def s(name):
            if name not in S:
                S[name] = sem(name)
            return S[name]

        LAYERS = ("at0", "xa0", "ff0", "at1", "xa1", "ff1")

        def ln(L, each):
            return each * LAYERS.index(L)

        block = ctx.enter_context(nc.Block())

        def wait(engine, semaphore, value):
            if not isinstance(value, int) or value > 0:
                engine.wait_ge(semaphore, value)

        def there(b):
            return not isinstance(b, int) or b >= 0

        def place(t):
            return TPB - 1 - t

        def pipelined(engine, step, before_first=None, before_loop=None):
            def batch(b, first, follow):
                for k in range(H):
                    if not first:
                        step(H + k, b - 1, follow)
                    step(k, b, follow)

            for k in range(H // 2 - 1, H):
                step(k, -1, True)
            if before_first:
                before_first()
            batch(0, True, True)
            if before_loop:
                before_loop()
            with engine.Fori(1, B - 1) as b:
                batch(b, False, True)
            batch(B - 1, False, False)
            for k in range(H, 2 * H):
                step(k, B - 1, None)

        @block.sync
        def _(sp):
            def load(name, dst, src):
                sp.dma_start(dst, src).then_inc(s("ld_" + name), 16)
            load("x", x[:, :, :], w["x"].rearrange("(n p) d -> p n d", p=P))
            load("w0", w0[:, :, :], w["w0"])
            load("rope", rope[:, :, :], w["rope"])
            load("sel", sel, w["sel"])
            load("sel", one_row[:, :], w["one_row"])
            load("xa0", wx0[:, :, :], w["wx0"])
            load("xa0", wbiasT[:, :, :], w["wbiasT"])
            load("gate0", wgate0[:, :], w["wgate0"])
            load("gate0", tie0[:, :, :], w["tie0"].partition_broadcast(P))
            load("at1", wqkv1[:, :, :], w["wqkv1"])
            load("at1", bqkv1[:, :, :], w["bqkv1"].partition_broadcast(P))
            load("at1", wo1[:, :], w["wo1"])
            load("at1", bo1[:, :], w["bo1"].partition_broadcast(P))
            load("at1", sincos[:, :, :], w["sincos"])
            load("at1", diag[:, :], w["diag"])
            load("at1", diag_h[:, :], w["diag_h"])
            load("xa1", wx1[:, :, :], w["wx1"])
            load("xa1", trib[:, :, :], w["tri"])
            load("xa1", identb[:, :], w["identb"])
            load("xa1", mask_i[:, :], w["mask"])
            load("ff1", wg1[:, :, :], w["wg1"])
            load("ff1", bg1[:, :, :], w["bg1"].partition_broadcast(P))
            load("ff1", b1[:, :, :], w["b1"])
            load("ff1", b2[:, :], w["b2"])
            load("ff1", tie1[:, :, :], w["tie1"].partition_broadcast(P))
            load("ff1", sel_e[:, :, :], w["sel_e"])
            load("ff0", wi0[:, :, :, :], w["wi0"])
            load("ff0", wo0[:, :, :, :], w["wo0"])

            def attention_keys(L):
                def keys(b, g):
                    if g % 2 == 0:
                        sp.wait_ge(s(L + "_ksev"), 1 + 2 * b + g // 2 + 1)
                        sp.sem_inc(s("keys_stacked"), 1)
                    sp.wait_ge(s(L + "_s"), H * b + HPG * g + HPG)
                    for j in range(HPG):
                        rows = slice(QUAD * j, QUAD * j + QUAD)
                        sp.dma_start(km[rows, HPG * g + j, :].bitcast(f32), ks[rows, g, :].bitcast(f32)
                                     ).then_inc(s(L + "_km%d" % g), 16)

                for g in range(G):
                    keys(0, g)
                with sp.Fori(1, B) as b:
                    for g in range(G):
                        keys(b, g)

            attention_keys("at0")
            sp.wait_ge(s("we_pe"), E0)
            load("w1", w1f, w["w1"])
            load("w1", w2f, w["w2"])
            if stop >= 4:
                attention_keys("xa1")
            sp.wait_ge(s("final"), 2)
            sp.dma_start(out.rearrange("(n p) d -> p n d", p=P), x[:, :, :]).then_inc(s("stored"), 16)
            sp.wait_ge(s("stored"), 16)
            if stop < 5:
                for n, c in (("ff0", 2), ("gate0", 2), ("at1", 7), ("xa1", 4), ("ff1", 6), ("w1", 2), ("xa0", 2), ("ctx", 2)):
                    sp.wait_ge(s("ld_" + n), 16 * c)

        @block.gpsimd
        def _(pool):
            own = OwnOrder(pool, s("pool_own"))
            pool.sem_inc(s("ff1_pad"), 2)
            pool.memset(halfs[:, :], -0.5).then_inc(s("const"), 1)
            pool.memset(mean_w[:, :], 1.0 / T).then_inc(s("const"), 1)
            pool.memset(nmax[:, :, :, :], 0.0).then_inc(s("const"), 1)
            pool.memset(vaug[:, :, :, :], 0.0).then_inc(s("const"), 1)
            pool.memset(km[:, :, :].bitcast(f32), 0.0).then_inc(s("const"), 1)
            pool.wait_ge(s("const"), 5)
            pool.memset(vaug[:, :, :, DH:DH + 1], 1.0).then_inc(s("const"), 1)
            pool.wait_ge(s("const"), 6)

            def layernorm(L):
                pool.wait_ge(s("ln_mv"), ln(L, NT) + NT)
                own.step(pool.tensor_scalar(vare[:, :], mv[:, :, 1], LN_EPS, None, ALU.add))
                pool.tensor_tensor(rstd[:, :], vare[:, :], halfs[:, :], ALU.pow).then_inc(s("ln_rstd"), 1)

            def attention_values(L, vals):
                with pool.Fori(0, B) as b:
                    for g in range(G):
                        pool.wait_ge(s(L + "_pv"), G * b + g + 1)
                        pool.tensor_copy(vaug[:, :, HPG * g:HPG * g + HPG, 0:DH],
                                         vals[:, ds(TPB * b, TPB), HPG * DH * g:HPG * DH * (g + 1)]
                                         .rearrange("p k (h d) -> p k h d", d=DH)).then_inc(s(L + "_vaug"), 1)

            layernorm("at0")
            for n, a in enumerate((1, 0)):
                pool.wait_ge(s("at0_rot"), 4 + 2 * (n + 1))
                pool.tensor_tensor(rot1[1][:, a, :], rot1[1][:, a, :], rot2[1][:, a, :], ALU.add).then_inc(s("at0_sum1"), 1)
            pool.wait_ge(s("ctx_mx"), 1)
            for k in range(TPB):
                pool.tensor_tensor(ek[:, k, :, :], ek[:, k, :, :],
                                   ctx_max[:, 2, k:k + 1, :].broadcast_to([P, B, D]), ALU.subtract).then_inc(s("ctx_kd"), 1)
            pool.wait_ge(s("ld_xa0"), 32)
            pool.tensor_tensor(expbT[:, :, :], wbiasT[:, :, :], wbiasT[:, :, :], ALU.subtract).then_inc(s("ctx_kd"), 1)
            for n, a in enumerate((1, 0)):
                pool.wait_ge(s("at0_hi"), 2 + n + 1)
                pool.tensor_tensor(qlo[:, a, HALF:2 * HALF], rot1[1][:, a, :], qhi[:, a, HALF:2 * HALF].bitcast(f32),
                                   ALU.subtract).then_inc(s("at0_lo1"), 1)
            pool.wait_ge(s("at0_vev"), 2)
            attention_values("at0", v_tok)
            pool.wait_ge(s("ctx_ek"), 1)
            pool.tensor_tensor(ekv[:, :, :, :], ek[:, :, :, :], ekv[:, :, :, :], ALU.mult).then_inc(s("ctx_ekv"), 1)
            if stop == 0:
                return
            layernorm("xa0")
            if stop == 1:
                return
            layernorm("ff0")

            def weights_rest(e):
                pool.wait_ge(s("w1_hi"), e + 1)
                pool.tensor_tensor(w1lo[:, e, :], w1f[:, e, :], w1hi[:, e, :].bitcast(f32), ALU.subtract
                                   ).then_inc(s("w1_lo"), 1)
                pool.tensor_tensor(w2lo[:, e, :, :], w2f[:, e, :, :], w2hi[:, e, :, :].bitcast(f32), ALU.subtract
                                   ).then_inc(s("w1_lo"), 1)

            for e in range(2):
                weights_rest(e)
            for n in range(NT):
                pool.wait_ge(s("ff0_pa"), n + 1)
                pool.wait_ge(s("ff0_pd"), n + 1)
                pool.tensor_tensor(prod[:, n % 2, 0:4, :], prod[:, n % 2, 0:4, :], prod[:, n % 2, 4:8, :], ALU.add
                                   ).then_inc(s("ff0_ps"), 1)
            if stop == 2:
                return
            layernorm("at1")
            pool.wait_ge(s("ld_at1"), 7 * 16)
            for i in range(2):
                pool.tensor_copy(rv[:, i, :, 2 * D:2 * D + 2], sincos[:, :, :])
            pool.wait_ge(s("ln_xn"), ln("at1", NT) + NT)
            pool.tensor_tensor(x[:, :, :], x[:, :, :], bo1[:, :].unsqueeze(1).broadcast_to([P, NT, D]), ALU.add
                               ).then_inc(s("at1_bo"), 1)

            def values(b):
                i = b % 2
                pool.wait_ge(s("at1_qe"), TPB * (b + 1))
                if b >= 2:
                    pool.wait_ge(s("at1_kv"), b - 1)
                for t in range(TPB):
                    for a in range(2):
                        last = pool.tensor_scalar(rv[:, i, t, a * D:a * D + D], qkv[:, i, t, 2 * D:3 * D],
                                                  sincos[:, t, a:a + 1], None, ALU.mult)
                last.then_inc(s("at1_rv"), 1)

            values(0)
            for b in range(B):
                pool.wait_ge(s("at1_nrm"), b + 1)
                pool.tensor_scalar(kc[:, b % 2, :, :], qkv[:, b % 2, :, D:2 * D], -1.0, 1.0, ALU.mult, ALU.add
                                   ).then_inc(s("at1_kc"), 1)
                if b + 1 < B:
                    values(b + 1)
            for e in range(2, E1):
                weights_rest(e)
            if stop == 3:
                return
            layernorm("xa1")
            attention_values("xa1", v1_tok)
            if stop == 4:
                return
            layernorm("ff1")
            cur = xnT

            def round_(r):
                for u in range(2 * E1):
                    U, hf = 2 * E1 * r + u, u // E1
                    c = slice(hf * HALF, hf * HALF + HALF)
                    pool.wait_ge(s("ff1_cmb"), 2 + U + 1)
                    pool.wait_ge(s("ff1_pad"), 2 + U)
                    pool.tensor_tensor(cur[:, c], cur[:, c], yw[:, u % 2, :], ALU.add).then_inc(s("ff1_pad"), 1)

            with pool.Fori(0, R1) as r:
                round_(r)

        @block.scalar
        def _(act):
            for L in ("at0", "xa1"):
                act.sem_inc(s(L + "_qsev"), 1)
                act.sem_inc(s(L + "_ksev"), 1)
                act.sem_inc(s(L + "_exp"), 2)
                act.sem_inc(s(L + "_oT"), 1)
            act.sem_inc(s("ff1_gel"), 4)
            act.sem_inc(s("ff1_ctev"), 1)
            act.sem_inc(s("ff1_cwb"), 1)
            for name, dst, src in (("ctx", ctxT[:, :], "ctxT"), ("ctx", wctx[:, :, :], "wctx"),
                                   ("ident", ident[:, :], "ident")):
                act.dma_start(dst, w[src]).then_inc(s("ld_" + name), 16)

            def evacuate_xnT(L):
                for hf in range(2):
                    act.wait_ge(s("ln_xT"), ln(L, 2) + hf + 1)
                    act.activation(xnT[:, hf * HALF:hf * HALF + HALF], ps[:, 6 + hf, :], ACT.Copy
                                   ).then_inc(s("ln_xnT"), 1)

            def context(tiles):
                for n in tiles:
                    b, jt = n // TPB, n % TPB
                    act.wait_ge(s("ctx_pe"), n + 1)
                    act.activation(ek[:, jt, b, :], ps[:, 4 + n % 2, 0:D], ACT.Copy)
                    act.activation(ekv[:, jt, b, :], ps[:, 4 + n % 2, D:2 * D], ACT.Copy)
                    act.activation(v1_tok[:, n, :], ps[:, 4 + n % 2, 2 * D:3 * D], ACT.Copy).then_inc(s("ctx_ev"), 1)

            def rotated(hf):
                for n, a in enumerate((1, 0)):
                    act.wait_ge(s(("at0_sum", "at0_sum1")[hf]), n + 1)
                    act.activation(qhi[:, a, hf * HALF:hf * HALF + HALF], rot1[hf][:, a, :], ACT.Copy
                                   ).then_inc(s("at0_hi"), 1)

            context(range(NT // 2))
            evacuate_xnT("at0")
            for hf in range(2):
                act.wait_ge(s("at0_v"), hf + 1)
                act.activation(v_tok[:, 4 * hf:4 * hf + 4, :], ps[:, 6 + hf, :].rearrange("p (n d) -> p n d", d=D),
                               ACT.Copy).then_inc(s("at0_vev"), 1)
            rotated(0)
            context(range(NT // 2, NT))

            def before_at0_scores():
                rotated(1)
                act.wait_ge(s("ctx_kd"), TPB)
                act.activation(ek[:, :, :, :], ek[:, :, :, :], ACT.Exp).then_inc(s("ctx_ek"), 1)
                act.wait_ge(s("ctx_kd"), TPB + 1)
                act.activation(expbT[:, :, :], expbT[:, :, :], ACT.Exp).then_inc(s("ctx_ek"), 1)

            def attention(L, causal):
                def stacked_keys(b, gg):
                    act.wait_ge(s(L + "_kstk"), 2 * b + gg + 1)
                    for g in (2 * gg, 2 * gg + 1):
                        wait(act, s(L + "_km%d" % g), 16 * HPG * b)
                    act.activation(ks[:, 2 * gg:2 * gg + 2, :], ps[:, 7, :].rearrange("p (g t) -> p g t", g=2),
                                   ACT.Identity, bias=one_row[:, :]).then_inc(s(L + "_ksev"), 1)

                def stacked_queries(b, gg):
                    act.wait_ge(s(L + "_qstk"), 2 * b + gg + 1)
                    act.activation(qs[:, 2 * gg:2 * gg + 2, :], ps[:, 6, :].rearrange("p (g t) -> p g t", g=2),
                                   ACT.Copy).then_inc(s(L + "_qsev"), 1)

                def step(k, b, follow):
                    if 7 <= k < H + 7:
                        h = k - 7
                        if there(b):
                            act.wait_ge(s(L + "_s"), H + H * b + h + 1)
                            if h % HPG == 0:
                                act.wait_ge(s(L + "_pv"), G + G * b + h // HPG - 1)
                            c = slice(P if causal else 0, TPB * T)
                            act.activation(prob[:, h % 8, c], ps[:, 2 + h % 2, c], ACT.Exp, scale=DH ** -0.5
                                           ).then_inc(s(L + "_exp"), 1)
                    if k == 7 and there(b):
                        stacked_queries(b, 1)
                    if k == 15 and follow:
                        stacked_queries(b + 1, 0)
                    if k in (8, 15) and follow:
                        stacked_keys(b + 1, int(k == 15))
                    if k in (17, 25) and there(b):
                        gg = k // 8 - 2
                        act.wait_ge(s(L + "_pv"), G + G * b + 2 * gg + 2)
                        act.activation(oT[:, 2 * gg:2 * gg + 2, :], ps[:, 4, :].rearrange("p (g t) -> p g t", g=2),
                                       ACT.Copy).then_inc(s(L + "_oT"), 1)
                    if causal and k == 29 and there(b):
                        act.wait_ge(s(L + "_onT"), b + 1)
                        act.activation(oNT[:, :, :], ps[:, 7, 0:TPB * P].rearrange("p (t n) -> p t n", t=TPB),
                                       ACT.Copy).then_inc(s(L + "_onTev"), 1)

                pipelined(act, step, None if causal else before_at0_scores)

            attention("at0", False)
            if stop == 0:
                return
            for hf in range(2):
                act.wait_ge(s("ctx_k1"), hf + 1)
                act.activation(k1hi[:, hf * HALF:hf * HALF + HALF], ps[:, hf, :], ACT.Copy).then_inc(s("ctx_hi"), 1)
            act.wait_ge(s("ctx_vm"), 1)
            act.activation(vmean[:, :, :], ps[:, 2, :].rearrange("p (b d) -> p b d", b=B), ACT.Copy
                           ).then_inc(s("ctx_vme"), 1)
            evacuate_xnT("xa0")
            for hf in range(2):
                act.wait_ge(s("xa0_q"), hf + 1)
                act.activation(eq[:, hf * HALF:hf * HALF + HALF], ps[:, 0, :], ACT.Exp, scale=-1.0
                               ).then_inc(s("xa0_eq"), 1)
            for k in range(2):
                act.wait_ge(s("we_pe"), 4 * (k + 1))
                act.activation(we0[:, 4 * k:4 * k + 4, :], ps[:, 4 + k, :].rearrange("p (e d) -> p e d", d=D),
                               ACT.Copy).then_inc(s("we_ev"), 1)
            if stop == 1:
                return
            evacuate_xnT("ff0")
            act.wait_ge(s("ld_w1"), 32)
            for e in range(E1):
                act.activation(w1hi[:, e, :], w1f[:, e, :], ACT.Copy)
                act.activation(w2hi[:, e, :, :], w2f[:, e, :, :], ACT.Copy).then_inc(s("w1_hi"), 1)
            act.wait_ge(s("ff0_dif"), 1)
            act.activation(dif[:, :], dif[:, :], ACT.Tanh).then_inc(s("ff0_th"), 1)
            act.wait_ge(s("ff0_cw"), 1)
            for n in range(NT):
                act.wait_ge(s("ff0_y"), n + 1)
                if n >= 2:
                    act.wait_ge(s("ff0_red"), n - 1)
                for e in range(E0 // 2):
                    last = act.activation(prod[:, n % 2, e, :], ps[:, 2 * (n % 2), e * D:e * D + D], ACT.Copy,
                                          scale=cw[:, n * E0 + e:n * E0 + e + 1])
                last.then_inc(s("ff0_pa"), 1)
            if stop == 2:
                return
            evacuate_xnT("at1")

            def exponentials(b):
                act.wait_ge(s("at1_sub"), b + 1)
                act.activation(qkv[:, b % 2, :, 0:2 * D], qkv[:, b % 2, :, 0:2 * D], ACT.Exp).then_inc(s("at1_ex"), 1)

            def queries(b):
                act.wait_ge(s("at1_qT"), b + 1)
                if b >= 2:
                    act.wait_ge(s("at1_out"), TPB * (b - 1))
                act.activation(qT[:, b % 2, 0, :], ps[:, 6, 0:T], ACT.Copy)
                act.activation(qT[:, b % 2, 1, :], ps[:, 6, 0:T], ACT.Copy, scale=-1.0, bias=1.0).then_inc(s("at1_qTe"), 1)

            def result(b):
                act.wait_ge(s("at1_aT"), b + 1)
                act.activation(attT.rearrange("p (l b) -> p b l", b=B)[:, b, :], ps[:, 7, 0:T], ACT.Copy
                               ).then_inc(s("at1_aTe"), 1)

            exponentials(0)
            exponentials(1)
            queries(0)
            for b in range(B):
                if b + 2 < B:
                    exponentials(b + 2)
                if b + 1 < B:
                    queries(b + 1)
                result(b)
            if stop == 3:
                return
            evacuate_xnT("xa1")
            for hf in range(2):
                act.wait_ge(s("xa1_q"), hf + 1)
                act.activation(qhi[:, 0, hf * HALF:hf * HALF + HALF], ps[:, hf, :], ACT.Copy).then_inc(s("xa1_hi"), 1)
            attention("xa1", True)
            if stop == 4:
                return
            evacuate_xnT("ff1")

            def spread_weights(U, u):
                act.wait_ge(s("ff1_bcd"), U + 1)
                act.activation(cwb[:, u % 8, :], ps[:, 6, :], ACT.Copy).then_inc(s("ff1_cwb"), 1)

            def gelus(U, u):
                for c in range(FC):
                    n = FC * U + c
                    act.wait_ge(s("ff1_up"), n + 1)
                    act.wait_ge(s("ff1_glo"), n + 1)
                    act.activation(gel[:, c, :], ps[:, c, :], ACT.Gelu_apprx_tanh,
                                   bias=b1[:, u % E1, c:c + 1]).then_inc(s("ff1_gel"), 1)

            def gate_tanh(Hf):
                act.wait_ge(s("ff1_dif"), Hf + 1)
                act.activation(dif[:, 0:4 * E1], dif[:, 0:4 * E1], ACT.Tanh).then_inc(s("ff1_th"), 1)

            def gate_rows(Hf, hf):
                act.wait_ge(s("ff1_ct"), Hf + 1)
                act.activation(cwT[:, hf, :], ps[0:2 * E1, 7, :], ACT.Copy).then_inc(s("ff1_ctev"), 1)

            def round_(r, last):
                U0, H0 = 2 * E1 * r, 2 * r
                for u in range(2 * E1):
                    if u == 3:
                        gate_rows(H0 + 1, 1)
                    if u == 7 and not last:
                        gate_rows(H0 + 2, 0)
                    if not (last and u == 7):
                        spread_weights(U0 + u + 1, u + 1)
                        gelus(U0 + u + 1, u + 1)
                    if u == 0:
                        gate_tanh(H0 + 1)
                    if u == 4 and not last:
                        gate_tanh(H0 + 2)

            gate_tanh(0)
            gate_rows(0, 0)
            spread_weights(0, 0)
            gelus(0, 0)
            with act.Fori(0, R1 - 1) as r:
                round_(r, False)
            round_(R1 - 1, True)

        @block.vector
        def _(dve):
            own = OwnOrder(dve, s("dve_own"))
            v = nc.vector
            for L in ("at0", "xa1"):
                dve.sem_inc(s(L + "_red"), 2)
                dve.sem_inc(s(L + "_mrg"), 1)
                dve.sem_inc(s(L + "_on"), 1)
                dve.sem_inc(s(L + "_res"), TPB)
            dve.sem_inc(s("ff1_glo"), 4)
            dve.sem_inc(s("ff1_cmb"), 2)

            def layernorm(L, meanwhile=None):
                own.wait()
                for n in range(NT):
                    own.mark(v.bn_stats(stats[:, n, :], x[:, n, :]))
                own.wait()
                for n in range(NT):
                    v.bn_aggr(mv[:, n, :], stats[:, n, :]).then_inc(s("ln_mv"), 1)
                if meanwhile:
                    meanwhile()
                dve.wait_ge(s("ln_rstd"), ln(L, 1) + 1)
                for n in range(NT):
                    v.tensor_scalar(xn[:, n, :], x[:, n, :], mv[:, n, 0:1], rstd[:, n:n + 1], ALU.subtract, ALU.mult
                                    ).then_inc(s("ln_xn"), 1)

            dve.wait_ge(s("ld_x"), 16)
            layernorm("at0")
            dve.wait_ge(s("ld_sel"), 32)
            own.mark(v.tensor_copy(selr[:, :, :, :, :], sel))

            dve.wait_ge(s("ld_rope"), 16)

            def rotate(hf, n, a):
                for part_, dst in enumerate((rot1[hf], rot2[hf])):
                    dve.wait_ge(s("at0_qk"), 4 * hf + 2 * n + part_ + 1)
                    v.tensor_tensor(dst[:, a, :].rearrange("p (b t) -> p b t", b=2),
                                    ps[:, 2 * a + part_, :].rearrange("p (b t) -> p b t", b=2),
                                    rope[:, part_:part_ + 1, :].broadcast_to([P, 2, T]), ALU.mult
                                    ).then_inc(s("at0_rot"), 1)

            def rotated_sum(n, a):
                dve.wait_ge(s("at0_rot"), 2 * (n + 1))
                v.tensor_tensor(rot1[0][:, a, :], rot1[0][:, a, :], rot2[0][:, a, :], ALU.add).then_inc(s("at0_sum"), 1)

            def rotated_rest(n, a):
                dve.wait_ge(s("at0_hi"), n + 1)
                v.tensor_tensor(qlo[:, a, 0:HALF], rot1[0][:, a, :], qhi[:, a, 0:HALF].bitcast(f32), ALU.subtract
                                ).then_inc(s("at0_lo"), 1)

            rotate(0, 0, 1)
            rotated_sum(0, 1)
            rotate(0, 1, 0)
            rotated_rest(0, 1)
            rotated_sum(1, 0)
            rotate(1, 0, 1)
            rotated_rest(1, 0)
            rotate(1, 1, 0)
            dve.wait_ge(s("ctx_ev"), NT)
            own.mark(v.tensor_tensor(ctx_max[:, 0, :, :], ek[:, :, 0, :], ek[:, :, 1, :], ALU.max))
            own.step(v.tensor_tensor(ctx_max[:, 1, :, :], ek[:, :, 2, :], ek[:, :, 3, :], ALU.max))
            v.tensor_tensor(ctx_max[:, 2, :, :], ctx_max[:, 0, :, :], ctx_max[:, 1, :, :], ALU.max
                            ).then_inc(s("ctx_mx"), 1)

            def attention(L, causal):
                def step(k, b, follow):
                    if not there(b):
                        return
                    if k < H:
                        dve.wait_ge(s(L + "_mx"), H * b + k + 1)
                        g, j = k // HPG, k % HPG
                        col = QUAD * j + MAXROW
                        v.tensor_reduce(nmax[:, :, g, col:col + 1],
                                        ps[:, k % 2, :].rearrange("p (t k) -> p t k", t=TPB), AX.X, ALU.max,
                                        negate=True).then_inc(s(L + "_red"), 1)
                    if k in (5, 9, 13, 17):
                        g = (k - 5) // 4
                        dve.wait_ge(s(L + "_t"), G * b + g + 1)
                        v.tensor_tensor(qs[:, g, :], ps[:, 5, 0:T], qs[:, g, :].bitcast(f32), ALU.add
                                        ).then_inc(s(L + "_mrg"), 1)
                    if k in (27, 28):
                        t = k - 27
                        dve.wait_ge(s(L + "_o"), TPB * b + t + 1)
                        o = ps[:, 7, :].rearrange("p (h c) -> p h c", c=QUAD)
                        v.reciprocal(rs[:, t, :].unsqueeze(2), o[:, :, DH:DH + 1]).then_inc(s(L + "_rs"), 1)
                        dve.wait_ge(s(L + "_rs"), TPB * b + t + 1)
                        on = v.tensor_tensor(oN[:, t, :].rearrange("p (h d) -> p h d", d=DH), o[:, :, 0:DH],
                                             rs[:, t, :].unsqueeze(2).broadcast_to([P, H, DH]), ALU.mult)
                        if causal:
                            on.then_inc(s(L + "_on1"), 1)
                            dve.wait_ge(s(L + "_on1"), TPB * b + t + 1)
                            v.tensor_tensor(odif[:, t:t + 1, :], vmean[:, ds(b, 1), :], oN[:, t:t + 1, :],
                                            ALU.subtract).then_inc(s(L + "_odif"), 1)
                            dve.wait_ge(s(L + "_odif"), TPB * b + t + 1)
                            v.scalar_tensor_tensor(oN[:, t, :], odif[:, t, :], maskf[:, ds(TPB * b + t, 1)],
                                                   oN[:, t, :], ALU.mult, ALU.add).then_inc(s(L + "_on"), 1)
                        else:
                            on.then_inc(s(L + "_on"), 1)
                            dve.wait_ge(s(L + "_on"), 1 + TPB * b + t + 1)
                            xb = x[:, ds(TPB * b + t, 1), :]
                            v.tensor_tensor(xb, xb, oN[:, t:t + 1, :], ALU.add).then_inc(s(L + "_res"), 1)
                    if causal and k == 30:
                        dve.wait_ge(s(L + "_wo"), b + 1)
                        xb = x[:, ds(TPB * b, TPB), :]
                        v.tensor_tensor(xb, xb, ps[:, 7, 0:TPB * D].rearrange("p (t d) -> p t d", t=TPB), ALU.add
                                        ).then_inc(s(L + "_res"), TPB)

                pipelined(dve, step)
                dve.wait_ge(s(L + "_res"), TPB * B + TPB)

            dve.wait_ge(s("const"), 6)
            attention("at0", False)

            def finish():
                own.wait()
                dve.sem_inc(s("final"), 2)
            if stop == 0:
                return finish()

            def k1_rest():
                for hf in range(2):
                    c = slice(hf * HALF, hf * HALF + HALF)
                    dve.wait_ge(s("ctx_hi"), hf + 1)
                    v.tensor_tensor(k1lo[:, c], ps[:, hf, :], k1hi[:, c].bitcast(f32), ALU.subtract
                                    ).then_inc(s("ctx_lo"), 1)

            layernorm("xa0", k1_rest)
            for hf in range(2):
                c = slice(hf * HALF, hf * HALF + HALF)
                dve.wait_ge(s("xa0_eq"), hf + 1)
                dve.wait_ge(s("xa0_dn"), hf + 1)
                own.step(v.scalar_tensor_tensor(den[:, c], eq[:, c], 1.0, ps[:, 1, :], ALU.add, ALU.mult))
                own.step(v.reciprocal(den[:, c], den[:, c]))
                v.tensor_tensor(yT[:, c], ps[:, 2, :], den[:, c], ALU.mult).then_inc(s("xa0_y"), 1)
                dve.wait_ge(s("xa0_o"), hf + 1)
                xb = x[:, 4 * hf:4 * hf + 4, :]
                v.tensor_tensor(xb, xb, ps[:, 3, :].rearrange("p (n d) -> p n d", d=D), ALU.add).then_inc(s("xa0_res"), 1)
            dve.wait_ge(s("xa0_res"), 2)
            if stop == 1:
                return finish()

            def gates_before(lps, bias, tie, n, E):
                m = n * E
                lv, lv3 = lg[:, 0:m], lg[:, 0:m].rearrange("p (n e) -> p n e", e=E)
                if bias is None:
                    own.step(v.tensor_copy(lv3, lps))
                else:
                    own.step(v.tensor_tensor(lv3, lps, bias, ALU.add))
                other = lv3.unsqueeze(2).broadcast_to([P, n, E, E])
                this = lv3.unsqueeze(3).broadcast_to([P, n, E, E])
                gt4 = gt[:, 0:m * E].rearrange("p (n e f) -> p n e f", e=E, f=E)
                eq4 = eqt[:, 0:m * E].rearrange("p (n e f) -> p n e f", e=E, f=E)
                own.mark(v.tensor_tensor(gt4, other, this, ALU.is_gt))
                own.step(v.tensor_tensor(eq4, other, this, ALU.is_equal))
                own.step(v.tensor_tensor(eq4, eq4, tie.unsqueeze(1).broadcast_to([P, n, E, E]), ALU.mult))
                own.step(v.tensor_tensor(gt4, gt4, eq4, ALU.add))
                own.step(v.tensor_reduce(rank[:, 0:m], gt[:, 0:m * E].rearrange("p (m f) -> p m f", f=E), AX.X, ALU.add))
                own.step(v.tensor_scalar(selh[:, 0:m], rank[:, 0:m], 2.0, 0.5, ALU.is_lt, ALU.mult))
                own.step(v.tensor_tensor(lsel[:, 0:m], selh[:, 0:m], lv, ALU.mult))
                own.step(v.tensor_reduce(half_sum[:, 0:n], lsel[:, 0:m].rearrange("p (n e) -> p n e", e=E), AX.X, ALU.add))
                return v.tensor_tensor(dif[:, 0:m].rearrange("p (n e) -> p n e", e=E), lv3,
                                       half_sum[:, 0:n].unsqueeze(2).broadcast_to([P, n, E]), ALU.subtract)

            layernorm("ff0")
            dve.wait_ge(s("ld_gate0"), 32)
            dve.wait_ge(s("ff0_lg"), 1)
            gates_before(ps[:, 4, 0:NT * E0].rearrange("p (n e) -> p n e", e=E0), None, tie0[:, :, :], NT, E0
                         ).then_inc(s("ff0_dif"), 1)
            dve.wait_ge(s("ff0_th"), 1)
            v.scalar_tensor_tensor(cw[:, :], dif[:, :], 1.0, selh[:, :], ALU.add, ALU.mult).then_inc(s("ff0_cw"), 1)
            dve.wait_ge(s("ff0_cw"), 1)
            for n in range(NT + 1):
                if n < NT:
                    dve.wait_ge(s("ff0_y"), n + 1)
                    v.tensor_tensor(prod[:, n % 2, 4:8, :], ps[:, 2 * (n % 2) + 1, :].rearrange("p (e d) -> p e d", d=D),
                                    cw[:, n * E0 + 4:n * E0 + 8].unsqueeze(2).broadcast_to([P, E0 // 2, D]), ALU.mult
                                    ).then_inc(s("ff0_pd"), 1)
                if n >= 1:
                    m = n - 1
                    dve.wait_ge(s("ff0_ps"), m + 1)
                    v.tensor_reduce(yT[:, m * D:m * D + D], prod[:, m % 2, 0:4, :].rearrange("p e d -> p d e"), AX.X, ALU.add
                                    ).then_inc(s("ff0_red"), 1)
                    dve.wait_ge(s("ff0_red"), m + 1)
                    own.mark(v.tensor_tensor(x[:, m, :], x[:, m, :], yT[:, m * D:m * D + D], ALU.add))
            if stop == 2:
                return finish()

            layernorm("at1")
            dve.wait_ge(s("ld_at1"), 7 * 16)

            def project(b):
                i = b % 2
                for t in range(TPB):
                    n = TPB * b + t
                    dve.wait_ge(s("at1_qkv"), n + 1)
                    v.tensor_tensor(qkv[:, i, t, :], ps[:, n % 2, 0:3 * D], bqkv1[:, :, :].rearrange("p a d -> p (a d)"),
                                    ALU.add).then_inc(s("at1_qe"), 1)
                dve.wait_ge(s("at1_qe"), TPB * (b + 1))
                heads = qkv[:, i, :, 0:2 * D].rearrange("p t (g d) -> p t g d", d=DH)
                own.step(v.tensor_reduce(mxq[:, i, 0:TPB, :], heads, AX.X, ALU.max))
                v.tensor_tensor(heads, heads, mxq[:, i, 0:TPB, :].unsqueeze(3).broadcast_to([P, TPB, 2 * H, DH]),
                                ALU.subtract).then_inc(s("at1_sub"), 1)

            def normalise(b):
                i = b % 2
                dve.wait_ge(s("at1_ex"), b + 1)
                heads = qkv[:, i, :, 0:2 * D].rearrange("p t (g d) -> p t g d", d=DH)
                sums = sumq[:, i, 0:TPB, :]
                own.step(v.tensor_reduce(sums, heads, AX.X, ALU.add))
                own.step(v.reciprocal(sums, sums))
                v.tensor_tensor(heads, heads, sums.unsqueeze(3).broadcast_to([P, TPB, 2 * H, DH]), ALU.mult
                                ).then_inc(s("at1_nrm"), 1)

            def blocks(b):
                dve.wait_ge(s("at1_kv"), b + 1)
                if b >= 1:
                    dve.wait_ge(s("at1_out"), TPB * b)
                for a in range(2):
                    halves = bd[:, a, :].rearrange("p (z c) -> p z c", z=2)
                    v.tensor_tensor(halves[:, :, 0:D], ps[:, 4 + a, 0:2 * D].rearrange("p (z c) -> p z c", z=2),
                                    diag[:, :].unsqueeze(1).broadcast_to([P, 2, D]), ALU.mult)
                    last = v.tensor_tensor(halves[:, :, D:D + H],
                                           ps[:, 4 + a, 2 * D:2 * D + 2].unsqueeze(2).broadcast_to([P, 2, H]),
                                           diag_h[:, :].unsqueeze(1).broadcast_to([P, 2, H]), ALU.mult)
                last.then_inc(s("at1_bd"), 1)

            def outputs(b):
                for t in range(TPB):
                    dve.wait_ge(s("at1_out"), TPB * b + t + 1)
                    if b >= 1 and t == 0:
                        dve.wait_ge(s("at1_aT"), b)
                    own.step(v.tensor_scalar(part[:, :, :], ps[:, 2:4, 0:D + H], sincos[:, t, 0:1], None, ALU.mult))
                    v.scalar_tensor_tensor(comb[:, :, :], ps[:, 2:4, D + H:2 * (D + H)], sincos[:, t, 1:2],
                                           part[:, :, :], ALU.mult, ALU.add).then_inc(s("at1_comb"), 1)
                    dve.wait_ge(s("at1_comb"), TPB * b + t + 1)
                    z = comb[:, :, D:D + H]
                    own.step(v.tensor_scalar(z, z, Z_EPS, None, ALU.max))
                    own.step(v.reciprocal(z, z))
                    own.step(v.tensor_tensor(att2[:, :, :].rearrange("p a (h d) -> p a h d", d=DH),
                                             comb[:, :, 0:D].rearrange("p a (h d) -> p a h d", d=DH),
                                             z.unsqueeze(3).broadcast_to([P, 2, H, DH]), ALU.mult))
                    v.tensor_tensor(att[:, t, :], att2[:, 0, :], att2[:, 1, :], ALU.add).then_inc(s("at1_att"), 1)

            project(0)
            project(1)
            normalise(0)
            for b in range(B):
                if b + 1 < B:
                    normalise(b + 1)
                blocks(b)
                if b + 2 < B:
                    project(b + 2)
                outputs(b)
            dve.wait_ge(s("at1_bo"), 1)
            for hf in range(2):
                dve.wait_ge(s("at1_wo"), hf + 1)
                xb = x[:, 4 * hf:4 * hf + 4, :]
                own.mark(v.tensor_tensor(xb, xb, ps[:, hf, :].rearrange("p (n d) -> p n d", d=D), ALU.add))
            if stop == 3:
                return finish()

            layernorm("xa1")
            dve.wait_ge(s("ld_xa1"), 64)
            own.mark(v.tensor_scalar(maskf[:, :], mask_i[:, :], 0, None, ALU.not_equal))
            own.wait()
            for hf in range(2):
                c = slice(hf * HALF, hf * HALF + HALF)
                dve.wait_ge(s("xa1_hi"), hf + 1)
                v.tensor_tensor(qlo[:, 0, c], ps[:, hf, :], qhi[:, 0, c].bitcast(f32), ALU.subtract
                                ).then_inc(s("xa1_lo"), 1)
            attention("xa1", True)
            if stop == 4:
                return finish()

            layernorm("ff1")
            dve.wait_ge(s("ld_ff1"), 6 * 16)
            own.step(v.tensor_copy(sel_er[:, :, :], sel_e[:, :, :]))
            cur = xnT

            def split_cur(hf):
                c = slice(hf * HALF, hf * HALF + HALF)
                own.step(v.tensor_copy(xhi[:, c], cur[:, c]))
                v.tensor_tensor(xlo[:, c], cur[:, c], xhi[:, c].bitcast(f32), ALU.subtract).then_inc(s("ff1_xs"), 1)

            def gate_a(Hf, r):
                dve.wait_ge(s("ff1_lg"), Hf + 1)
                gates_before(ps[:, 7, 0:4 * E1].rearrange("p (n e) -> p n e", e=E1),
                             bg1[:, ds(r, 1), :].broadcast_to([P, 4, E1]), tie1[:, :, :], 4, E1
                             ).then_inc(s("ff1_dif"), 1)

            def gate_b(Hf):
                m = 4 * E1
                dve.wait_ge(s("ff1_th"), Hf + 1)
                own.step(v.scalar_tensor_tensor(cw[:, 0:m], dif[:, 0:m], 1.0, selh[:, 0:m], ALU.add, ALU.mult))
                own.step(v.tensor_copy(cwr[:, 0:m], cw[:, 0:m]))
                c3, r3 = (a[:, 0:m].rearrange("p (n e) -> p n e", e=E1) for a in (cw, cwr))
                own.mark(v.tensor_copy(cwhl[:, :, 0:E1], r3.bitcast(f32)))
                v.tensor_tensor(cwhl[:, :, E1:2 * E1], c3, r3.bitcast(f32), ALU.subtract).then_inc(s("ff1_cwd"), 1)

            def split_gelus(U, u):
                for c in range(FC):
                    n = FC * U + c
                    dve.wait_ge(s("ff1_gel"), 4 + n + 1)
                    if c == 0:
                        dve.wait_ge(s("ff1_dn"), U + 1)
                    v.tensor_copy(ghi[:, u % 2, c, :], gel[:, c, :]).then_inc(s("ff1_ghi"), 1)
                    dve.wait_ge(s("ff1_ghi"), n + 1)
                    v.tensor_tensor(glo[:, u % 2, c, :], gel[:, c, :], ghi[:, u % 2, c, :].bitcast(f32), ALU.subtract
                                    ).then_inc(s("ff1_glo"), 1)

            def combine(U, u):
                dve.wait_ge(s("ff1_dn"), 2 + U + 1)
                dve.wait_ge(s("ff1_cwb"), 1 + U + 1)
                dve.wait_ge(s("ff1_pad"), U + 1)
                v.scalar_tensor_tensor(yw[:, u % 2, :], ps[:, 4 + u % 2, :], b2[:, u % E1:u % E1 + 1], cwb[:, u, :],
                                       ALU.add, ALU.mult).then_inc(s("ff1_cmb"), 1)

            def round_(r, last):
                U0, H0 = 2 * E1 * r, 2 * r
                for u in range(2 * E1):
                    if u == 1:
                        dve.wait_ge(s("ff1_pad"), U0 + 2)
                        split_cur(1)
                    if u == 5 and not last:
                        dve.wait_ge(s("ff1_pad"), U0 + 2 + E1)
                        split_cur(0)
                    if u == 1:
                        gate_b(H0 + 1)
                    if u == 5 and not last:
                        gate_b(H0 + 2)
                    if not (last and u == 7):
                        split_gelus(U0 + u + 1, u + 1)
                    combine(U0 + u, u)
                    if u == 0:
                        gate_a(H0 + 1, r)
                    if u == 4 and not last:
                        gate_a(H0 + 2, r + 1)

            dve.wait_ge(s("ln_xnT"), ln("ff1", 2) + 2)
            split_cur(0)
            gate_a(0, 0)
            gate_b(0)
            split_gelus(0, 0)
            per = 2 * 1 + 2 * (9 + 3)
            with dve.Fori(0, R1 - 1) as r:
                own.loop(r, per)
                round_(r, False)
                own.end(R1 - 1)
            round_(R1 - 1, True)
            for hf in range(2):
                dve.wait_ge(s("fin_T"), hf + 1)
                xb = x[:, 4 * hf:4 * hf + 4, :]
                v.tensor_tensor(xb, xb, ps[:, hf, :].rearrange("p (n d) -> p n d", d=D), ALU.add).then_inc(s("final"), 1)

        @block.tensor
        def _(pe):
            for L in ("at0", "xa1"):
                pe.sem_inc(s(L + "_pv"), G)
                pe.sem_inc(s(L + "_s"), H)
            pe.sem_inc(s("ff1_dn"), 2)

            def transpose_xn(L):
                for n in range(NT):
                    pe.wait_ge(s("ln_xn"), ln(L, NT) + n + 1)
                    last = pe.transpose(ps[:, 6 + n // 4, (n % 4) * P:(n % 4) * P + P], xn[:, n, :], ident[:, :])
                    if n % 4 == 3:
                        last.then_inc(s("ln_xT"), 1)

            def context(tiles):
                for n in tiles:
                    if n >= 2:
                        pe.wait_ge(s("ctx_ev"), n - 1)
                    pe.matmul(ps[:, 4 + n % 2, 0:3 * D], ctxT[:, n * P:n * P + P], wctx[:, 0:3, :], start=True, stop=True
                              ).then_inc(s("ctx_pe"), 1)

            def rotary_projections(hf):
                c = slice(hf * HALF, hf * HALF + HALF)
                for n, k in enumerate((2, 3, 0, 1)):
                    if hf:
                        pe.wait_ge(s("at0_rot"), n + 1)
                    pe.matmul(ps[:, k, :], w0[:, k, :], xnT[:, c], start=True, stop=True).then_inc(s("at0_qk"), 1)

            pe.wait_ge(s("ld_ctx"), 32)
            context(range(NT // 2))
            pe.wait_ge(s("ld_ident"), 16)
            transpose_xn("at0")
            pe.wait_ge(s("ld_w0"), 16)
            pe.wait_ge(s("ln_xnT"), ln("at0", 2) + 1)
            rotary_projections(0)
            for hf in range(2):
                pe.wait_ge(s("ln_xnT"), ln("at0", 2) + hf + 1)
                for n in range(4):
                    tile = 4 * hf + n
                    last = pe.matmul(ps[:, 6 + hf, n * D:n * D + D], xnT[:, tile * P:tile * P + P], w0[:, 4, :],
                                     start=True, stop=True)
                last.then_inc(s("at0_v"), 1)
            context(range(NT // 2, NT))
            rotary_projections(1)

            def attention(L, causal, k_hi, k_lo, before_first=None, before_loop=None):
                def stack(side, b, g, bank, hi, lo, done):
                    o = ps[:, bank, (g % 2) * T:(g % 2) * T + T]
                    pe.matmul(o, selr[:, side, g, 0, :], hi[:, ds(b * T, T)], start=True, stop=False)
                    last = pe.matmul(o, selr[:, side, g, 1, :], lo[:, ds(b * T, T)], start=False, stop=True)
                    if g % 2:
                        last.then_inc(done, 1)

                def stack_queries(b, g):
                    if g % 2 == 0:
                        pe.wait_ge(s(L + "_qsev"), 2 * b + g // 2 + 1)
                    stack(0, b, g, 6, qhi[:, 0, :], qlo[:, 0, :], s(L + "_qstk"))

                def stack_keys(b, g):
                    if g % 2 == 0:
                        pe.wait_ge(s(L + "_ksev"), 2 * b + g // 2 + 1)
                        wait(pe, s(L + "_on"), 1 + TPB * (b - 2 + g // 2))
                        if causal:
                            wait(pe, s(L + "_res"), TPB + TPB * (b - 2 + g // 2))
                    stack(1, b, g, 7, k_hi, k_lo, s(L + "_kstk"))

                def step(k, b, follow):
                    now = there(b)
                    if k < H and now:
                        h = k
                        if h % HPG == 0:
                            pe.wait_ge(s(L + "_km%d" % (h // HPG)), 16 * HPG * (b + 1))
                        if h % 8 == 0:
                            pe.wait_ge(s(L + "_qsev"), 1 + 2 * b + h // 8 + 1)
                        pe.wait_ge(s(L + "_red"), H * b + h + 1)
                        for t in range(TPB):
                            at = place(t) * T
                            last = pe.matmul(ps[:, h % 2, at:at + T], qs[:, h // HPG, t * P:t * P + P], km[:, h, :],
                                             start=True, stop=not causal)
                            if causal:
                                last = pe.matmul(ps[:, h % 2, at + t * P:at + T], identb[:, :], trib[:, 0:TPB - t, :],
                                                 start=False, stop=True)
                        last.then_inc(s(L + "_mx"), 1)
                    if k in (5, 9, 13, 17) and now:
                        g = (k - 5) // 4
                        pe.wait_ge(s(L + "_red"), 2 + H * b + HPG * g + HPG)
                        pe.wait_ge(s(L + "_mrg"), G * b + g + 1)
                        for t in range(TPB):
                            last = pe.transpose(ps[:, 5, t * P:t * P + P], nmax[:, place(t), g, :], ident[:, :])
                        last.then_inc(s(L + "_t"), 1)
                    if 7 <= k < H + 7 and now:
                        h = k - 7
                        if h % HPG == 0:
                            pe.wait_ge(s(L + "_mrg"), 1 + G * b + h // HPG + 1)
                        pe.wait_ge(s(L + "_exp"), H * b + h + 1)
                        for t in range(TPB):
                            at = place(t) * T
                            last = pe.matmul(ps[:, 2 + h % 2, at:at + T], km[:, h, t * P:t * P + P], qs[:, h // HPG, :],
                                             start=True, stop=not causal)
                            if causal:
                                last = pe.matmul(ps[:, 2 + h % 2, at + t * P:at + t * P + P], identb[:, :],
                                                 trib[:, TPB, :], start=False, stop=True)
                        last.then_inc(s(L + "_s"), 1)
                    if 12 <= k < 28 and k % HPG < TPB and now:
                        g, t = (k - 12) // HPG, k % HPG
                        if t == 0:
                            pe.wait_ge(s(L + "_vaug"), G * b + g + 1)
                            if g % 2 == 0:
                                pe.wait_ge(s(L + "_oT"), TPB * b + g // 2 + 1)
                            pe.wait_ge(s(L + "_exp"), 2 + H * b + HPG * g + HPG)
                        for j in range(HPG):
                            h = HPG * g + j
                            first = P if causal and t else 0
                            last = pe.matmul(ps[QUAD * j:QUAD * j + QUAD, 4, (g % 2) * T + first:(g % 2) * T + T],
                                             vaug[:, t, h, :], prob[:, h % 8, place(t) * T + first:place(t) * T + T],
                                             start=(t == 0), stop=(t == TPB - 1))
                        if t == TPB - 1:
                            last.then_inc(s(L + "_pv"), 1)
                    if k in (3, 4) and now:
                        stack_queries(b, k - 1)
                    if k in (9, 10) and follow:
                        stack_queries(b + 1, k - 9)
                    if k in (7, 8) and follow:
                        stack_keys(b + 1, k - 7)
                    if k == 15 and follow:
                        stack_keys(b + 1, 2)
                        stack_keys(b + 1, 3)
                    if k == 27 and now:
                        pe.wait_ge(s(L + "_oT"), 1 + 2 * b + 2)
                    if k in (27, 28) and now:
                        t = k - 27
                        pe.wait_ge(s(L + "_ksev"), 1 + 2 * b + {True: 5, False: 4, None: 2}[follow])
                        pe.wait_ge(s(L + "_on"), TPB * b + t + 1)
                        for g in range(G):
                            last = pe.transpose(ps[:, 7, g * P:g * P + P], oT[:, g, t * P:t * P + P], ident[:, :])
                        last.then_inc(s(L + "_o"), 1)
                    if causal and k == 29 and now:
                        pe.wait_ge(s(L + "_on"), 1 + TPB * b + TPB)
                        for t in range(TPB):
                            last = pe.transpose(ps[:, 7, t * P:t * P + P], oN[:, t, :], ident[:, :])
                        last.then_inc(s(L + "_onT"), 1)
                    if causal and k == 30 and now:
                        pe.wait_ge(s(L + "_onTev"), b + 1)
                        for t in range(TPB):
                            last = pe.matmul(ps[:, 7, t * D:t * D + D], oNT[:, t, :], wx1[:, 1, :],
                                             start=True, stop=True)
                        last.then_inc(s(L + "_wo"), 1)

                pipelined(pe, step, before_first, before_loop)

            pe.wait_ge(s("at0_vev"), 2)
            pe.wait_ge(s("at0_lo"), 2)
            attention("at0", False, qhi[:, 1, :], qlo[:, 1, :],
                      lambda: (pe.wait_ge(s("at0_rot"), 8), pe.wait_ge(s("ctx_ev"), NT)),
                      lambda: pe.wait_ge(s("at0_lo1"), 2))
            if stop == 0:
                return

            for hf in range(2):
                pe.matmul(ps[:, hf, :], wctx[:, 3, :], ctxT[:, hf * HALF:hf * HALF + HALF], start=True, stop=True
                          ).then_inc(s("ctx_k1"), 1)
            pe.wait_ge(s("const"), 6)
            for b in range(B):
                for k in range(TPB):
                    last = pe.matmul(ps[:, 2, b * D:b * D + D], mean_w[:, :], v1_tok[:, TPB * b + k, :],
                                     start=(k == 0), stop=(k == TPB - 1))
            last.then_inc(s("ctx_vm"), 1)

            def expert_products(experts):
                pe.wait_ge(s("ld_ff0"), 32)
                for e in experts:
                    for c in range(F0 // P):
                        last = pe.matmul(ps[:, 4 + e // 4, (e % 4) * D:(e % 4) * D + D], wi0[:, e, c, :], wo0[:, e, c, :],
                                         start=(c == 0), stop=(c == F0 // P - 1))
                    last.then_inc(s("we_pe"), 1)

            transpose_xn("xa0")
            pe.wait_ge(s("ld_xa0"), 32)
            pe.wait_ge(s("ctx_ek"), 2)
            pe.wait_ge(s("ctx_ekv"), 1)
            for hf in range(2):
                pe.wait_ge(s("ln_xnT"), ln("xa0", 2) + hf + 1)
                pe.wait_ge(s("ctx_lo"), 2)
                pe.wait_ge(s("ctx_vme"), 1)
                if hf:
                    pe.wait_ge(s("xa0_eq"), 1)
                    pe.wait_ge(s("xa0_y"), 1)
                pe.matmul(ps[:, 0, :], wx0[:, 0, :], xnT[:, hf * HALF:hf * HALF + HALF], start=True, stop=True
                          ).then_inc(s("xa0_q"), 1)
                for bank, src in ((1, ek), (2, ekv)):
                    for bl in range(2):
                        for k in range(TPB):
                            last = pe.matmul(ps[:, bank, bl * T:bl * T + T], src[:, k, 2 * hf + bl, :], expbT[:, k, :],
                                             start=(k == 0), stop=(k == TPB - 1))
                last.then_inc(s("xa0_dn"), 1)
                expert_products(range(4 * hf, 4 * hf + 4))
                pe.wait_ge(s("xa0_y"), hf + 1)
                if hf:
                    pe.wait_ge(s("xa0_res"), 1)
                for n in range(4):
                    tile = 4 * hf + n
                    last = pe.matmul(ps[:, 3, n * D:n * D + D], yT[:, tile * P:tile * P + P], wx0[:, 1, :],
                                     start=True, stop=True)
                last.then_inc(s("xa0_o"), 1)
            if stop == 1:
                return

            transpose_xn("ff0")
            pe.wait_ge(s("ld_gate0"), 32)
            pe.wait_ge(s("we_ev"), 2)
            pe.wait_ge(s("ln_xnT"), ln("ff0", 2) + 2)
            for n in range(NT):
                last = pe.matmul(ps[:, 4, n * E0:n * E0 + E0], xnT[:, n * P:n * P + P], wgate0[:, :], start=True, stop=True)
            last.then_inc(s("ff0_lg"), 1)
            for n in range(NT):
                if n >= 2:
                    pe.wait_ge(s("ff0_pa"), n - 1)
                    pe.wait_ge(s("ff0_pd"), n - 1)
                for k in range(2):
                    last = pe.matmul(ps[:, 2 * (n % 2) + k, :], xnT[:, n * P:n * P + P], we0[:, 4 * k:4 * k + 4, :],
                                     start=True, stop=True)
                last.then_inc(s("ff0_y"), 1)
            if stop == 2:
                return

            transpose_xn("at1")
            pe.wait_ge(s("ld_at1"), 7 * 16)

            def qkv_tiles(b):
                for t in range(TPB):
                    n = TPB * b + t
                    pe.wait_ge(s("ln_xnT"), ln("at1", 2) + n // 4 + 1)
                    if n >= 2:
                        pe.wait_ge(s("at1_qe"), n - 1)
                    pe.matmul(ps[:, n % 2, 0:3 * D], xnT[:, n * P:n * P + P], wqkv1[:, :, :], start=True, stop=True
                              ).then_inc(s("at1_qkv"), 1)

            def keys_values(b):
                i = b % 2
                pe.wait_ge(s("at1_nrm"), b + 1)
                if b >= 1:
                    pe.wait_ge(s("at1_qTe"), b)
                else:
                    pe.wait_ge(s("ln_xnT"), ln("at1", 2) + 2)
                for t in range(TPB):
                    last = pe.transpose(ps[:, 6, t * P:t * P + P], qkv[:, i, t, 0:D], ident[:, :])
                last.then_inc(s("at1_qT"), 1)
                pe.wait_ge(s("at1_rv"), b + 1)
                pe.wait_ge(s("at1_kc"), b + 1)
                if b >= 1:
                    pe.wait_ge(s("at1_bd"), b)
                for a in range(2):
                    for t in range(TPB):
                        keys = (qkv[:, i, t, D:2 * D], kc[:, i, t, :])[a]
                        last = pe.matmul(ps[:, 4 + a, 0:2 * D + 2], keys, rv[:, i, t, :],
                                         start=(t == 0), stop=(t == TPB - 1))
                last.then_inc(s("at1_kv"), 1)

            qkv_tiles(0)
            qkv_tiles(1)
            keys_values(0)
            for b in range(B):
                i = b % 2
                if b + 2 < B:
                    qkv_tiles(b + 2)
                pe.wait_ge(s("at1_bd"), b + 1)
                pe.wait_ge(s("at1_qTe"), b + 1)
                for t in range(TPB):
                    if TPB * b + t >= 1:
                        pe.wait_ge(s("at1_comb"), TPB * b + t)
                    for a in range(2):
                        last = pe.matmul(ps[:, 2 + a, 0:2 * (D + H)], qT[:, i, a, t * P:t * P + P], bd[:, a, :],
                                         start=True, stop=True)
                    last.then_inc(s("at1_out"), 1)
                    if t == 0 and b + 1 < B:
                        keys_values(b + 1)
                pe.wait_ge(s("at1_att"), TPB * (b + 1))
                if b >= 1:
                    pe.wait_ge(s("at1_aTe"), b)
                for t in range(TPB):
                    last = pe.transpose(ps[:, 7, t * P:t * P + P], att[:, t, :], ident[:, :])
                last.then_inc(s("at1_aT"), 1)
            pe.wait_ge(s("at1_aTe"), B)
            for hf in range(2):
                for n in range(4):
                    r = 4 * hf + n
                    last = pe.matmul(ps[:, hf, n * D:n * D + D], attT[:, r * P:r * P + P], wo1[:, :], start=True, stop=True)
                last.then_inc(s("at1_wo"), 1)
            if stop == 3:
                return

            transpose_xn("xa1")
            pe.wait_ge(s("ld_xa1"), 64)
            for hf in range(2):
                pe.wait_ge(s("ln_xnT"), ln("xa1", 2) + hf + 1)
                pe.matmul(ps[:, hf, :], wx1[:, 0, :], xnT[:, hf * HALF:hf * HALF + HALF], start=True, stop=True
                          ).then_inc(s("xa1_q"), 1)
            pe.wait_ge(s("xa1_lo"), 2)
            attention("xa1", True, k1hi[:, :], k1lo[:, :])
            if stop == 4:
                return

            transpose_xn("ff1")
            cur = xnT
            pe.wait_ge(s("ln_xnT"), ln("ff1", 2) + 2)
            pe.wait_ge(s("ld_ff1"), 6 * 16)
            pe.wait_ge(s("w1_lo"), 2 * E1)

            def logits(Hf, hf, r):
                pe.wait_ge(s("ff1_ctev"), Hf + 1)
                for n in range(4):
                    tile = 4 * hf + n
                    last = pe.matmul(ps[:, 7, n * E1:n * E1 + E1], cur[:, tile * P:tile * P + P],
                                     wg1[:, ds(r, 1), :], start=True, stop=True)
                last.then_inc(s("ff1_lg"), 1)

            def gate_rows(Hf):
                pe.wait_ge(s("ff1_cwd"), Hf + 1)
                for n in range(4):
                    last = pe.transpose(ps[0:2 * E1, 7, n * P:n * P + P], cwhl[:, n, :], ident[:, :])
                last.then_inc(s("ff1_ct"), 1)

            def up(U, u):
                u = u % (2 * E1)
                hf, e = u // E1, u % E1
                if e == 0:
                    pe.wait_ge(s("ff1_ctev"), 1 + U // E1 + 1 if isinstance(U, int) else 0) if False else None
                c = slice(hf * HALF, hf * HALF + HALF)
                pe.wait_ge(s("ff1_cwb"), U + 1)
                pe.matmul(ps[:, 6, :], sel_er[:, e, :], cwT[:, hf, :], start=True, stop=True).then_inc(s("ff1_bcd"), 1)
                for k in range(FC):
                    pe.wait_ge(s("ff1_gel"), FC * U + k + 1)
                    f = slice(k * P, k * P + P)
                    pe.matmul(ps[:, k, :], w1hi[:, e, f], xhi[:, c], start=True, stop=False)
                    pe.matmul(ps[:, k, :], w1lo[:, e, f], xhi[:, c], start=False, stop=False)
                    pe.matmul(ps[:, k, :], w1hi[:, e, f], xlo[:, c], start=False, stop=True).then_inc(s("ff1_up"), 1)

            def down(U, u):
                e = u % E1
                pe.wait_ge(s("ff1_cmb"), U + 1)
                o = ps[:, 4 + u % 2, :]
                for k in range(FC):
                    pe.wait_ge(s("ff1_glo"), 4 + FC * U + k + 1)
                    pe.matmul(o, w2hi[:, e, k, :], ghi[:, u % 2, k, :], start=(k == 0), stop=False)
                    pe.matmul(o, w2lo[:, e, k, :], ghi[:, u % 2, k, :], start=False, stop=False)
                    last = pe.matmul(o, w2hi[:, e, k, :], glo[:, u % 2, k, :], start=False, stop=(k == FC - 1))
                last.then_inc(s("ff1_dn"), 1)

            def round_(r, last):
                U0, H0 = 2 * E1 * r, 2 * r
                for u in range(2 * E1):
                    if u == 3:
                        pe.wait_ge(s("ff1_ctev"), 1 + H0 + 2)
                        pe.wait_ge(s("ff1_xs"), H0 + 2)
                    if u == 7 and not last:
                        pe.wait_ge(s("ff1_ctev"), 1 + H0 + 3)
                        pe.wait_ge(s("ff1_xs"), H0 + 3)
                    if not (last and u == 7):
                        up(U0 + u + 1, u + 1)
                    if u == 2:
                        gate_rows(H0 + 1)
                    if u == 6 and not last:
                        gate_rows(H0 + 2)
                    down(U0 + u, u)
                    if u == 0:
                        pe.wait_ge(s("ff1_pad"), U0 + 2)
                        logits(H0 + 1, 1, r)
                    if u == 4 and not last:
                        pe.wait_ge(s("ff1_pad"), U0 + 2 + E1)
                        logits(H0 + 2, 0, r + 1)

            logits(0, 0, 0)
            gate_rows(0)
            pe.wait_ge(s("ff1_ctev"), 2)
            pe.wait_ge(s("ff1_xs"), 1)
            up(0, 0)
            with pe.Fori(0, R1 - 1) as r:
                round_(r, False)
            round_(R1 - 1, True)
            pe.wait_ge(s("ff1_pad"), 2 + 2 * E1 * R1)
            for hf in range(2):
                for n in range(4):
                    tile = 4 * hf + n
                    last = pe.transpose(ps[:, hf, n * P:n * P + P], cur[:, tile * P:tile * P + P], ident[:, :])
                last.then_inc(s("fin_T"), 1)


def shape_constants():
    import numpy as np
    f = np.float32
    c = {"ident": np.eye(P, dtype=f)}
    inv_freq = (f(1.0) / f(10000.0) ** (np.arange(0, DH, 2, dtype=f) / f(DH))).astype(f)
    angle = np.outer(np.arange(T, dtype=f), inv_freq).astype(f)
    pair = (np.arange(D) % DH) // 2
    sign = np.where(np.arange(D) % 2 == 0, -1, 1).astype(f)
    c["rope"] = np.ascontiguousarray(np.stack([np.cos(angle)[:, pair].T, np.sin(angle)[:, pair].T * sign[:, None]], 1)).astype(f)
    sel = np.zeros((P, 2, G, 2, P), f)
    for g in range(G):
        for j in range(HPG):
            for d in range(DH):
                src = (HPG * g + j) * DH + d
                for side, parts in enumerate(((0, 1, 0), (0, 0, 1))):
                    for copy, part in enumerate(parts):
                        sel[src, side, g, part, QUAD * j + DH * copy + d] = 1
    c["sel"] = sel
    c["one_row"] = (np.arange(P) % QUAD == MAXROW).astype(f).reshape(P, 1)
    row, col = np.arange(P)[:, None], np.arange(P)[None, :]
    later_key, earlier_query = np.where(col > row, -1e9, 0), np.where(row > col, -1e9, 0)
    c["tri"] = np.stack([later_key, np.full((P, P), -1e9), earlier_query], 1).astype(np.dtype("bfloat16"))
    c["identb"] = np.eye(P, dtype=np.dtype("bfloat16"))
    idx = (f(np.pi / 2) * np.arange(1, T + 1, dtype=f) / f(T)).astype(f)
    c["sincos"] = np.ascontiguousarray(np.stack([np.sin(idx), np.cos(idx)], 1).reshape(TPB, P, 2).transpose(1, 0, 2)).astype(f)
    head = np.arange(D) // DH
    c["diag"] = (head[:, None] == head[None, :]).astype(f)
    c["diag_h"] = (head[:, None] == np.arange(H)[None, :]).astype(f)
    for n, E in (("tie0", E0), ("tie1", E1)):
        c[n] = (np.arange(E)[None, :] < np.arange(E)[:, None]).astype(f)
    c["sel_e"] = np.ascontiguousarray(np.broadcast_to(
        (np.arange(2 * E1)[:, None] % E1 == np.arange(E1)[None, :])[:, :, None], (2 * E1, E1, P))).astype(f)
    return c


def laid_out(a):
    import numpy as np
    T_ = lambda m: np.ascontiguousarray(np.asarray(m).T)
    swap = np.arange(D) ^ 1
    w = {
        "x": np.asarray(a["x"]).reshape(B * T, D),
        "ctxT": T_(np.asarray(a["ctx_1024"]).reshape(B * T, D)),
        "w0": np.stack([T_(a["L0_attn_wq"]), T_(np.asarray(a["L0_attn_wq"])[swap]), T_(a["L0_attn_wk"]),
                        T_(np.asarray(a["L0_attn_wk"])[swap]), T_(a["L0_attn_wv"])], 1),
        "wctx": np.stack([T_(a["L0_xattn_Wk"]), T_(a["L0_xattn_Wv"]), np.asarray(a["L1_xattn_WV"]),
                          np.asarray(a["L1_xattn_WK"])], 1),
        "wx0": np.stack([T_(a["L0_xattn_Wq"]), T_(a["L0_xattn_Wo"])], 1),
        "wbiasT": T_(a["L0_xattn_W_bias"]).reshape(TPB, P, T).transpose(1, 0, 2),
        "wgate0": T_(a["L0_ffn_w_gate"]),
        "wi0": np.asarray(a["L0_ffn_w_in"]).reshape(E0, F0 // P, P, D).transpose(2, 0, 1, 3),
        "wo0": np.asarray(a["L0_ffn_w_out"]).transpose(0, 2, 1).reshape(E0, F0 // P, P, D).transpose(2, 0, 1, 3),
        "wqkv1": np.stack([np.asarray(a["L1_attn_W" + n]) for n in "qkv"], 1),
        "bqkv1": np.stack([np.asarray(a["L1_attn_b" + n]) for n in "qkv"], 0),
        "wo1": np.asarray(a["L1_attn_Wo"]),
        "bo1": np.asarray(a["L1_attn_bo"]),
        "wx1": np.stack([np.asarray(a["L1_xattn_WQ"]), np.asarray(a["L1_xattn_WO"])], 1),
        "mask": np.asarray(a["mask_BxS2_ik0"]).reshape(NT, P).T,
        "wg1": np.asarray(a["L1_ffn_Wg"]).transpose(1, 0, 2),
        "bg1": np.asarray(a["L1_ffn_bg"]),
        "w1": np.asarray(a["L1_ffn_W1"]).transpose(1, 0, 2),
        "b1": np.asarray(a["L1_ffn_b1"]).reshape(E1, FC, P).transpose(2, 0, 1),
        "w2": np.asarray(a["L1_ffn_W2"]).reshape(E1, FC, P, D).transpose(2, 0, 1, 3),
        "b2": T_(a["L1_ffn_b2"]),
    }
    w.update(shape_constants())
    return {"in_" + n: np.ascontiguousarray(m) for n, m in w.items()}


def kernel(**inputs):
    import numpy as np
    import concourse.bacc as bacc
    from concourse.bass_utils import run_bass_kernel_spmd

    arrays = laid_out(inputs)
    nc = bacc.Bacc("TRN2", target_bir_lowering=False, num_devices=1)
    w = {n[3:]: nc.dram_tensor(n, m.shape, mybir.dt.from_np(m.dtype), kind="ExternalInput").ap() for n, m in arrays.items()}
    out = nc.dram_tensor("out", (B * T, D), mybir.dt.float32, kind="ExternalOutput").ap()
    decoder_kernel(nc, w, out)
    r = run_bass_kernel_spmd(nc, [arrays], core_ids=[0])
    return np.asarray(r.results[0]["out"]).reshape(B, T, D)
```

```python
import concourse.bass as bass
from concourse import mybir
from contextlib import ExitStack

B, T, D = 4, 256, 128
H, DH = 16, 8
P = 128
NT = B * T // P
TPB = T // P
HALF = B * T // 2
HPG = 4
G = H // HPG
QUAD = P // HPG
MAXROW = 3 * DH
E0, F0 = 8, 512
E1, F1, R1 = 4, 512, 4
FC = F1 // P
LN_EPS, Z_EPS = 1e-5, 1e-6


class OwnOrder:

    def __init__(self, engine, semaphore):
        self.engine, self.semaphore, self.base, self.n = engine, semaphore, 0, 0

    def mark(self, instruction):
        instruction.then_inc(self.semaphore, 1)
        self.n += 1

    def wait(self):
        self.engine.wait_ge(self.semaphore, self.base + self.n)

    def step(self, instruction):
        self.mark(instruction)
        self.wait()

    def loop(self, i, per):
        self.outer, self.per = self.base + self.n, per
        self.base, self.n = i * per + self.outer, 0

    def end(self, count):
        assert self.n == self.per, self.n
        self.base, self.n = self.outer + count * self.per, 0


def decoder_kernel(nc, w, out, stop=99):
    f32, f32r, bf16 = mybir.dt.float32, mybir.dt.float32r, mybir.dt.bfloat16
    ALU, ACT, AX = mybir.AluOpType, mybir.ActivationFunctionType, mybir.AxisListType
    ds = bass.ds
    ctx = ExitStack()
    with ctx:
        def sb(name, shape, dt=f32):
            return ctx.enter_context(nc.sbuf_tensor(name, shape, dt))

        def sem(name):
            return ctx.enter_context(nc.semaphore(name))

        x = sb("x", [P, NT, D])
        ident = sb("ident", [P, P])
        identb = sb("identb", [P, P], bf16)
        trib = sb("trib", [P, TPB + 1, P], bf16)
        one_row = sb("one_row", [P, 1])
        sincos = sb("sincos", [P, TPB, 2])
        diag = sb("diag", [P, P])
        diag_h = sb("diag_h", [P, H])
        tie0 = sb("tie0", [P, E0, E0])
        tie1 = sb("tie1", [P, E1, E1])
        wgate0 = sb("wgate0", [P, E0])
        wi0 = sb("wi0", [P, E0, F0 // P, D])
        wo0 = sb("wo0", [P, E0, F0 // P, D])
        wqkv1 = sb("wqkv1", [P, 3, D])
        bqkv1 = sb("bqkv1", [P, 3, D])
        wo1 = sb("wo1", [P, D])
        bo1 = sb("bo1", [P, D])
        wx1 = sb("wx1", [P, 2, D])
        mask_i = sb("mask_i", [P, NT], mybir.dt.int32)
        wg1 = sb("wg1", [P, R1, E1])
        bg1 = sb("bg1", [P, R1, E1])
        b1 = sb("b1", [P, E1, FC])
        b2 = sb("b2", [P, E1])

        selr = sb("selr", [P, 2, G, 2, P], f32r)
        mean_w = sb("mean_w", [P, P])
        halfs = sb("halfs", [P, NT])
        v1_tok = sb("v1_tok", [P, NT, D])
        k1hi = sb("k1hi", [P, B * T], f32r)
        k1lo = sb("k1lo", [P, B * T], f32r)
        maskf = sb("maskf", [P, NT])

        early = ExitStack()

        def sb_early(name, shape, dt=f32):
            return early.enter_context(nc.sbuf_tensor(name, shape, dt))

        rope = sb_early("rope", [P, 2, T])
        w0 = sb_early("w0", [P, 5, D])
        ctxT = sb_early("ctxT", [P, B * T])
        wctx = sb_early("wctx", [P, 4, D])
        wx0 = sb_early("wx0", [P, 2, D])
        wbiasT = sb_early("wbiasT", [P, TPB, T])
        expbT = sb_early("expbT", [P, TPB, T])
        ek = sb_early("ek", [P, TPB, B, D])
        ekv = sb_early("ekv", [P, TPB, B, D])
        v_tok = sb_early("v_tok", [P, NT, D])
        early.close()
        w1hi = sb("w1hi", [P, E1, F1], f32r)
        w1lo = sb("w1lo", [P, E1, F1], f32r)
        w2hi = sb("w2hi", [P, E1, FC, D], f32r)
        w2lo = sb("w2lo", [P, E1, FC, D], f32r)
        cwT = sb("cwT", [2 * E1, 2, HALF], f32r)
        sel_er = sb("sel_er", [2 * E1, E1, P], f32r)

        stats = sb("stats", [P, NT, 6])
        mv = sb("mv", [P, NT, 2])
        rstd = sb("rstd", [P, NT])
        vare = sb("vare", [P, NT])
        xn = sb("xn", [P, NT, D])
        xnT = sb("xnT", [P, B * T])
        big = sb("big", [P, 8192])
        bigr = sb("bigr", [P, 8192], f32r)
        ps = ctx.enter_context(nc.psum_tensor("ps", [P, 8, 512], f32))

        w1f = wo0[:, 0:E1, :, :].rearrange("p e c d -> p e (c d)")
        w2f = wi0[:, 0:E1, :, :]
        sel = big[:, 4096:6144].rearrange("p (a g i m) -> p a g i m", a=2, g=G, i=2)
        rot1 = (big[:, 0:1024].rearrange("p (a n) -> p a n", a=2),
                xn[:, :, :].rearrange("p (a t) d -> p a (t d)", a=2))
        rot2 = tuple(big[:, n:n + 1024].rearrange("p (a n) -> p a n", a=2) for n in (1024, 7168))
        ctx_max = big[:, 6144:6912].rearrange("p (m k d) -> p m k d", m=3, k=TPB)
        qhi = bigr[:, 0:2048].rearrange("p (a n) -> p a n", a=2)
        qlo = bigr[:, 2048:4096].rearrange("p (a n) -> p a n", a=2)
        qs = sb("qs", [P, G, T], f32r)
        ks = sb("ks", [P, G, T], f32r)
        km = bigr[:, 4096:8192].rearrange("p (h t) -> p h t", h=H)
        vaug = sb("vaug", [P, TPB, H, QUAD])
        nmax = sb("nmax", [P, TPB, G, P])
        prob = big[:, 0:4096].rearrange("p (s n) -> p s n", s=8)
        oT = big[:, 6144:7168].rearrange("p (g t) -> p g t", g=G)
        gt, eqt = (xn[:, n:n + 4, :].rearrange("p n d -> p (n d)") for n in (0, 4))
        we0 = big[:, 7168:8192].rearrange("p (e d) -> p e d", e=E0)
        ratio = big[:, 4096:5120]
        gate_q = big[:, 0:1024]
        weights = big[:, 5120:6144]
        yT = big[:, 2048:3072]
        prod = big[:, 0:2048].rearrange("p (i e d) -> p i e d", i=2, e=E0)
        qkv = big[:, 0:1536].rearrange("p (i t c) -> p i t c", i=2, t=TPB)
        kc = big[:, 1536:2048].rearrange("p (i t c) -> p i t c", i=2, t=TPB)
        rv = big[:, 2048:3080].rearrange("p (i t c) -> p i t c", i=2, t=TPB)
        qT = big[:, 3080:4104].rearrange("p (i a c) -> p i a c", i=2, a=2)
        bd = big[:, 4104:4680].rearrange("p (a c) -> p a c", a=2)
        part = big[:, 4680:4968].rearrange("p (a c) -> p a c", a=2)
        comb = big[:, 4968:5256].rearrange("p (a c) -> p a c", a=2)
        att2 = big[:, 5256:5512].rearrange("p (a c) -> p a c", a=2)
        att = big[:, 5512:5768].rearrange("p (t c) -> p t c", t=TPB)
        attT = big[:, 5768:6792]
        gel = big[:, 0:2048].rearrange("p (s n) -> p s n", s=4)
        cwb = big[:, 2048:6144].rearrange("p (u n) -> p u n", u=8)
        yw = big[:, 6144:7168].rearrange("p (u n) -> p u n", u=2)
        ghi = bigr[:, 0:4096].rearrange("p (u c n) -> p u c n", u=2, c=FC)
        glo = bigr[:, 4096:8192].rearrange("p (u c n) -> p u c n", u=2, c=FC)
        xhi, xlo = k1hi, k1lo
        oN = sb("oN", [P, TPB, D])
        odif = sb("odif", [P, TPB, D])
        vmean = sb("vmean", [P, B, D])
        mxq = sb("mxq", [P, 2, 2 * TPB, 32])
        sumq = sb("sumq", [P, 2, 2 * TPB, 32])
        lg = sb("lg", [P, NT * E0])
        rank = sb("rank", [P, NT * E0])
        selh = sb("selh", [P, NT * E0])
        lsel = sb("lsel", [P, NT * E0])
        half_sum = sb("half_sum", [P, NT])
        dif = sb("dif", [P, NT * E0])
        cw = sb("cw", [P, NT * E0])
        cwr = sb("cwr", [P, NT * E0], f32r)
        cwhl = sb("cwhl", [P, 4, 2 * E1])
        sel_e = sb("sel_e", [2 * E1, E1, P])
        oNT = sb("oNT", [P, TPB, P])
        rs = sb("rs", [P, TPB, H])

        S = {}

        def s(name):
            if name not in S:
                S[name] = sem(name)
            return S[name]

        LAYERS = ("at0", "xa0", "ff0", "at1", "xa1", "ff1")

        def ln(L, each):
            return each * LAYERS.index(L)

        block = ctx.enter_context(nc.Block())

        def wait(engine, semaphore, value):
            if not isinstance(value, int) or value > 0:
                engine.wait_ge(semaphore, value)

        def there(b):
            return not isinstance(b, int) or b >= 0

        AFT_STEP = H + 2

        def place(t):
            return TPB - 1 - t

        def pipelined(engine, step, before_first=None, before_loop=None, beside={}):
            def batch(b, first, follow):
                for k in range(H):
                    if not first:
                        step(H + k, b - 1, follow)
                    step(k, b, follow)

            for k in range(H // 2 - 1, H):
                step(k, -1, True)
            if before_first:
                before_first()
            batch(0, True, True)
            if before_loop:
                before_loop()
            with engine.Fori(1, B - 1) as b:
                batch(b, False, True)
            batch(B - 1, False, False)
            for k in range(H, 2 * H):
                step(k, B - 1, None)
                if k in beside:
                    beside[k]()

        @block.sync
        def _(sp):
            def load(name, dst, src):
                sp.dma_start(dst, src).then_inc(s("ld_" + name), 16)
            load("x", x[:, :, :], w["x"].rearrange("(n p) d -> p n d", p=P))
            load("w0", w0[:, :, :], w["w0"])
            load("rope", rope[:, :, :], w["rope"])
            load("sel", sel, w["sel"])
            load("sel", one_row[:, :], w["one_row"])
            load("xa0", wx0[:, :, :], w["wx0"])
            load("xa0", wbiasT[:, :, :], w["wbiasT"])
            load("gate0", wgate0[:, :], w["wgate0"])
            load("gate0", tie0[:, :, :], w["tie0"].partition_broadcast(P))
            load("at1", wqkv1[:, :, :], w["wqkv1"])
            load("at1", bqkv1[:, :, :], w["bqkv1"].partition_broadcast(P))
            load("at1", wo1[:, :], w["wo1"])
            load("at1", bo1[:, :], w["bo1"].partition_broadcast(P))
            load("at1", sincos[:, :, :], w["sincos"])
            load("at1", diag[:, :], w["diag"])
            load("at1", diag_h[:, :], w["diag_h"])
            load("xa1", wx1[:, :, :], w["wx1"])
            load("xa1", trib[:, :, :], w["tri"])
            load("xa1", identb[:, :], w["identb"])
            load("xa1", mask_i[:, :], w["mask"])
            load("ff1", wg1[:, :, :], w["wg1"])
            load("ff1", bg1[:, :, :], w["bg1"].partition_broadcast(P))
            load("ff1", b1[:, :, :], w["b1"])
            load("ff1", b2[:, :], w["b2"])
            load("ff1", tie1[:, :, :], w["tie1"].partition_broadcast(P))
            load("ff1", sel_e[:, :, :], w["sel_e"])
            load("ff0", wi0[:, :, :, :], w["wi0"])
            load("ff0", wo0[:, :, :, :], w["wo0"])

            def attention_keys(L):
                def keys(b, g):
                    if g % 2 == 0:
                        sp.wait_ge(s(L + "_ksev"), 1 + 2 * b + g // 2 + 1)
                        sp.sem_inc(s("keys_stacked"), 1)
                    sp.wait_ge(s(L + "_s"), H * b + HPG * g + HPG)
                    for j in range(HPG):
                        rows = slice(QUAD * j, QUAD * j + QUAD)
                        sp.dma_start(km[rows, HPG * g + j, :].bitcast(f32), ks[rows, g, :].bitcast(f32)
                                     ).then_inc(s(L + "_km%d" % g), 16)

                for g in range(G):
                    keys(0, g)
                with sp.Fori(1, B) as b:
                    for g in range(G):
                        keys(b, g)

            attention_keys("at0")
            sp.wait_ge(s("we_pe"), E0)
            load("w1", w1f, w["w1"])
            load("w1", w2f, w["w2"])
            if stop >= 4:
                attention_keys("xa1")
            sp.wait_ge(s("final"), 2)
            sp.dma_start(out.rearrange("(n p) d -> p n d", p=P), x[:, :, :]).then_inc(s("stored"), 16)
            sp.wait_ge(s("stored"), 16)
            if stop < 5:
                for n, c in (("ff0", 2), ("gate0", 2), ("at1", 7), ("xa1", 4), ("ff1", 6), ("w1", 2), ("xa0", 2), ("ctx", 2)):
                    sp.wait_ge(s("ld_" + n), 16 * c)

        @block.gpsimd
        def _(pool):
            own = OwnOrder(pool, s("pool_own"))
            pool.sem_inc(s("ff1_pad"), 2)
            pool.memset(halfs[:, :], -0.5).then_inc(s("const"), 1)
            pool.memset(mean_w[:, :], 1.0 / T).then_inc(s("const"), 1)
            pool.memset(nmax[:, :, :, :], 0.0).then_inc(s("const"), 1)
            pool.memset(vaug[:, :, :, :], 0.0).then_inc(s("const"), 1)
            pool.memset(km[:, :, :].bitcast(f32), 0.0).then_inc(s("const"), 1)
            pool.wait_ge(s("const"), 5)
            pool.memset(vaug[:, :, :, DH:DH + 1], 1.0).then_inc(s("const"), 1)
            pool.wait_ge(s("const"), 6)

            def rstds(L, hf):
                n = slice(4 * hf, 4 * hf + 4)
                pool.wait_ge(s("ln_mv"), ln(L, NT) + 4 * hf + 4)
                own.step(pool.tensor_scalar(vare[:, n], mv[:, n, 1], LN_EPS, None, ALU.add))
                pool.tensor_tensor(rstd[:, n], vare[:, n], halfs[:, n], ALU.pow).then_inc(s("ln_rstd"), 1)

            def attention_values(L, vals):
                with pool.Fori(0, B) as b:
                    for g in range(G):
                        pool.wait_ge(s(L + "_pv"), G * b + g + 1)
                        pool.tensor_copy(vaug[:, :, HPG * g:HPG * g + HPG, 0:DH],
                                         vals[:, ds(TPB * b, TPB), HPG * DH * g:HPG * DH * (g + 1)]
                                         .rearrange("p k (h d) -> p k h d", d=DH)).then_inc(s(L + "_vaug"), 1)

            for hf in range(2):
                rstds("at0", hf)
            for n, a in enumerate((1, 0)):
                pool.wait_ge(s("at0_rot"), 4 + 2 * (n + 1))
                pool.tensor_tensor(rot1[1][:, a, :], rot1[1][:, a, :], rot2[1][:, a, :], ALU.add).then_inc(s("at0_sum1"), 1)
            pool.wait_ge(s("ctx_mx"), 1)
            for k in range(TPB):
                pool.tensor_tensor(ek[:, k, :, :], ek[:, k, :, :],
                                   ctx_max[:, 2, k:k + 1, :].broadcast_to([P, B, D]), ALU.subtract).then_inc(s("ctx_kd"), 1)
            pool.wait_ge(s("ld_xa0"), 32)
            pool.tensor_tensor(expbT[:, :, :], wbiasT[:, :, :], wbiasT[:, :, :], ALU.subtract).then_inc(s("ctx_kd"), 1)
            for n, a in enumerate((1, 0)):
                pool.wait_ge(s("at0_hi"), 2 + n + 1)
                pool.tensor_tensor(qlo[:, a, HALF:2 * HALF], rot1[1][:, a, :], qhi[:, a, HALF:2 * HALF].bitcast(f32),
                                   ALU.subtract).then_inc(s("at0_lo1"), 1)
            pool.wait_ge(s("at0_vev"), 2)
            attention_values("at0", v_tok)
            pool.wait_ge(s("ctx_ek"), 1)
            pool.tensor_tensor(ekv[:, :, :, :], ek[:, :, :, :], ekv[:, :, :, :], ALU.mult).then_inc(s("ctx_ekv"), 1)
            if stop == 0:
                return

            def ratios(hf):
                c = slice(hf * HALF, hf * HALF + HALF)
                pool.wait_ge(s("xa0_rec"), hf + 1)
                pool.wait_ge(s("xa0_dne"), 2 * hf + 2)
                pool.tensor_tensor(ratio[:, c], ratio[:, c], weights[:, c], ALU.mult).then_inc(s("xa0_rat"), 1)

            for hf in range(2):
                rstds("xa0", hf)
                ratios(hf)
            if stop == 1:
                return
            for hf in range(2):
                rstds("ff0", hf)

            def weights_rest(e):
                pool.wait_ge(s("w1_hi"), e + 1)
                pool.tensor_tensor(w1lo[:, e, :], w1f[:, e, :], w1hi[:, e, :].bitcast(f32), ALU.subtract
                                   ).then_inc(s("w1_lo"), 1)
                pool.tensor_tensor(w2lo[:, e, :, :], w2f[:, e, :, :], w2hi[:, e, :, :].bitcast(f32), ALU.subtract
                                   ).then_inc(s("w1_lo"), 1)

            weights_rest(0)
            for n in range(NT):
                pool.wait_ge(s("ff0_pa"), n + 1)
                pool.wait_ge(s("ff0_pd"), n + 1)
                pool.tensor_tensor(prod[:, n % 2, 0:4, :], prod[:, n % 2, 0:4, :], prod[:, n % 2, 4:8, :], ALU.add
                                   ).then_inc(s("ff0_ps"), 1)
            if stop == 2:
                return
            for hf in range(2):
                rstds("at1", hf)
            pool.wait_ge(s("ld_at1"), 7 * 16)
            for i in range(2):
                pool.tensor_copy(rv[:, i, :, 2 * D:2 * D + 2], sincos[:, :, :])
            pool.wait_ge(s("ln_xn"), ln("at1", NT) + NT)
            pool.tensor_tensor(x[:, :, :], x[:, :, :], bo1[:, :].unsqueeze(1).broadcast_to([P, NT, D]), ALU.add
                               ).then_inc(s("at1_bo"), 1)

            def values(b):
                i = b % 2
                pool.wait_ge(s("at1_qe"), TPB * (b + 1))
                if b >= 2:
                    pool.wait_ge(s("at1_kv"), b - 1)
                for t in range(TPB):
                    for a in range(2):
                        last = pool.tensor_scalar(rv[:, i, t, a * D:a * D + D], qkv[:, i, t, 2 * D:3 * D],
                                                  sincos[:, t, a:a + 1], None, ALU.mult)
                last.then_inc(s("at1_rv"), 1)

            values(0)
            for b in range(B):
                pool.wait_ge(s("at1_nrm"), b + 1)
                pool.tensor_scalar(kc[:, b % 2, :, :], qkv[:, b % 2, :, D:2 * D], -1.0, 1.0, ALU.mult, ALU.add
                                   ).then_inc(s("at1_kc"), 1)
                if b + 1 < B:
                    values(b + 1)
            for e in range(1, E1):
                weights_rest(e)
            if stop == 3:
                return
            for hf in range(2):
                rstds("xa1", hf)
            attention_values("xa1", v1_tok)
            if stop == 4:
                return
            for hf in range(2):
                rstds("ff1", hf)
            cur = xnT

            def round_(r):
                for u in range(2 * E1):
                    U, hf = 2 * E1 * r + u, u // E1
                    c = slice(hf * HALF, hf * HALF + HALF)
                    pool.wait_ge(s("ff1_cmb"), 2 + U + 1)
                    pool.wait_ge(s("ff1_pad"), 2 + U)
                    pool.tensor_tensor(cur[:, c], cur[:, c], yw[:, u % 2, :], ALU.add).then_inc(s("ff1_pad"), 1)

            with pool.Fori(0, R1) as r:
                round_(r)

        @block.scalar
        def _(act):
            for L in ("at0", "xa1"):
                act.sem_inc(s(L + "_qsev"), 2)
                act.sem_inc(s(L + "_ksev"), 1)
                act.sem_inc(s(L + "_exp"), 2)
                act.sem_inc(s(L + "_oT"), 1)
            act.sem_inc(s("ff1_gel"), 4)
            act.sem_inc(s("ff1_ctev"), 1)
            act.sem_inc(s("ff1_cwb"), 1)
            for name, dst, src in (("ctx", ctxT[:, :], "ctxT"), ("ctx", wctx[:, :, :], "wctx"),
                                   ("ident", ident[:, :], "ident")):
                act.dma_start(dst, w[src]).then_inc(s("ld_" + name), 16)

            def evacuate_xnT(L, hf, bank=None):
                act.wait_ge(s("ln_xT"), ln(L, 2) + hf + 1)
                act.activation(xnT[:, hf * HALF:hf * HALF + HALF], ps[:, bank or 6 + hf, :], ACT.Copy
                               ).then_inc(s("ln_xnT"), 1)

            def context(tiles):
                for n in tiles:
                    b, jt = n // TPB, n % TPB
                    act.wait_ge(s("ctx_pe"), n + 1)
                    act.activation(ek[:, jt, b, :], ps[:, 4 + n % 2, 0:D], ACT.Copy)
                    act.activation(ekv[:, jt, b, :], ps[:, 4 + n % 2, D:2 * D], ACT.Copy)
                    act.activation(v1_tok[:, n, :], ps[:, 4 + n % 2, 2 * D:3 * D], ACT.Copy).then_inc(s("ctx_ev"), 1)

            def rotated(hf):
                for n, a in enumerate((1, 0)):
                    act.wait_ge(s(("at0_sum", "at0_sum1")[hf]), n + 1)
                    act.activation(qhi[:, a, hf * HALF:hf * HALF + HALF], rot1[hf][:, a, :], ACT.Copy
                                   ).then_inc(s("at0_hi"), 1)

            context(range(NT // 2))
            for hf in range(2):
                evacuate_xnT("at0", hf)
            for hf in range(2):
                act.wait_ge(s("at0_v"), hf + 1)
                act.activation(v_tok[:, 4 * hf:4 * hf + 4, :], ps[:, 6 + hf, :].rearrange("p (n d) -> p n d", d=D),
                               ACT.Copy).then_inc(s("at0_vev"), 1)
            rotated(0)
            context(range(NT // 2, NT))

            def before_at0_scores():
                rotated(1)
                act.wait_ge(s("ctx_kd"), TPB)
                act.activation(ek[:, :, :, :], ek[:, :, :, :], ACT.Exp).then_inc(s("ctx_ek"), 1)
                act.wait_ge(s("ctx_kd"), TPB + 1)
                act.activation(expbT[:, :, :], expbT[:, :, :], ACT.Exp).then_inc(s("ctx_ek"), 1)

            def evacuate_aft_sums(hf):
                c = slice(hf * HALF, hf * HALF + HALF)
                act.wait_ge(s("xa0_dn"), 2 * hf + 1)
                act.activation(weights[:, c], ps[:, 2 * hf, :], ACT.Copy).then_inc(s("xa0_dne"), 1)
                act.wait_ge(s("xa0_dn"), 2 * hf + 2)
                act.activation(ratio[:, c], ps[:, 2 * hf + 1, :], ACT.Copy, scale=0.5).then_inc(s("xa0_dne"), 1)

            def attention(L, causal):
                def stacked_keys(b, gg):
                    act.wait_ge(s(L + "_kstk"), 2 * b + gg + 1)
                    for g in (2 * gg, 2 * gg + 1):
                        wait(act, s(L + "_km%d" % g), 16 * HPG * b)
                    act.activation(ks[:, 2 * gg:2 * gg + 2, :], ps[:, 7, :].rearrange("p (g t) -> p g t", g=2),
                                   ACT.Identity, bias=one_row[:, :]).then_inc(s(L + "_ksev"), 1)

                def stacked_queries(b, g):
                    act.wait_ge(s(L + "_qstk"), 2 * b + g // 2 + 1)
                    act.activation(qs[:, g, :], ps[:, 6, (g % 2) * T:(g % 2) * T + T], ACT.Copy
                                   ).then_inc(s(L + "_qsev"), 1)

                def step(k, b, follow):
                    if follow is None and not causal and k == AFT_STEP + 1:
                        evacuate_aft_sums(0)
                    if 7 <= k < H + 7:
                        h = k - 7
                        if there(b):
                            act.wait_ge(s(L + "_s"), H + H * b + h + 1)
                            if h % HPG == 0:
                                act.wait_ge(s(L + "_pv"), G + G * b + h // HPG - 1)
                            c = slice(P if causal else 0, TPB * T)
                            act.activation(prob[:, h % 8, c], ps[:, 2 + h % 2, c], ACT.Exp, scale=DH ** -0.5
                                           ).then_inc(s(L + "_exp"), 1)
                    if k in (5, 7) and there(b):
                        stacked_queries(b, 2 + k // 7)
                    if k in (12, 15) and follow:
                        stacked_queries(b + 1, k // 15)
                    if k in (8, 15) and follow:
                        stacked_keys(b + 1, int(k == 15))
                    if k in (17, 25) and there(b):
                        gg = k // 8 - 2
                        act.wait_ge(s(L + "_pv"), G + G * b + 2 * gg + 2)
                        act.activation(oT[:, 2 * gg:2 * gg + 2, :], ps[:, 4, :].rearrange("p (g t) -> p g t", g=2),
                                       ACT.Copy).then_inc(s(L + "_oT"), 1)
                    if causal and k == 30 and there(b):
                        act.wait_ge(s(L + "_onT"), b + 1)
                        act.activation(oNT[:, :, :], ps[:, 7, 0:TPB * P].rearrange("p (t n) -> p t n", t=TPB),
                                       ACT.Copy).then_inc(s(L + "_onTev"), 1)

                pipelined(act, step, None if causal else before_at0_scores,
                          beside={H + 9: lambda: evacuate_xnT("ff1", 0, 1)} if causal else {})

            attention("at0", False)
            if stop == 0:
                return
            evacuate_aft_sums(1)
            for hf in range(2):
                evacuate_xnT("xa0", hf)
                act.wait_ge(s("xa0_q"), hf + 1)
                act.activation(gate_q[:, hf * HALF:hf * HALF + HALF], ps[:, 4 + hf, :], ACT.Tanh, scale=0.5
                               ).then_inc(s("xa0_th"), 1)
            for k in range(2):
                act.wait_ge(s("we_pe"), 4 * (k + 1))
                act.activation(we0[:, 4 * k:4 * k + 4, :], ps[:, 4 + k, :].rearrange("p (e d) -> p e d", d=D),
                               ACT.Copy).then_inc(s("we_ev"), 1)
            if stop == 1:
                return
            for hf in range(2):
                evacuate_xnT("ff0", hf)
            for hf in range(2):
                act.wait_ge(s("ctx_k1"), hf + 1)
                act.activation(k1hi[:, hf * HALF:hf * HALF + HALF], ps[:, 6 + hf, :], ACT.Copy).then_inc(s("ctx_hi"), 1)
            act.wait_ge(s("ctx_vm"), 1)
            act.activation(vmean[:, :, :], ps[:, 5, :].rearrange("p (b d) -> p b d", b=B), ACT.Copy
                           ).then_inc(s("ctx_vme"), 1)

            def rounded_weights(experts):
                for e in experts:
                    act.activation(w1hi[:, e, :], w1f[:, e, :], ACT.Copy)
                    act.activation(w2hi[:, e, :, :], w2f[:, e, :, :], ACT.Copy).then_inc(s("w1_hi"), 1)

            act.wait_ge(s("ld_w1"), 32)
            rounded_weights(range(1))
            act.wait_ge(s("ff0_dif"), 1)
            act.activation(dif[:, :], dif[:, :], ACT.Tanh).then_inc(s("ff0_th"), 1)
            act.wait_ge(s("ff0_cw"), 1)
            for n in range(NT):
                act.wait_ge(s("ff0_y"), n + 1)
                if n >= 2:
                    act.wait_ge(s("ff0_red"), n - 1)
                for e in range(E0 // 2):
                    last = act.activation(prod[:, n % 2, e, :], ps[:, 2 * (n % 2), e * D:e * D + D], ACT.Copy,
                                          scale=cw[:, n * E0 + e:n * E0 + e + 1])
                last.then_inc(s("ff0_pa"), 1)
            rounded_weights(range(1, E1))
            if stop == 2:
                return
            for hf in range(2):
                evacuate_xnT("at1", hf)

            def exponentials(b):
                act.wait_ge(s("at1_sub"), b + 1)
                act.activation(qkv[:, b % 2, :, 0:2 * D], qkv[:, b % 2, :, 0:2 * D], ACT.Exp).then_inc(s("at1_ex"), 1)

            def queries(b):
                act.wait_ge(s("at1_qT"), b + 1)
                if b >= 2:
                    act.wait_ge(s("at1_out"), TPB * (b - 1))
                act.activation(qT[:, b % 2, 0, :], ps[:, 6, 0:T], ACT.Copy)
                act.activation(qT[:, b % 2, 1, :], ps[:, 6, 0:T], ACT.Copy, scale=-1.0, bias=1.0).then_inc(s("at1_qTe"), 1)

            def result(b):
                act.wait_ge(s("at1_aT"), b + 1)
                act.activation(attT.rearrange("p (l b) -> p b l", b=B)[:, b, :], ps[:, 7, 0:T], ACT.Copy
                               ).then_inc(s("at1_aTe"), 1)

            exponentials(0)
            exponentials(1)
            queries(0)
            for b in range(B):
                if b + 2 < B:
                    exponentials(b + 2)
                if b + 1 < B:
                    queries(b + 1)
                result(b)
            if stop == 3:
                return
            for hf in range(2):
                evacuate_xnT("xa1", hf)
                act.wait_ge(s("xa1_q"), hf + 1)
                act.activation(qhi[:, 0, hf * HALF:hf * HALF + HALF], ps[:, hf, :], ACT.Copy).then_inc(s("xa1_hi"), 1)
            attention("xa1", True)

            def spread_weights(U, u):
                act.wait_ge(s("ff1_bcd"), U + 1)
                act.activation(cwb[:, u % 8, :], ps[:, 6, :], ACT.Copy).then_inc(s("ff1_cwb"), 1)

            def gelus(U, u):
                for c in range(FC):
                    n = FC * U + c
                    act.wait_ge(s("ff1_up"), n + 1)
                    act.wait_ge(s("ff1_glo"), n + 1)
                    act.activation(gel[:, c, :], ps[:, c, :], ACT.Gelu_apprx_tanh,
                                   bias=b1[:, u % E1, c:c + 1]).then_inc(s("ff1_gel"), 1)

            def gate_tanh(Hf):
                act.wait_ge(s("ff1_dif"), Hf + 1)
                act.activation(dif[:, 0:4 * E1], dif[:, 0:4 * E1], ACT.Tanh).then_inc(s("ff1_th"), 1)

            def gate_rows(Hf, hf, bank=7):
                act.wait_ge(s("ff1_ct"), Hf + 1)
                act.activation(cwT[:, hf, :], ps[0:2 * E1, bank, :], ACT.Copy).then_inc(s("ff1_ctev"), 1)

            def round_(r, last):
                U0, H0 = 2 * E1 * r, 2 * r
                for u in range(2 * E1):
                    if u == 3:
                        gate_rows(H0 + 1, 1)
                    if u == 7 and not last:
                        gate_rows(H0 + 2, 0)
                    if not (last and u == 7):
                        spread_weights(U0 + u + 1, u + 1)
                        gelus(U0 + u + 1, u + 1)
                    if u == 0:
                        gate_tanh(H0 + 1)
                    if u == 4 and not last:
                        gate_tanh(H0 + 2)

            gate_tanh(0)
            gelus(0, 0)
            gate_rows(0, 0, 6)
            evacuate_xnT("ff1", 1, 5)
            spread_weights(0, 0)
            with act.Fori(0, R1 - 1) as r:
                round_(r, False)
            round_(R1 - 1, True)

        @block.vector
        def _(dve):
            own = OwnOrder(dve, s("dve_own"))
            v = nc.vector
            for L in ("at0", "xa1"):
                dve.sem_inc(s(L + "_red"), 2)
                dve.sem_inc(s(L + "_mrg"), 1)
                dve.sem_inc(s(L + "_on"), 1)
                dve.sem_inc(s(L + "_res"), TPB)
            dve.sem_inc(s("ff1_glo"), 4)
            dve.sem_inc(s("ff1_cmb"), 2)

            def ln_stats(L, hf):
                tiles = range(4 * hf, 4 * hf + 4)
                own.wait()
                for n in tiles:
                    own.mark(v.bn_stats(stats[:, n, :], x[:, n, :]))
                own.wait()
                for n in tiles:
                    v.bn_aggr(mv[:, n, :], stats[:, n, :]).then_inc(s("ln_mv"), 1)

            def ln_normalise(L, hf):
                dve.wait_ge(s("ln_rstd"), ln(L, 2) + hf + 1)
                for n in range(4 * hf, 4 * hf + 4):
                    v.tensor_scalar(xn[:, n, :], x[:, n, :], mv[:, n, 0:1], rstd[:, n:n + 1], ALU.subtract, ALU.mult
                                    ).then_inc(s("ln_xn"), 1)

            dve.wait_ge(s("ld_x"), 16)
            ln_stats("at0", 0)
            ln_stats("at0", 1)
            ln_normalise("at0", 0)
            ln_normalise("at0", 1)
            dve.wait_ge(s("ld_sel"), 32)
            own.mark(v.tensor_copy(selr[:, :, :, :, :], sel))

            dve.wait_ge(s("ld_rope"), 16)

            def rotate(hf, n, a):
                for part_, dst in enumerate((rot1[hf], rot2[hf])):
                    dve.wait_ge(s("at0_qk"), 4 * hf + 2 * n + part_ + 1)
                    v.tensor_tensor(dst[:, a, :].rearrange("p (b t) -> p b t", b=2),
                                    ps[:, 2 * a + part_, :].rearrange("p (b t) -> p b t", b=2),
                                    rope[:, part_:part_ + 1, :].broadcast_to([P, 2, T]), ALU.mult
                                    ).then_inc(s("at0_rot"), 1)

            def rotated_sum(n, a):
                dve.wait_ge(s("at0_rot"), 2 * (n + 1))
                v.tensor_tensor(rot1[0][:, a, :], rot1[0][:, a, :], rot2[0][:, a, :], ALU.add).then_inc(s("at0_sum"), 1)

            def rotated_rest(n, a):
                dve.wait_ge(s("at0_hi"), n + 1)
                v.tensor_tensor(qlo[:, a, 0:HALF], rot1[0][:, a, :], qhi[:, a, 0:HALF].bitcast(f32), ALU.subtract
                                ).then_inc(s("at0_lo"), 1)

            rotate(0, 0, 1)
            rotated_sum(0, 1)
            rotate(0, 1, 0)
            rotated_rest(0, 1)
            rotated_sum(1, 0)
            rotate(1, 0, 1)
            rotated_rest(1, 0)
            rotate(1, 1, 0)
            dve.wait_ge(s("ctx_ev"), NT)
            own.mark(v.tensor_tensor(ctx_max[:, 0, :, :], ek[:, :, 0, :], ek[:, :, 1, :], ALU.max))
            own.step(v.tensor_tensor(ctx_max[:, 1, :, :], ek[:, :, 2, :], ek[:, :, 3, :], ALU.max))
            v.tensor_tensor(ctx_max[:, 2, :, :], ctx_max[:, 0, :, :], ctx_max[:, 1, :, :], ALU.max
                            ).then_inc(s("ctx_mx"), 1)

            def reciprocal_weights(hf):
                c = slice(hf * HALF, hf * HALF + HALF)
                dve.wait_ge(s("xa0_dne"), 2 * hf + 1)
                v.reciprocal(weights[:, c], weights[:, c]).then_inc(s("xa0_rec"), 1)

            def attention(L, causal, next_layer, beside={}):
                def step(k, b, follow):
                    if not there(b):
                        return
                    if follow is None and k == AFT_STEP:
                        dve.wait_ge(s(L + "_res"), TPB + 2 * TPB)
                        ln_stats(next_layer, 0)
                    if follow is None and not causal and k == AFT_STEP + 1:
                        reciprocal_weights(0)
                    if follow is None and k == AFT_STEP + 1:
                        ln_normalise(next_layer, 0)
                    if k < H:
                        dve.wait_ge(s(L + "_mx"), H * b + k + 1)
                        g, j = k // HPG, k % HPG
                        col = QUAD * j + MAXROW
                        v.tensor_reduce(nmax[:, :, g, col:col + 1],
                                        ps[:, k % 2, :].rearrange("p (t k) -> p t k", t=TPB), AX.X, ALU.max,
                                        negate=True).then_inc(s(L + "_red"), 1)
                    if k in (5, 9, 13, 17):
                        g = (k - 5) // 4
                        dve.wait_ge(s(L + "_t"), G * b + g + 1)
                        v.tensor_tensor(qs[:, g, :], ps[:, 5, 0:T], qs[:, g, :].bitcast(f32), ALU.add
                                        ).then_inc(s(L + "_mrg"), 1)
                    if k in (27, 28):
                        t = k - 27
                        dve.wait_ge(s(L + "_o"), TPB * b + t + 1)
                        o = ps[:, 7, :].rearrange("p (h c) -> p h c", c=QUAD)
                        v.reciprocal(rs[:, t, :].unsqueeze(2), o[:, :, DH:DH + 1]).then_inc(s(L + "_rs"), 1)
                        dve.wait_ge(s(L + "_rs"), TPB * b + t + 1)
                        on = v.tensor_tensor(oN[:, t, :].rearrange("p (h d) -> p h d", d=DH), o[:, :, 0:DH],
                                             rs[:, t, :].unsqueeze(2).broadcast_to([P, H, DH]), ALU.mult)
                        if causal:
                            on.then_inc(s(L + "_on1"), 1)
                            dve.wait_ge(s(L + "_on1"), TPB * b + t + 1)
                            v.tensor_tensor(odif[:, t:t + 1, :], vmean[:, ds(b, 1), :], oN[:, t:t + 1, :],
                                            ALU.subtract).then_inc(s(L + "_odif"), 1)
                            dve.wait_ge(s(L + "_odif"), TPB * b + t + 1)
                            v.scalar_tensor_tensor(oN[:, t, :], odif[:, t, :], maskf[:, ds(TPB * b + t, 1)],
                                                   oN[:, t, :], ALU.mult, ALU.add).then_inc(s(L + "_on"), 1)
                        else:
                            on.then_inc(s(L + "_on"), 1)
                            dve.wait_ge(s(L + "_on"), 1 + TPB * b + t + 1)
                            xb = x[:, ds(TPB * b + t, 1), :]
                            v.tensor_tensor(xb, xb, oN[:, t:t + 1, :], ALU.add).then_inc(s(L + "_res"), 1)
                    if causal and k == 31:
                        dve.wait_ge(s(L + "_wo"), b + 1)
                        xb = x[:, ds(TPB * b, TPB), :]
                        v.tensor_tensor(xb, xb, ps[:, 7, 0:TPB * D].rearrange("p (t d) -> p t d", t=TPB), ALU.add
                                        ).then_inc(s(L + "_res"), TPB)

                pipelined(dve, step, beside=beside)
                dve.wait_ge(s(L + "_res"), TPB * B + TPB)

            dve.wait_ge(s("const"), 6)
            attention("at0", False, "xa0")

            def finish():
                own.wait()
                dve.sem_inc(s("final"), 2)
            if stop == 0:
                return finish()

            ln_stats("xa0", 1)
            reciprocal_weights(1)
            ln_normalise("xa0", 1)
            for hf in range(2):
                c = slice(hf * HALF, hf * HALF + HALF)
                dve.wait_ge(s("xa0_th"), hf + 1)
                dve.wait_ge(s("xa0_rat"), hf + 1)
                v.scalar_tensor_tensor(yT[:, c], gate_q[:, c], 1.0, ratio[:, c], ALU.add, ALU.mult
                                       ).then_inc(s("xa0_y"), 1)
            for hf in range(2):
                dve.wait_ge(s("xa0_o"), hf + 1)
                xb = x[:, 4 * hf:4 * hf + 4, :]
                v.tensor_tensor(xb, xb, ps[:, hf, :].rearrange("p (n d) -> p n d", d=D), ALU.add
                                ).then_inc(s("xa0_res"), 1)
                dve.wait_ge(s("xa0_res"), hf + 1)
                ln_stats("ff0", hf)
            if stop == 1:
                return finish()

            def gates_before(lps, bias, tie, n, E):
                m = n * E
                lv, lv3 = lg[:, 0:m], lg[:, 0:m].rearrange("p (n e) -> p n e", e=E)
                if bias is None:
                    own.step(v.tensor_copy(lv3, lps))
                else:
                    own.step(v.tensor_tensor(lv3, lps, bias, ALU.add))
                other = lv3.unsqueeze(2).broadcast_to([P, n, E, E])
                this = lv3.unsqueeze(3).broadcast_to([P, n, E, E])
                gt4 = gt[:, 0:m * E].rearrange("p (n e f) -> p n e f", e=E, f=E)
                eq4 = eqt[:, 0:m * E].rearrange("p (n e f) -> p n e f", e=E, f=E)
                own.mark(v.tensor_tensor(gt4, other, this, ALU.is_gt))
                own.step(v.tensor_tensor(eq4, other, this, ALU.is_equal))
                own.step(v.tensor_tensor(eq4, eq4, tie.unsqueeze(1).broadcast_to([P, n, E, E]), ALU.mult))
                own.step(v.tensor_tensor(gt4, gt4, eq4, ALU.add))
                own.step(v.tensor_reduce(rank[:, 0:m], gt[:, 0:m * E].rearrange("p (m f) -> p m f", f=E), AX.X, ALU.add))
                own.step(v.tensor_scalar(selh[:, 0:m], rank[:, 0:m], 2.0, 0.5, ALU.is_lt, ALU.mult))
                own.step(v.tensor_tensor(lsel[:, 0:m], selh[:, 0:m], lv, ALU.mult))
                own.step(v.tensor_reduce(half_sum[:, 0:n], lsel[:, 0:m].rearrange("p (n e) -> p n e", e=E), AX.X, ALU.add))
                return v.tensor_tensor(dif[:, 0:m].rearrange("p (n e) -> p n e", e=E), lv3,
                                       half_sum[:, 0:n].unsqueeze(2).broadcast_to([P, n, E]), ALU.subtract)

            for hf in range(2):
                ln_normalise("ff0", hf)
            dve.wait_ge(s("ld_gate0"), 32)
            dve.wait_ge(s("ff0_lg"), 1)
            gates_before(ps[:, 4, 0:NT * E0].rearrange("p (n e) -> p n e", e=E0), None, tie0[:, :, :], NT, E0
                         ).then_inc(s("ff0_dif"), 1)
            dve.wait_ge(s("ff0_th"), 1)
            v.scalar_tensor_tensor(cw[:, :], dif[:, :], 1.0, selh[:, :], ALU.add, ALU.mult).then_inc(s("ff0_cw"), 1)
            dve.wait_ge(s("ff0_cw"), 1)
            for n in range(NT + 1):
                if n < NT:
                    dve.wait_ge(s("ff0_y"), n + 1)
                    v.tensor_tensor(prod[:, n % 2, 4:8, :], ps[:, 2 * (n % 2) + 1, :].rearrange("p (e d) -> p e d", d=D),
                                    cw[:, n * E0 + 4:n * E0 + 8].unsqueeze(2).broadcast_to([P, E0 // 2, D]), ALU.mult
                                    ).then_inc(s("ff0_pd"), 1)
                if n >= 1:
                    m = n - 1
                    dve.wait_ge(s("ff0_ps"), m + 1)
                    v.tensor_reduce(yT[:, m * D:m * D + D], prod[:, m % 2, 0:4, :].rearrange("p e d -> p d e"), AX.X, ALU.add
                                    ).then_inc(s("ff0_red"), 1)
                    dve.wait_ge(s("ff0_red"), m + 1)
                    own.mark(v.tensor_tensor(x[:, m, :], x[:, m, :], yT[:, m * D:m * D + D], ALU.add))
                    if m == NT // 2:
                        ln_stats("at1", 0)
            if stop == 2:
                return finish()

            def k1_rest():
                for hf in range(2):
                    c = slice(hf * HALF, hf * HALF + HALF)
                    dve.wait_ge(s("ctx_hi"), hf + 1)
                    v.tensor_tensor(k1lo[:, c], ps[:, 6 + hf, :], k1hi[:, c].bitcast(f32), ALU.subtract
                                    ).then_inc(s("ctx_lo"), 1)

            ln_stats("at1", 1)
            ln_normalise("at1", 0)
            k1_rest()
            ln_normalise("at1", 1)
            dve.wait_ge(s("ld_at1"), 7 * 16)

            def project(b):
                i = b % 2
                for t in range(TPB):
                    n = TPB * b + t
                    dve.wait_ge(s("at1_qkv"), n + 1)
                    v.tensor_tensor(qkv[:, i, t, :], ps[:, n % 2, 0:3 * D], bqkv1[:, :, :].rearrange("p a d -> p (a d)"),
                                    ALU.add).then_inc(s("at1_qe"), 1)
                dve.wait_ge(s("at1_qe"), TPB * (b + 1))
                heads = qkv[:, i, :, 0:2 * D].rearrange("p t (g d) -> p t g d", d=DH)
                own.step(v.tensor_reduce(mxq[:, i, 0:TPB, :], heads, AX.X, ALU.max))
                v.tensor_tensor(heads, heads, mxq[:, i, 0:TPB, :].unsqueeze(3).broadcast_to([P, TPB, 2 * H, DH]),
                                ALU.subtract).then_inc(s("at1_sub"), 1)

            def normalise(b):
                i = b % 2
                dve.wait_ge(s("at1_ex"), b + 1)
                heads = qkv[:, i, :, 0:2 * D].rearrange("p t (g d) -> p t g d", d=DH)
                sums = sumq[:, i, 0:TPB, :]
                own.step(v.tensor_reduce(sums, heads, AX.X, ALU.add))
                own.step(v.reciprocal(sums, sums))
                v.tensor_tensor(heads, heads, sums.unsqueeze(3).broadcast_to([P, TPB, 2 * H, DH]), ALU.mult
                                ).then_inc(s("at1_nrm"), 1)

            def blocks(b):
                dve.wait_ge(s("at1_kv"), b + 1)
                if b >= 1:
                    dve.wait_ge(s("at1_out"), TPB * b)
                for a in range(2):
                    halves = bd[:, a, :].rearrange("p (z c) -> p z c", z=2)
                    v.tensor_tensor(halves[:, :, 0:D], ps[:, 4 + a, 0:2 * D].rearrange("p (z c) -> p z c", z=2),
                                    diag[:, :].unsqueeze(1).broadcast_to([P, 2, D]), ALU.mult)
                    last = v.tensor_tensor(halves[:, :, D:D + H],
                                           ps[:, 4 + a, 2 * D:2 * D + 2].unsqueeze(2).broadcast_to([P, 2, H]),
                                           diag_h[:, :].unsqueeze(1).broadcast_to([P, 2, H]), ALU.mult)
                last.then_inc(s("at1_bd"), 1)

            def outputs(b):
                for t in range(TPB):
                    dve.wait_ge(s("at1_out"), TPB * b + t + 1)
                    if b >= 1 and t == 0:
                        dve.wait_ge(s("at1_aT"), b)
                    own.step(v.tensor_scalar(part[:, :, :], ps[:, 2:4, 0:D + H], sincos[:, t, 0:1], None, ALU.mult))
                    v.scalar_tensor_tensor(comb[:, :, :], ps[:, 2:4, D + H:2 * (D + H)], sincos[:, t, 1:2],
                                           part[:, :, :], ALU.mult, ALU.add).then_inc(s("at1_comb"), 1)
                    dve.wait_ge(s("at1_comb"), TPB * b + t + 1)
                    z = comb[:, :, D:D + H]
                    own.step(v.tensor_scalar(z, z, Z_EPS, None, ALU.max))
                    own.step(v.reciprocal(z, z))
                    own.step(v.tensor_tensor(att2[:, :, :].rearrange("p a (h d) -> p a h d", d=DH),
                                             comb[:, :, 0:D].rearrange("p a (h d) -> p a h d", d=DH),
                                             z.unsqueeze(3).broadcast_to([P, 2, H, DH]), ALU.mult))
                    v.tensor_tensor(att[:, t, :], att2[:, 0, :], att2[:, 1, :], ALU.add).then_inc(s("at1_att"), 1)

            project(0)
            project(1)
            normalise(0)
            for b in range(B):
                if b + 1 < B:
                    normalise(b + 1)
                blocks(b)
                if b + 2 < B:
                    project(b + 2)
                outputs(b)
            dve.wait_ge(s("at1_bo"), 1)
            for hf in range(2):
                dve.wait_ge(s("at1_wo"), hf + 1)
                xb = x[:, 4 * hf:4 * hf + 4, :]
                own.mark(v.tensor_tensor(xb, xb, ps[:, hf, :].rearrange("p (n d) -> p n d", d=D), ALU.add))
                ln_stats("xa1", hf)
            if stop == 3:
                return finish()

            for hf in range(2):
                ln_normalise("xa1", hf)
            dve.wait_ge(s("ld_xa1"), 64)
            dve.wait_ge(s("ld_ff1"), 6 * 16)
            own.mark(v.tensor_copy(sel_er[:, :, :], sel_e[:, :, :]))
            own.mark(v.tensor_scalar(maskf[:, :], mask_i[:, :], 0, None, ALU.not_equal))
            own.wait()
            for hf in range(2):
                c = slice(hf * HALF, hf * HALF + HALF)
                dve.wait_ge(s("xa1_hi"), hf + 1)
                v.tensor_tensor(qlo[:, 0, c], ps[:, hf, :], qhi[:, 0, c].bitcast(f32), ALU.subtract
                                ).then_inc(s("xa1_lo"), 1)
            cur = xnT

            def split_cur(hf):
                c = slice(hf * HALF, hf * HALF + HALF)
                own.step(v.tensor_copy(xhi[:, c], cur[:, c]))
                v.tensor_tensor(xlo[:, c], cur[:, c], xhi[:, c].bitcast(f32), ALU.subtract).then_inc(s("ff1_xs"), 1)

            def gate_a(Hf, r, bank=7):
                dve.wait_ge(s("ff1_lg"), Hf + 1)
                gates_before(ps[:, bank, 0:4 * E1].rearrange("p (n e) -> p n e", e=E1),
                             bg1[:, ds(r, 1), :].broadcast_to([P, 4, E1]), tie1[:, :, :], 4, E1
                             ).then_inc(s("ff1_dif"), 1)

            def first_gates():
                dve.wait_ge(s("ln_xnT"), ln("ff1", 2) + 1)
                split_cur(0)
                gate_a(0, 0, 6)

            attention("xa1", True, "ff1", {H + 12: first_gates})

            def gate_b(Hf):
                m = 4 * E1
                dve.wait_ge(s("ff1_th"), Hf + 1)
                own.step(v.scalar_tensor_tensor(cw[:, 0:m], dif[:, 0:m], 1.0, selh[:, 0:m], ALU.add, ALU.mult))
                own.step(v.tensor_copy(cwr[:, 0:m], cw[:, 0:m]))
                c3, r3 = (a[:, 0:m].rearrange("p (n e) -> p n e", e=E1) for a in (cw, cwr))
                own.mark(v.tensor_copy(cwhl[:, :, 0:E1], r3.bitcast(f32)))
                v.tensor_tensor(cwhl[:, :, E1:2 * E1], c3, r3.bitcast(f32), ALU.subtract).then_inc(s("ff1_cwd"), 1)

            def split_gelus(U, u):
                for c in range(FC):
                    n = FC * U + c
                    dve.wait_ge(s("ff1_gel"), 4 + n + 1)
                    if c == 0:
                        dve.wait_ge(s("ff1_dn"), U + 1)
                    v.tensor_copy(ghi[:, u % 2, c, :], gel[:, c, :]).then_inc(s("ff1_ghi"), 1)
                    dve.wait_ge(s("ff1_ghi"), n + 1)
                    v.tensor_tensor(glo[:, u % 2, c, :], gel[:, c, :], ghi[:, u % 2, c, :].bitcast(f32), ALU.subtract
                                    ).then_inc(s("ff1_glo"), 1)

            def combine(U, u):
                dve.wait_ge(s("ff1_dn"), 2 + U + 1)
                dve.wait_ge(s("ff1_cwb"), 1 + U + 1)
                dve.wait_ge(s("ff1_pad"), U + 1)
                v.scalar_tensor_tensor(yw[:, u % 2, :], ps[:, 4 + u % 2, :], b2[:, u % E1:u % E1 + 1], cwb[:, u, :],
                                       ALU.add, ALU.mult).then_inc(s("ff1_cmb"), 1)

            def round_(r, last):
                U0, H0 = 2 * E1 * r, 2 * r
                for u in range(2 * E1):
                    if u == 1:
                        dve.wait_ge(s("ff1_pad"), U0 + 2)
                        split_cur(1)
                    if u == 5 and not last:
                        dve.wait_ge(s("ff1_pad"), U0 + 2 + E1)
                        split_cur(0)
                    if u == 1:
                        gate_b(H0 + 1)
                    if u == 5 and not last:
                        gate_b(H0 + 2)
                    if not (last and u == 7):
                        split_gelus(U0 + u + 1, u + 1)
                    combine(U0 + u, u)
                    if u == 0:
                        gate_a(H0 + 1, r)
                    if u == 4 and not last:
                        gate_a(H0 + 2, r + 1)

            ln_stats("ff1", 1)
            gate_b(0)
            ln_normalise("ff1", 1)
            split_gelus(0, 0)
            dve.wait_ge(s("ln_xnT"), ln("ff1", 2) + 2)
            per = 2 * 1 + 2 * (9 + 3)
            with dve.Fori(0, R1 - 1) as r:
                own.loop(r, per)
                round_(r, False)
                own.end(R1 - 1)
            round_(R1 - 1, True)
            for hf in range(2):
                dve.wait_ge(s("fin_T"), hf + 1)
                xb = x[:, 4 * hf:4 * hf + 4, :]
                v.tensor_tensor(xb, xb, ps[:, hf, :].rearrange("p (n d) -> p n d", d=D), ALU.add).then_inc(s("final"), 1)

        @block.tensor
        def _(pe):
            for L in ("at0", "xa1"):
                pe.sem_inc(s(L + "_pv"), G)
                pe.sem_inc(s(L + "_s"), H)
            pe.sem_inc(s("ff1_dn"), 2)

            def transpose_xn(L, hf, bank=None):
                for i in range(4):
                    n = 4 * hf + i
                    pe.wait_ge(s("ln_xn"), ln(L, NT) + n + 1)
                    last = pe.transpose(ps[:, bank or 6 + hf, i * P:i * P + P], xn[:, n, :], ident[:, :])
                last.then_inc(s("ln_xT"), 1)

            def context(tiles):
                for n in tiles:
                    if n >= 2:
                        pe.wait_ge(s("ctx_ev"), n - 1)
                    pe.matmul(ps[:, 4 + n % 2, 0:3 * D], ctxT[:, n * P:n * P + P], wctx[:, 0:3, :], start=True, stop=True
                              ).then_inc(s("ctx_pe"), 1)

            def rotary_projections(hf):
                c = slice(hf * HALF, hf * HALF + HALF)
                for n, k in enumerate((2, 3, 0, 1)):
                    if hf:
                        pe.wait_ge(s("at0_rot"), n + 1)
                    pe.matmul(ps[:, k, :], w0[:, k, :], xnT[:, c], start=True, stop=True).then_inc(s("at0_qk"), 1)

            pe.wait_ge(s("ld_ctx"), 32)
            context(range(NT // 2))
            pe.wait_ge(s("ld_ident"), 16)
            for hf in range(2):
                transpose_xn("at0", hf)
            pe.wait_ge(s("ld_w0"), 16)
            pe.wait_ge(s("ln_xnT"), ln("at0", 2) + 1)
            rotary_projections(0)
            for hf in range(2):
                pe.wait_ge(s("ln_xnT"), ln("at0", 2) + hf + 1)
                for n in range(4):
                    tile = 4 * hf + n
                    last = pe.matmul(ps[:, 6 + hf, n * D:n * D + D], xnT[:, tile * P:tile * P + P], w0[:, 4, :],
                                     start=True, stop=True)
                last.then_inc(s("at0_v"), 1)
            context(range(NT // 2, NT))
            rotary_projections(1)

            def attention(L, causal, k_hi, k_lo, before_first=None, before_loop=None, aft_sums=None,
                          beside={}):
                def stack(side, b, g, bank, hi, lo, done):
                    o = ps[:, bank, (g % 2) * T:(g % 2) * T + T]
                    pe.matmul(o, selr[:, side, g, 0, :], hi[:, ds(b * T, T)], start=True, stop=False)
                    last = pe.matmul(o, selr[:, side, g, 1, :], lo[:, ds(b * T, T)], start=False, stop=True)
                    if g % 2:
                        last.then_inc(done, 1)

                def stack_queries(b, g):
                    if g % 2 == 0:
                        pe.wait_ge(s(L + "_qsev"), G * b + g + 2)
                    stack(0, b, g, 6, qhi[:, 0, :], qlo[:, 0, :], s(L + "_qstk"))

                def stack_keys(b, g):
                    if g % 2 == 0:
                        pe.wait_ge(s(L + "_ksev"), 2 * b + g // 2 + 1)
                        wait(pe, s(L + "_on"), 1 + TPB * (b - 2 + g // 2))
                        if causal:
                            wait(pe, s(L + "_res"), TPB + TPB * (b - 2 + g // 2))
                    stack(1, b, g, 7, k_hi, k_lo, s(L + "_kstk"))

                def step(k, b, follow):
                    now = there(b)
                    if aft_sums and follow is None and k == AFT_STEP:
                        pe.wait_ge(s(L + "_red"), 2 + H * B)
                        aft_sums(0)
                    if k < H and now:
                        h = k
                        if h % HPG == 0:
                            pe.wait_ge(s(L + "_km%d" % (h // HPG)), 16 * HPG * (b + 1))
                        if h % HPG == 0:
                            pe.wait_ge(s(L + "_qsev"), 2 + G * b + h // HPG + 1)
                        pe.wait_ge(s(L + "_red"), H * b + h + 1)
                        for t in range(TPB):
                            at = place(t) * T
                            last = pe.matmul(ps[:, h % 2, at:at + T], qs[:, h // HPG, t * P:t * P + P], km[:, h, :],
                                             start=True, stop=not causal)
                            if causal:
                                last = pe.matmul(ps[:, h % 2, at + t * P:at + T], identb[:, :], trib[:, 0:TPB - t, :],
                                                 start=False, stop=True)
                        last.then_inc(s(L + "_mx"), 1)
                    if k in (5, 9, 13, 17) and now:
                        g = (k - 5) // 4
                        pe.wait_ge(s(L + "_red"), 2 + H * b + HPG * g + HPG)
                        pe.wait_ge(s(L + "_mrg"), G * b + g + 1)
                        for t in range(TPB):
                            last = pe.transpose(ps[:, 5, t * P:t * P + P], nmax[:, place(t), g, :], ident[:, :])
                        last.then_inc(s(L + "_t"), 1)
                    if 7 <= k < H + 7 and now:
                        h = k - 7
                        if h % HPG == 0:
                            pe.wait_ge(s(L + "_mrg"), 1 + G * b + h // HPG + 1)
                        pe.wait_ge(s(L + "_exp"), H * b + h + 1)
                        for t in range(TPB):
                            at = place(t) * T
                            last = pe.matmul(ps[:, 2 + h % 2, at:at + T], km[:, h, t * P:t * P + P], qs[:, h // HPG, :],
                                             start=True, stop=not causal)
                            if causal:
                                last = pe.matmul(ps[:, 2 + h % 2, at + t * P:at + t * P + P], identb[:, :],
                                                 trib[:, TPB, :], start=False, stop=True)
                        last.then_inc(s(L + "_s"), 1)
                    if 12 <= k < 28 and k % HPG < TPB and now:
                        g, t = (k - 12) // HPG, k % HPG
                        if t == 0:
                            pe.wait_ge(s(L + "_vaug"), G * b + g + 1)
                            if g % 2 == 0:
                                pe.wait_ge(s(L + "_oT"), TPB * b + g // 2 + 1)
                            pe.wait_ge(s(L + "_exp"), 2 + H * b + HPG * g + HPG)
                        for j in range(HPG):
                            h = HPG * g + j
                            first = P if causal and t else 0
                            last = pe.matmul(ps[QUAD * j:QUAD * j + QUAD, 4, (g % 2) * T + first:(g % 2) * T + T],
                                             vaug[:, t, h, :], prob[:, h % 8, place(t) * T + first:place(t) * T + T],
                                             start=(t == 0), stop=(t == TPB - 1))
                        if t == TPB - 1:
                            last.then_inc(s(L + "_pv"), 1)
                    if k in (3, 4) and now:
                        stack_queries(b, k - 1)
                    if k in (9, 10) and follow:
                        stack_queries(b + 1, k - 9)
                    if k in (7, 8) and follow:
                        stack_keys(b + 1, k - 7)
                    if k == 15 and follow:
                        stack_keys(b + 1, 2)
                        stack_keys(b + 1, 3)
                    if k == 27 and now:
                        pe.wait_ge(s(L + "_oT"), 1 + 2 * b + 2)
                    if k in (27, 28) and now:
                        t = k - 27
                        pe.wait_ge(s(L + "_ksev"), 1 + 2 * b + {True: 5, False: 4, None: 2}[follow])
                        pe.wait_ge(s(L + "_on"), TPB * b + t + 1)
                        for g in range(G):
                            last = pe.transpose(ps[:, 7, g * P:g * P + P], oT[:, g, t * P:t * P + P], ident[:, :])
                        last.then_inc(s(L + "_o"), 1)
                    if causal and k == 30 and now:
                        pe.wait_ge(s(L + "_on"), 1 + TPB * b + TPB)
                        for t in range(TPB):
                            last = pe.transpose(ps[:, 7, t * P:t * P + P], oN[:, t, :], ident[:, :])
                        last.then_inc(s(L + "_onT"), 1)
                    if causal and k == 31 and now:
                        pe.wait_ge(s(L + "_onTev"), b + 1)
                        for t in range(TPB):
                            last = pe.matmul(ps[:, 7, t * D:t * D + D], oNT[:, t, :], wx1[:, 1, :],
                                             start=True, stop=True)
                        last.then_inc(s(L + "_wo"), 1)

                pipelined(pe, step, before_first, before_loop, beside)

            def aft_sums(hf):
                pe.wait_ge(s("ctx_ek"), 2)
                pe.wait_ge(s("ctx_ekv"), 1)
                for a, src in enumerate((ek, ekv)):
                    for bl in range(2):
                        for t in range(TPB):
                            last = pe.matmul(ps[:, 2 * hf + a, bl * T:bl * T + T], src[:, t, 2 * hf + bl, :],
                                             expbT[:, t, :], start=(t == 0), stop=(t == TPB - 1))
                    last.then_inc(s("xa0_dn"), 1)

            pe.wait_ge(s("at0_vev"), 2)
            pe.wait_ge(s("at0_lo"), 2)
            attention("at0", False, qhi[:, 1, :], qlo[:, 1, :],
                      lambda: (pe.wait_ge(s("at0_rot"), 8), pe.wait_ge(s("ctx_ev"), NT)),
                      lambda: pe.wait_ge(s("at0_lo1"), 2),
                      aft_sums)
            if stop == 0:
                return

            aft_sums(1)
            pe.wait_ge(s("ld_xa0"), 32)
            for hf in range(2):
                transpose_xn("xa0", hf)
                pe.wait_ge(s("ln_xnT"), ln("xa0", 2) + hf + 1)
                pe.matmul(ps[:, 4 + hf, :], wx0[:, 0, :], xnT[:, hf * HALF:hf * HALF + HALF], start=True, stop=True
                          ).then_inc(s("xa0_q"), 1)
            for hf in range(2):
                pe.wait_ge(s("xa0_y"), hf + 1)
                for n in range(4):
                    tile = 4 * hf + n
                    last = pe.matmul(ps[:, hf, n * D:n * D + D], yT[:, tile * P:tile * P + P], wx0[:, 1, :],
                                     start=True, stop=True)
                last.then_inc(s("xa0_o"), 1)
            pe.wait_ge(s("ld_ff0"), 32)
            for e in range(E0):
                for c in range(F0 // P):
                    last = pe.matmul(ps[:, 4 + e // 4, (e % 4) * D:(e % 4) * D + D], wi0[:, e, c, :], wo0[:, e, c, :],
                                     start=(c == 0), stop=(c == F0 // P - 1))
                last.then_inc(s("we_pe"), 1)
            if stop == 1:
                return

            for hf in range(2):
                transpose_xn("ff0", hf)
            pe.wait_ge(s("ld_gate0"), 32)
            pe.wait_ge(s("we_ev"), 2)
            pe.wait_ge(s("ln_xnT"), ln("ff0", 2) + 2)
            for n in range(NT):
                last = pe.matmul(ps[:, 4, n * E0:n * E0 + E0], xnT[:, n * P:n * P + P], wgate0[:, :], start=True, stop=True)
            last.then_inc(s("ff0_lg"), 1)
            for hf in range(2):
                pe.matmul(ps[:, 6 + hf, :], wctx[:, 3, :], ctxT[:, hf * HALF:hf * HALF + HALF], start=True, stop=True
                          ).then_inc(s("ctx_k1"), 1)
            pe.wait_ge(s("const"), 6)
            for b in range(B):
                for k in range(TPB):
                    last = pe.matmul(ps[:, 5, b * D:b * D + D], mean_w[:, :], v1_tok[:, TPB * b + k, :],
                                     start=(k == 0), stop=(k == TPB - 1))
            last.then_inc(s("ctx_vm"), 1)
            for n in range(NT):
                if n >= 2:
                    pe.wait_ge(s("ff0_pa"), n - 1)
                    pe.wait_ge(s("ff0_pd"), n - 1)
                for k in range(2):
                    last = pe.matmul(ps[:, 2 * (n % 2) + k, :], xnT[:, n * P:n * P + P], we0[:, 4 * k:4 * k + 4, :],
                                     start=True, stop=True)
                last.then_inc(s("ff0_y"), 1)
            if stop == 2:
                return

            pe.wait_ge(s("ctx_lo"), 2)
            pe.wait_ge(s("ctx_vme"), 1)
            pe.wait_ge(s("ld_at1"), 7 * 16)
            transpose_xn("at1", 0)

            def qkv_tiles(b):
                for t in range(TPB):
                    n = TPB * b + t
                    pe.wait_ge(s("ln_xnT"), ln("at1", 2) + n // 4 + 1)
                    if n >= 2:
                        pe.wait_ge(s("at1_qe"), n - 1)
                    pe.matmul(ps[:, n % 2, 0:3 * D], xnT[:, n * P:n * P + P], wqkv1[:, :, :], start=True, stop=True
                              ).then_inc(s("at1_qkv"), 1)

            def keys_values(b):
                i = b % 2
                pe.wait_ge(s("at1_nrm"), b + 1)
                if b >= 1:
                    pe.wait_ge(s("at1_qTe"), b)
                else:
                    pe.wait_ge(s("ln_xnT"), ln("at1", 2) + 2)
                for t in range(TPB):
                    last = pe.transpose(ps[:, 6, t * P:t * P + P], qkv[:, i, t, 0:D], ident[:, :])
                last.then_inc(s("at1_qT"), 1)
                pe.wait_ge(s("at1_rv"), b + 1)
                pe.wait_ge(s("at1_kc"), b + 1)
                if b >= 1:
                    pe.wait_ge(s("at1_bd"), b)
                for a in range(2):
                    for t in range(TPB):
                        keys = (qkv[:, i, t, D:2 * D], kc[:, i, t, :])[a]
                        last = pe.matmul(ps[:, 4 + a, 0:2 * D + 2], keys, rv[:, i, t, :],
                                         start=(t == 0), stop=(t == TPB - 1))
                last.then_inc(s("at1_kv"), 1)

            qkv_tiles(0)
            transpose_xn("at1", 1)
            qkv_tiles(1)
            keys_values(0)
            for b in range(B):
                i = b % 2
                if b + 2 < B:
                    qkv_tiles(b + 2)
                pe.wait_ge(s("at1_bd"), b + 1)
                pe.wait_ge(s("at1_qTe"), b + 1)
                for t in range(TPB):
                    if TPB * b + t >= 1:
                        pe.wait_ge(s("at1_comb"), TPB * b + t)
                    for a in range(2):
                        last = pe.matmul(ps[:, 2 + a, 0:2 * (D + H)], qT[:, i, a, t * P:t * P + P], bd[:, a, :],
                                         start=True, stop=True)
                    last.then_inc(s("at1_out"), 1)
                    if t == 0 and b + 1 < B:
                        keys_values(b + 1)
                pe.wait_ge(s("at1_att"), TPB * (b + 1))
                if b >= 1:
                    pe.wait_ge(s("at1_aTe"), b)
                for t in range(TPB):
                    last = pe.transpose(ps[:, 7, t * P:t * P + P], att[:, t, :], ident[:, :])
                last.then_inc(s("at1_aT"), 1)
            pe.wait_ge(s("at1_aTe"), B)
            for hf in range(2):
                for n in range(4):
                    r = 4 * hf + n
                    last = pe.matmul(ps[:, hf, n * D:n * D + D], attT[:, r * P:r * P + P], wo1[:, :], start=True, stop=True)
                last.then_inc(s("at1_wo"), 1)
            if stop == 3:
                return

            pe.wait_ge(s("ld_xa1"), 64)
            for hf in range(2):
                transpose_xn("xa1", hf)
                pe.wait_ge(s("ln_xnT"), ln("xa1", 2) + hf + 1)
                pe.matmul(ps[:, hf, :], wx1[:, 0, :], xnT[:, hf * HALF:hf * HALF + HALF], start=True, stop=True
                          ).then_inc(s("xa1_q"), 1)
            pe.wait_ge(s("xa1_lo"), 2)
            cur = xnT

            def logits(Hf, hf, r, bank=7):
                pe.wait_ge(s("ff1_ctev"), Hf + 1)
                for n in range(4):
                    tile = 4 * hf + n
                    last = pe.matmul(ps[:, bank, n * E1:n * E1 + E1], cur[:, tile * P:tile * P + P],
                                     wg1[:, ds(r, 1), :], start=True, stop=True)
                last.then_inc(s("ff1_lg"), 1)

            def gate_rows(Hf, bank=7):
                pe.wait_ge(s("ff1_cwd"), Hf + 1)
                for n in range(4):
                    last = pe.transpose(ps[0:2 * E1, bank, n * P:n * P + P], cwhl[:, n, :], ident[:, :])
                last.then_inc(s("ff1_ct"), 1)

            def first_logits():
                pe.wait_ge(s("ld_ff1"), 6 * 16)
                pe.wait_ge(s("ln_xnT"), ln("ff1", 2) + 1)
                logits(0, 0, 0, 6)

            attention("xa1", True, k1hi[:, :], k1lo[:, :],
                      beside={H + 8: lambda: transpose_xn("ff1", 0, 1), H + 11: first_logits})
            pe.wait_ge(s("w1_lo"), 2 * E1)

            def up(U, u):
                u = u % (2 * E1)
                hf, e = u // E1, u % E1
                c = slice(hf * HALF, hf * HALF + HALF)
                for k in range(FC):
                    pe.wait_ge(s("ff1_gel"), FC * U + k + 1)
                    f = slice(k * P, k * P + P)
                    pe.matmul(ps[:, k, :], w1hi[:, e, f], xhi[:, c], start=True, stop=False)
                    pe.matmul(ps[:, k, :], w1lo[:, e, f], xhi[:, c], start=False, stop=False)
                    pe.matmul(ps[:, k, :], w1hi[:, e, f], xlo[:, c], start=False, stop=True).then_inc(s("ff1_up"), 1)

            def spread(U, u):
                u = u % (2 * E1)
                pe.wait_ge(s("ff1_cwb"), U + 1)
                pe.matmul(ps[:, 6, :], sel_er[:, u % E1, :], cwT[:, u // E1, :], start=True, stop=True
                          ).then_inc(s("ff1_bcd"), 1)

            def down(U, u):
                e = u % E1
                pe.wait_ge(s("ff1_cmb"), U + 1)
                o = ps[:, 4 + u % 2, :]
                for k in range(FC):
                    pe.wait_ge(s("ff1_glo"), 4 + FC * U + k + 1)
                    pe.matmul(o, w2hi[:, e, k, :], ghi[:, u % 2, k, :], start=(k == 0), stop=False)
                    pe.matmul(o, w2lo[:, e, k, :], ghi[:, u % 2, k, :], start=False, stop=False)
                    last = pe.matmul(o, w2hi[:, e, k, :], glo[:, u % 2, k, :], start=False, stop=(k == FC - 1))
                last.then_inc(s("ff1_dn"), 1)

            def round_(r, last):
                U0, H0 = 2 * E1 * r, 2 * r
                for u in range(2 * E1):
                    if u == 3:
                        pe.wait_ge(s("ff1_ctev"), 1 + H0 + 2)
                        pe.wait_ge(s("ff1_xs"), H0 + 2)
                    if u == 7 and not last:
                        pe.wait_ge(s("ff1_ctev"), 1 + H0 + 3)
                        pe.wait_ge(s("ff1_xs"), H0 + 3)
                    if not (last and u == 7):
                        spread(U0 + u + 1, u + 1)
                        up(U0 + u + 1, u + 1)
                    if u == 2:
                        gate_rows(H0 + 1)
                    if u == 6 and not last:
                        gate_rows(H0 + 2)
                    down(U0 + u, u)
                    if u == 0:
                        pe.wait_ge(s("ff1_pad"), U0 + 2)
                        logits(H0 + 1, 1, r)
                    if u == 4 and not last:
                        pe.wait_ge(s("ff1_pad"), U0 + 2 + E1)
                        logits(H0 + 2, 0, r + 1)

            pe.wait_ge(s("ff1_xs"), 1)
            up(0, 0)
            gate_rows(0, 6)
            transpose_xn("ff1", 1, 5)
            pe.wait_ge(s("ff1_ctev"), 2)
            spread(0, 0)
            pe.wait_ge(s("xa1_res"), TPB + TPB * B)
            pe.wait_ge(s("ln_xnT"), ln("ff1", 2) + 2)
            with pe.Fori(0, R1 - 1) as r:
                round_(r, False)
            round_(R1 - 1, True)
            pe.wait_ge(s("ff1_pad"), 2 + 2 * E1 * R1)
            for hf in range(2):
                for n in range(4):
                    tile = 4 * hf + n
                    last = pe.transpose(ps[:, hf, n * P:n * P + P], cur[:, tile * P:tile * P + P], ident[:, :])
                last.then_inc(s("fin_T"), 1)


def shape_constants():
    import numpy as np
    f = np.float32
    c = {"ident": np.eye(P, dtype=f)}
    inv_freq = (f(1.0) / f(10000.0) ** (np.arange(0, DH, 2, dtype=f) / f(DH))).astype(f)
    angle = np.outer(np.arange(T, dtype=f), inv_freq).astype(f)
    pair = (np.arange(D) % DH) // 2
    sign = np.where(np.arange(D) % 2 == 0, -1, 1).astype(f)
    c["rope"] = np.ascontiguousarray(np.stack([np.cos(angle)[:, pair].T, np.sin(angle)[:, pair].T * sign[:, None]], 1)).astype(f)
    sel = np.zeros((P, 2, G, 2, P), f)
    for g in range(G):
        for j in range(HPG):
            for d in range(DH):
                src = (HPG * g + j) * DH + d
                for side, parts in enumerate(((0, 1, 0), (0, 0, 1))):
                    for copy, part in enumerate(parts):
                        sel[src, side, g, part, QUAD * j + DH * copy + d] = 1
    c["sel"] = sel
    c["one_row"] = (np.arange(P) % QUAD == MAXROW).astype(f).reshape(P, 1)
    row, col = np.arange(P)[:, None], np.arange(P)[None, :]
    later_key, earlier_query = np.where(col > row, -1e9, 0), np.where(row > col, -1e9, 0)
    c["tri"] = np.stack([later_key, np.full((P, P), -1e9), earlier_query], 1).astype(np.dtype("bfloat16"))
    c["identb"] = np.eye(P, dtype=np.dtype("bfloat16"))
    idx = (f(np.pi / 2) * np.arange(1, T + 1, dtype=f) / f(T)).astype(f)
    c["sincos"] = np.ascontiguousarray(np.stack([np.sin(idx), np.cos(idx)], 1).reshape(TPB, P, 2).transpose(1, 0, 2)).astype(f)
    head = np.arange(D) // DH
    c["diag"] = (head[:, None] == head[None, :]).astype(f)
    c["diag_h"] = (head[:, None] == np.arange(H)[None, :]).astype(f)
    for n, E in (("tie0", E0), ("tie1", E1)):
        c[n] = (np.arange(E)[None, :] < np.arange(E)[:, None]).astype(f)
    c["sel_e"] = np.ascontiguousarray(np.broadcast_to(
        (np.arange(2 * E1)[:, None] % E1 == np.arange(E1)[None, :])[:, :, None], (2 * E1, E1, P))).astype(f)
    return c


def laid_out(a):
    import numpy as np
    T_ = lambda m: np.ascontiguousarray(np.asarray(m).T)
    swap = np.arange(D) ^ 1
    w = {
        "x": np.asarray(a["x"]).reshape(B * T, D),
        "ctxT": T_(np.asarray(a["ctx_1024"]).reshape(B * T, D)),
        "w0": np.stack([T_(a["L0_attn_wq"]), T_(np.asarray(a["L0_attn_wq"])[swap]), T_(a["L0_attn_wk"]),
                        T_(np.asarray(a["L0_attn_wk"])[swap]), T_(a["L0_attn_wv"])], 1),
        "wctx": np.stack([T_(a["L0_xattn_Wk"]), T_(a["L0_xattn_Wv"]), np.asarray(a["L1_xattn_WV"]),
                          np.asarray(a["L1_xattn_WK"])], 1),
        "wx0": np.stack([T_(a["L0_xattn_Wq"]), T_(a["L0_xattn_Wo"])], 1),
        "wbiasT": T_(a["L0_xattn_W_bias"]).reshape(TPB, P, T).transpose(1, 0, 2),
        "wgate0": T_(a["L0_ffn_w_gate"]),
        "wi0": np.asarray(a["L0_ffn_w_in"]).reshape(E0, F0 // P, P, D).transpose(2, 0, 1, 3),
        "wo0": np.asarray(a["L0_ffn_w_out"]).transpose(0, 2, 1).reshape(E0, F0 // P, P, D).transpose(2, 0, 1, 3),
        "wqkv1": np.stack([np.asarray(a["L1_attn_W" + n]) for n in "qkv"], 1),
        "bqkv1": np.stack([np.asarray(a["L1_attn_b" + n]) for n in "qkv"], 0),
        "wo1": np.asarray(a["L1_attn_Wo"]),
        "bo1": np.asarray(a["L1_attn_bo"]),
        "wx1": np.stack([np.asarray(a["L1_xattn_WQ"]), np.asarray(a["L1_xattn_WO"])], 1),
        "mask": np.asarray(a["mask_BxS2_ik0"]).reshape(NT, P).T,
        "wg1": np.asarray(a["L1_ffn_Wg"]).transpose(1, 0, 2),
        "bg1": np.asarray(a["L1_ffn_bg"]),
        "w1": np.asarray(a["L1_ffn_W1"]).transpose(1, 0, 2),
        "b1": np.asarray(a["L1_ffn_b1"]).reshape(E1, FC, P).transpose(2, 0, 1),
        "w2": np.asarray(a["L1_ffn_W2"]).reshape(E1, FC, P, D).transpose(2, 0, 1, 3),
        "b2": T_(a["L1_ffn_b2"]),
    }
    w.update(shape_constants())
    return {"in_" + n: np.ascontiguousarray(m) for n, m in w.items()}


def kernel(**inputs):
    import numpy as np
    import concourse.bacc as bacc
    from concourse.bass_utils import run_bass_kernel_spmd

    arrays = laid_out(inputs)
    nc = bacc.Bacc("TRN2", target_bir_lowering=False, num_devices=1)
    w = {n[3:]: nc.dram_tensor(n, m.shape, mybir.dt.from_np(m.dtype), kind="ExternalInput").ap() for n, m in arrays.items()}
    out = nc.dram_tensor("out", (B * T, D), mybir.dt.float32, kind="ExternalOutput").ap()
    decoder_kernel(nc, w, out)
    r = run_bass_kernel_spmd(nc, [arrays], core_ids=[0])
    return np.asarray(r.results[0]["out"]).reshape(B, T, D)
```
